# Optimizing a Trainium2 kernel written in Bass

```python
import numpy as np
import jax
import jax.numpy as jnp

def _softmax(x, axis=-1):
    return jax.nn.softmax(x, axis=axis)

def _gelu(x):
    return jax.nn.gelu(x, approximate=True)

def _silu(x):
    return jax.nn.silu(x)

def _sigmoid(x):
    return jax.nn.sigmoid(x)

def _layernorm(x, axis=-1, eps=1e-05):
    m = jnp.mean(x, axis=axis, keepdims=True)
    v = jnp.var(x, axis=axis, keepdims=True)
    return (x - m) / jnp.sqrt(v + eps)

def _scatter_add(tgt, idx, src, axis=0):
    return tgt.at[idx].add(src)

def _segment_sum(src, seg, n):
    return jax.ops.segment_sum(src, seg, n)
kernel_name = 'mk_seq_postln_d1_jaxref_r4_8e168a'

def setup_inputs(seed: int=0):
    np.random.seed(seed)
    _w = jnp.asarray

    def _L0_attn_setup():
        import jax, jax.numpy as jnp
        import numpy as np
        E = 256
        H = 16
        HD = E // H
        MAX_REL = 20
        key = jax.random.key(seed)
        ks = jax.random.split(key, 12)
        B, S = (4, 256)

        def lin_w(k):
            return jax.random.normal(k, (E, E), dtype=jnp.float32) * (1.0 / np.sqrt(E))
        return {'hidden_states': jax.random.normal(ks[0], (B, S, E), dtype=jnp.float32), 'Wq': lin_w(ks[1]), 'bq': jnp.zeros((E,), jnp.float32), 'Wk': lin_w(ks[2]), 'bk': jnp.zeros((E,), jnp.float32), 'Wv': lin_w(ks[3]), 'bv': jnp.zeros((E,), jnp.float32), 'Wo': lin_w(ks[4]), 'bo': jnp.zeros((E,), jnp.float32), 'rel_k': jax.random.uniform(ks[5], (2 * MAX_REL + 1, HD), jnp.float32, -0.24, 0.24), 'rel_v': jax.random.uniform(ks[6], (2 * MAX_REL + 1, HD), jnp.float32, -0.24, 0.24)}
    _L0_attn_in = _L0_attn_setup()

    def _L0_ffn_setup():
        import jax, jax.numpy as jnp
        import numpy as np
        B, S, D, F, E, TOP_K = (4, 512, 256, 1024, 8, 2)
        LN_EPS = 1e-05
        key = jax.random.key(seed)
        ks = jax.random.split(key, 4)
        sc = lambda fan_in: 1.0 / np.sqrt(fan_in)
        return {'x': jax.random.normal(ks[0], (B, S, D), jnp.float32), 'W1': jax.random.normal(ks[1], (E, D, F), jnp.float32) * sc(D), 'b1': jnp.zeros((E, F), jnp.float32), 'W2': jax.random.normal(ks[2], (E, F, D), jnp.float32) * sc(F), 'b2': jnp.zeros((E, D), jnp.float32), 'Wr': jax.random.normal(ks[3], (D, E), jnp.float32) * sc(D), 'br': jnp.zeros((E,), jnp.float32), 'gamma': jnp.ones((D,), jnp.float32), 'beta': jnp.zeros((D,), jnp.float32)}
    _L0_ffn_in = _L0_ffn_setup()
    _d = {'L0_attn_hidden_states': _L0_attn_in['hidden_states'], 'L0_attn_Wq': _L0_attn_in['Wq'], 'L0_attn_bq': _L0_attn_in['bq'], 'L0_attn_Wk': _L0_attn_in['Wk'], 'L0_attn_bk': _L0_attn_in['bk'], 'L0_attn_Wv': _L0_attn_in['Wv'], 'L0_attn_bv': _L0_attn_in['bv'], 'L0_attn_Wo': _L0_attn_in['Wo'], 'L0_attn_bo': _L0_attn_in['bo'], 'L0_attn_rel_k': _L0_attn_in['rel_k'], 'L0_attn_rel_v': _L0_attn_in['rel_v'], 'L0_ffn_W1': _L0_ffn_in['W1'], 'L0_ffn_b1': _L0_ffn_in['b1'], 'L0_ffn_W2': _L0_ffn_in['W2'], 'L0_ffn_b2': _L0_ffn_in['b2'], 'L0_ffn_Wr': _L0_ffn_in['Wr'], 'L0_ffn_br': _L0_ffn_in['br'], 'L0_ffn_gamma': _L0_ffn_in['gamma'], 'L0_ffn_beta': _L0_ffn_in['beta']}
    _x0 = _d['L0_attn_hidden_states']
    _d['L0_attn_hidden_states'] = jax.random.normal(jax.random.fold_in(jax.random.key(seed), 1), (2, 2048, 256), dtype=_x0.dtype)
    del _x0
    return _d

def reference(L0_attn_hidden_states, L0_attn_Wq, L0_attn_bq, L0_attn_Wk, L0_attn_bk, L0_attn_Wv, L0_attn_bv, L0_attn_Wo, L0_attn_bo, L0_attn_rel_k, L0_attn_rel_v, L0_ffn_W1, L0_ffn_b1, L0_ffn_W2, L0_ffn_b2, L0_ffn_Wr, L0_ffn_br, L0_ffn_gamma, L0_ffn_beta):

    def _L0_attn_ref(hidden_states, Wq, bq, Wk, bk, Wv, bv, Wo, bo, rel_k, rel_v):
        import jax, jax.numpy as jnp
        import numpy as np
        E = 256
        H = 16
        HD = E // H
        MAX_REL = 20
        B, S, _ = hidden_states.shape
        scale = jnp.sqrt(jnp.float32(HD))

        def proj(W, b):
            return (hidden_states @ W.T + b).reshape(B, S, H, HD).transpose(0, 2, 1, 3)
        q = proj(Wq, bq)
        k = proj(Wk, bk)
        v = proj(Wv, bv)
        pos = jnp.arange(S)
        idx = jnp.clip(pos[None, :] - pos[:, None], -MAX_REL, MAX_REL) + MAX_REL
        rk2 = rel_k[idx]
        rv2 = rel_v[idx]
        attn1 = jnp.einsum('bhqd,bhkd->bhqk', q, k)
        attn2 = jnp.einsum('bhqd,qkd->bhqk', q, rk2)
        attn = jax.nn.softmax((attn1 + attn2) / scale, axis=-1)
        w1 = jnp.einsum('bhqk,bhkd->bhqd', attn, v)
        w2 = jnp.einsum('bhqk,qkd->bhqd', attn, rv2)
        x = (w1 + w2).transpose(0, 2, 1, 3).reshape(B, S, E)
        out = x @ Wo.T + bo
        return out

    def _L0_ffn_ref(x, W1, b1, W2, b2, Wr, br, gamma, beta):
        import jax, jax.numpy as jnp
        import numpy as np
        B, S, D, F, E, TOP_K = (4, 512, 256, 1024, 8, 2)
        LN_EPS = 1e-05
        b, s, d = x.shape
        e = Wr.shape[1]
        rw = jax.nn.softmax(x.mean(axis=1) @ Wr + br, axis=-1)
        x_flat = x.reshape(-1, d)
        rw_tok = jnp.repeat(rw, s, axis=0)
        tk_w, tk_i = jax.lax.top_k(rw_tok, TOP_K)
        tk_w = jax.nn.softmax(tk_w, axis=-1)
        h = jax.nn.gelu(jnp.einsum('nd,edf->enf', x_flat, W1) + b1[:, None, :], approximate=False)
        expert_out = jnp.einsum('enf,efd->end', h, W2) + b2[:, None, :]
        onehot = jax.nn.one_hot(tk_i, e, dtype=x.dtype)
        cw = jnp.einsum('nk,nke->ne', tk_w, onehot)
        out = jnp.einsum('ne,end->nd', cw, expert_out).reshape(b, s, d)
        y = out + x
        mu = y.mean(axis=-1, keepdims=True)
        var = y.var(axis=-1, keepdims=True)
        return (y - mu) / jnp.sqrt(var + LN_EPS) * gamma + beta
    x = L0_attn_hidden_states
    x = _layernorm(x + _L0_attn_ref(x, L0_attn_Wq, L0_attn_bq, L0_attn_Wk, L0_attn_bk, L0_attn_Wv, L0_attn_bv, L0_attn_Wo, L0_attn_bo, L0_attn_rel_k, L0_attn_rel_v), axis=-1)
    x = _layernorm(x + _L0_ffn_ref(x, L0_ffn_W1, L0_ffn_b1, L0_ffn_W2, L0_ffn_b2, L0_ffn_Wr, L0_ffn_br, L0_ffn_gamma, L0_ffn_beta), axis=-1)
    return x

_drawn_inputs = setup_inputs


def setup_inputs(seed=0):
    import zlib

    import numpy as np

    out = dict(_drawn_inputs(seed))
    spreads = {'L0_attn_bq': (0.0, 0.8),
     'L0_attn_bk': (0.0, 2.0),
     'L0_attn_bv': (0.0, 0.1),
     'L0_attn_bo': (0.0, 0.1),
     'L0_ffn_b1': (0.0, 0.351),
     'L0_ffn_b2': (0.0, 0.1),
     'L0_ffn_br': (0.0, 0.1),
     'L0_ffn_gamma': (1.0, 0.2),
     'L0_ffn_beta': (0.0, 0.1)}
    factors = {'L0_attn_rel_k': 7.442}
    for name, (base, spread) in spreads.items():
        noise = np.random.default_rng([zlib.crc32(name.encode()), seed]).standard_normal(out[name].shape)
        drawn = base * np.exp(spread * noise) if base else spread * noise
        out[name] = jnp.asarray(drawn.astype(out[name].dtype))
    for name, factor in factors.items():
        out[name] = (out[name] * factor).astype(out[name].dtype)
    return out
```

```python
from contextlib import ExitStack

import concourse.bass as bass
from concourse import mybir

F32 = mybir.dt.float32
BF16 = mybir.dt.bfloat16
U32 = mybir.dt.uint32
ALU = mybir.AluOpType
ACT = mybir.ActivationFunctionType
AX = mybir.AxisListType

P = 128
B, S, E = 2, 2048, 256
H, HD = 16, 16
HG = 4
NG = H // HG
GD = HG * HD
HP = 32
MR = 20
NREL = 2 * MR + 1
QT = S // P
CH = 512
QC = S // CH
TPC = CH // P
KE = E // P
PARTS = 3
Q_PART = [0, 0, 1, 1, 0, 2]
K_PART = [0, 1, 0, 1, 2, 0]
KR = HD * len(Q_PART)
SCALE = HD ** -0.5
HALF = P // 2
LINE = 2 * P
F = 1024
NE = 8
TOPK = 2
KF = F // P
EPS = 1e-5


class Count:

    def __init__(self, sem):
        self.sem, self.n = sem, 0

    def inc(self, ins, by=1):
        ins.then_inc(self.sem, by)
        self.n += by

    def link(self, eng, ins):
        self.inc(ins)
        eng.wait_ge(self.sem, self.n)


def relative_lines(eng, chain, line, rel):
    first, last = rel[:, 0:1], rel[:, NREL - 1:NREL]
    chain.link(eng, eng.memset(line[:, :, :], 0.0))
    o = P - 1
    far0 = o - MR
    eng.tensor_scalar(line[:, 0, 0:far0], line[:, 0, 0:far0], first, last, ALU.add, ALU.subtract)
    eng.tensor_scalar(line[:, 0, far0:o + MR], rel[:, 0:NREL - 1], last, None, ALU.subtract)
    eng.tensor_scalar(line[:, 0, LINE - MR:LINE], rel[:, 1:MR + 1], first, None, ALU.subtract)
    eng.tensor_scalar(line[:, 1, 0:MR - 1], rel[:, MR + 1:NREL - 1], last, None, ALU.subtract)
    eng.tensor_scalar(line[:, 1, o - MR + 1:o + MR + 1], rel[:, 1:NREL], first, None, ALU.subtract)
    chain.link(eng, eng.tensor_scalar(line[:, 1, o + MR + 1:LINE], line[:, 1, o + MR + 1:LINE],
                                      last, first, ALU.add, ALU.subtract))


def split_parts(eng, chain, parts, rest, src):
    chain.link(eng, eng.tensor_copy(parts[0], src))
    chain.link(eng, eng.tensor_tensor(rest, src, parts[0], ALU.subtract))
    chain.link(eng, eng.tensor_copy(parts[1], rest))
    chain.link(eng, eng.tensor_tensor(parts[2], rest, parts[1], ALU.subtract))


def setup(nc, t, rel_k, rel_v):
    with ExitStack() as ctx:
        sb = lambda n, s, d: ctx.enter_context(nc.sbuf_tensor(n, s, d))
        sem = lambda n: ctx.enter_context(nc.semaphore(n))
        relk = sb("relk", [HD, NREL], F32)
        relv = sb("relv", [HD, NREL], F32)
        linek = sb("linek", [HD, 2, LINE], F32)
        linev = sb("linev", [HD, 2, LINE], F32)
        restk = sb("restk", [HD, 2, LINE], F32)
        partk = sb("partk", [HD, PARTS, 2, LINE], BF16)
        turned = sb("turned", [P, 2, 2, HP], F32)
        ps = ctx.enter_context(nc.psum_tensor("setup_ps", [P, 4, HD], F32))
        s_rel, s_line, s_v = sem("s_rel"), sem("s_line"), sem("s_v")
        s_pool = sem("s_pool")
        s_id, s_idp, s_turn, s_turned, s_store = sem("s_id"), sem("s_idp"), sem("s_turn"), sem("s_turned"), sem("s_store")
        block = ctx.enter_context(nc.Block())

        @block.sync
        def _(sp):
            with nc.allow_non_contiguous_dma("small tables"):
                sp.dma_start(relk[:, :], rel_k.rearrange("r d -> d r")).then_inc(s_rel, 16)
                sp.dma_start(relv[:, :], rel_v.rearrange("r d -> d r")).then_inc(s_rel, 16)
            sp.wait_ge(s_line, 1)
            for r, part in enumerate(K_PART):
                sp.dma_start(t["line"][HD * r:HD * (r + 1), :, :], partk[:, part, :, :]).then_inc(s_store, 16)
            sp.wait_ge(s_turned, 1)
            sp.dma_start(t["line_v"].rearrange("k (h p) d -> p k h d", p=P), turned[:, :, :, :]).then_inc(s_store, 16)
            sp.wait_ge(s_store, 16 * (len(K_PART) + 1))
            for kind in range(2):
                src = t["line_v"]
                row = src[kind]
                first = HALF if kind == 0 else 0
                ap = bass.AP(row.tensor, row.offset + first * HP, [[HP, P], [1, HALF * HP]])
                sp.dma_start(t["rvt"][:, kind, :, :].rearrange("p r d -> p (r d)"), ap).then_inc(s_store, 16)
            sp.wait_ge(s_store, 16 * (len(K_PART) + 3))

        @block.gpsimd
        def _(pool):
            pool.memset(t["ident"][:, :], 0.0).then_inc(s_idp, 1)
            pool.wait_ge(s_idp, 1)
            pool.affine_select(out=t["ident"][:, :], in_=t["ident"][:, :], compare_op=ALU.not_equal, fill=1.0,
                               base=0, pattern=[[-1, P]], channel_multiplier=1).then_inc(s_id, 1)
            pool.wait_ge(s_id, 1)
            chain = Count(s_pool)
            chain.link(pool, pool.memset(t["masked"][:, :, :], 0.0))
            for k, (lo, hi) in enumerate([(0, 32), (0, 96), (32, 128), (96, 128)]):
                for q in range(lo // 32, hi // 32):
                    chain.link(pool, pool.tensor_copy(t["masked"][32 * q:32 * q + 32, k, :],
                                                      t["ident"][32 * q:32 * q + 32, :]))
            for j in range(3):
                pool.tensor_copy(t["ident3"][:, j, :], t["ident"][:, :])
            pool.tensor_copy(t["identb"][:, :], t["ident"][:, :])

        @block.vector
        def _(dve):
            chain = Count(s_v)
            chain.link(dve, dve.memset(turned[:, :, :, :], 0.0))
            dve.wait_ge(s_rel, 32)
            relative_lines(dve, chain, linek, relk)
            split_parts(dve, chain, [partk[:, i, :, :] for i in range(PARTS)], restk[:, :, :], linek[:, :, :])
            dve.memset(t["tiny"][0:1, 0:1], 0.0).then_inc(s_line, 1)
            relative_lines(dve, chain, linev, relv)
            dve.memset(t["tiny"][0:1, 0:1], 0.0).then_inc(s_line, 1)
            dve.wait_ge(s_turn, 1)
            dve.tensor_copy(turned[:, :, :, 0:HD], ps[:, :, :].rearrange("p (k h) d -> p k h d", k=2)).then_inc(s_turned, 1)

        @block.tensor
        def _(pe):
            pe.wait_ge(s_id, 1)
            pe.wait_ge(s_line, 2)
            for kind in range(2):
                for half in range(2):
                    mm = pe.transpose(ps[:, 2 * kind + half, :], linev[:, kind, P * half:P * half + P],
                                      t["ident"][0:HD, 0:HD])
            mm.then_inc(s_turn, 1)


def project(nc, t, x, wq, bq, wk, bk, wv, bv, wo, rel_k, rel_v):
    with ExitStack() as ctx:
        sb = lambda n, s, d: ctx.enter_context(nc.sbuf_tensor(n, s, d))
        sem = lambda n: ctx.enter_context(nc.semaphore(n))
        ident = t["ident"]
        wn = sb("wn", [P, 4, KE, E], F32)
        wt = sb("wt", [P, 3, KE, E], F32)
        bcol = sb("bcol", [P, 2, KE], F32)
        rcol = sb("rcol", [P, 2], F32)
        bias = sb("bias", [P, 3, KE], F32)
        vrow = sb("vrow", [P, E], F32)
        rrow = sb("rrow", [P, 2, HD], F32)
        vbias = sb("vbias", [P, 2, H, HD], F32)
        xn = sb("xn", [P, 2, TPC, E], F32)
        xt = sb("xt", [P, 2, KE, CH], F32)
        full = sb("full", [P, 2, 3, KE, CH], F32)
        rest = sb("rest", [P, 3, KE, CH], F32)
        parts = sb("parts", [P, 2, 3, PARTS, KE, CH], BF16)
        vst = sb("vst", [P, 2, TPC, NG, 2, HG, HP], F32)
        ps = ctx.enter_context(nc.psum_tensor("proj_ps", [P, 8, CH], F32))
        (s_w, s_wt, s_wtc, s_xt, s_xta, s_xtv, s_qk, s_v, s_full, s_hi, s_r1, s_mid, s_lo, s_vst, s_bias,
         s_vinit) = [sem(n) for n in (
             "w_loaded", "w_turned", "w_copied", "x_turned", "xt_by_act", "xt_by_dve", "qk_done", "v_done",
             "full_ready", "hi_ready", "rest_ready", "mid_ready", "lo_ready", "v_staged", "bias_ready", "v_init")]
        s_x = [sem(f"x_loaded{i}") for i in range(2)]
        s_st = [sem(f"stored{i}") for i in range(2)]
        s_bias_chain = sem("bias_chain")
        block = ctx.enter_context(nc.Block())
        NC = QC
        STORES = 3 * 4 + NG
        W_LOADS = 16 * (9 + 2 * P // HD)

        def store(sp, b, c):
            for kind in range(3):
                sp.wait_ge(s_lo, b * (3 * NC) + 3 * c + kind + 1)
                for m in range(KE):
                    for h in range(2):
                        src = parts[HALF * h:HALF * h + HALF, c % 2, kind, :, m, :]
                        g = b * NG + (2 * m + h)
                        if kind == 0:
                            dst = t["qp"][bass.ds(g, 1), :, :, CH * c:CH * (c + 1)].rearrange("o a p t -> p (o a) t")
                        else:
                            dst = t["kp"][bass.ds(g, 1), kind - 1, :, :, CH * c:CH * (c + 1)].rearrange(
                                "o a p t -> p (o a) t")
                        sp.dma_start(dst, src).then_inc(s_st[c % 2], 16)
            sp.wait_ge(s_vst, b * (2 * TPC * NC) + 2 * TPC * (c + 1))
            for hg in range(NG):
                g = b * NG + hg
                dst = t["vp"][bass.ds(g, 1), CH * c:CH * (c + 1), :, :].rearrange("o (t p) v x -> p (o t) v x", p=P)
                sp.dma_start(dst, vst[:, c % 2, :, hg, :, :, :].rearrange("p t v h d -> p t v (h d)")).then_inc(s_st[c % 2], 16)

        @block.sync
        def _(sp):
            with nc.allow_non_contiguous_dma("small biases"):
                for i, w in enumerate((wq, wk, wv, wo)):
                    sp.dma_start(wn[:, i, :, :], w.rearrange("(m p) e -> p m e", p=P)).then_inc(s_w, 16)
                for i, b in enumerate((bq, bk)):
                    sp.dma_start(bcol[:, i, :], b.rearrange("(m p) -> p m", p=P)).then_inc(s_w, 16)
                for i in range(P // HD):
                    sp.dma_start(rcol[HD * i:HD * i + HD, 0:1], rel_k[0:1, :].rearrange("r d -> d r")).then_inc(s_w, 16)
                    sp.dma_start(rcol[HD * i:HD * i + HD, 1:2],
                                 rel_k[NREL - 1:NREL, :].rearrange("r d -> d r")).then_inc(s_w, 16)
                sp.dma_start(vrow[:, :], bv.partition_broadcast(P)).then_inc(s_w, 16)
                sp.dma_start(rrow[:, 0, :], rel_v[0, :].partition_broadcast(P)).then_inc(s_w, 16)
                sp.dma_start(rrow[:, 1, :], rel_v[NREL - 1, :].partition_broadcast(P)).then_inc(s_w, 16)
            with sp.Fori(0, B) as b:
                for c in range(NC):
                    if c >= 2:
                        sp.wait_ge(s_xt, b * (2 * NC) + 2 * (c - 1))
                    sp.dma_start(xn[:, c % 2, :, :],
                                 x[bass.ds(b, 1), CH * c:CH * (c + 1), :].rearrange("o (t p) e -> p (o t) e", p=P)
                                 ).then_inc(s_x[c % 2], 16)
                    if c >= 1:
                        store(sp, b, c - 1)
                store(sp, b, NC - 1)
            for i in range(2):
                sp.wait_ge(s_st[i], 8 * STORES * NC * B)

        @block.tensor
        def _(pe):
            pe.wait_ge(s_w, W_LOADS)
            for i in range(4):
                for m in range(KE):
                    for k in range(KE):
                        mm = pe.transpose(ps[:, i, CH // 2 * k + P * m:CH // 2 * k + P * m + P],
                                          wn[:, i, m, P * k:P * k + P], ident[:, :])
                mm.then_inc(s_wt, 1)
            pe.wait_ge(s_wtc, 4)
            with pe.Fori(0, B) as b:
                for c in range(NC):
                    pe.wait_ge(s_x[c % 2], b * (8 * NC) + 16 * (c // 2 + 1))
                    for k in range(KE):
                        if c:
                            pe.wait_ge((s_xta, s_xtv)[k], b * NC + c)
                        for tt in range(TPC):
                            mm = pe.transpose(ps[:, k, P * tt:P * tt + P], xn[:, c % 2, tt, P * k:P * k + P], ident[:, :])
                        mm.then_inc(s_xt, 1)
                    pe.wait_ge(s_xta, b * NC + c + 1)
                    pe.wait_ge(s_xtv, b * NC + c + 1)
                    if c:
                        pe.wait_ge(s_full, b * (6 * NC) + 6 * c)
                    for i in range(2):
                        for m in range(KE):
                            for k in range(KE):
                                mm = pe.matmul(ps[:, 2 + 2 * i + m, :], wt[:, i, k, P * m:P * m + P], xt[:, c % 2, k, :],
                                               start=(k == 0), stop=(k == KE - 1))
                            mm.then_inc(s_qk, 1)
                    if c:
                        pe.wait_ge(s_vst, b * (2 * TPC * NC) + 2 * TPC * c)
                    for tt in range(TPC):
                        for k in range(KE):
                            mm = pe.matmul(ps[:, 6 + tt // 2, E * (tt % 2):E * (tt % 2) + E],
                                           xt[:, c % 2, k, P * tt:P * tt + P], wt[:, 2, k, :],
                                           start=(k == 0), stop=(k == KE - 1))
                        if tt % 2:
                            mm.then_inc(s_v, 1)
                pe.wait_ge(s_full, (b + 1) * (6 * NC))
                pe.wait_ge(s_vst, (b + 1) * (2 * TPC * NC))

        @block.scalar
        def _(act):
            act.wait_ge(s_bias, 1)
            with act.Fori(0, B) as b:
                for c in range(NC):
                    act.wait_ge(s_xt, b * (2 * NC) + 2 * c + 1)
                    if c >= 2:
                        act.wait_ge(s_v, b * (2 * NC) + 2 * (c - 1))
                    act.activation(xt[:, c % 2, 0, :], ps[:, 0, :], ACT.Copy).then_inc(s_xta, 1)
                    if c >= 2:
                        act.wait_ge(s_lo, b * (3 * NC) + 3 * (c - 1))
                    for m in range(KE):
                        act.wait_ge(s_qk, b * (4 * NC) + 4 * c + m + 1)
                        act.activation(full[:, c % 2, 0, m, :], ps[:, 2 + m, :], ACT.Identity,
                                       bias=bias[:, 0, m:m + 1], scale=SCALE).then_inc(s_full, 1)
                    for m in range(KE):
                        act.wait_ge(s_qk, b * (4 * NC) + 4 * c + 3 + m)
                        for v in range(2):
                            act.activation(full[:, c % 2, 1 + v, m, :], ps[:, 4 + m, :], ACT.Identity,
                                           bias=bias[:, 1 + v, m:m + 1]).then_inc(s_full, 1)
                    if c >= 2:
                        act.wait_ge(s_st[c % 2], b * (8 * STORES * NC) + 16 * STORES * (c // 2))
                    for kind in range(3):
                        act.wait_ge(s_full, b * (6 * NC) + 6 * c + (2 if kind == 0 else 6))
                        act.activation(parts[:, c % 2, kind, 0, :, :], full[:, c % 2, kind, :, :], ACT.Copy).then_inc(s_hi, 1)
                act.wait_ge(s_lo, (b + 1) * (3 * NC))
                act.wait_ge(s_v, (b + 1) * (2 * NC))
                for i in range(2):
                    act.wait_ge(s_st[i], (b + 1) * (8 * STORES * NC))

        @block.gpsimd
        def _(pool):
            pool.memset(vst[:, :, :, :, :, :, :], 0.0).then_inc(s_vinit, 1)
            pool.wait_ge(s_vinit, 1)
            pool.memset(vst[:, :, :, :, :, :, HD:HD + 1].rearrange("p a t g v h o -> p (a t g v h) o"), 1.0).then_inc(s_vinit, 1)
            with pool.Fori(0, B) as b:
                for c in range(NC):
                    for kind in range(3):
                        pool.wait_ge(s_mid, b * (3 * NC) + 3 * c + kind + 1)
                        pool.tensor_tensor(parts[:, c % 2, kind, 2, :, :], rest[:, kind, :, :],
                                           parts[:, c % 2, kind, 1, :, :], ALU.subtract).then_inc(s_lo, 1)

        @block.vector
        def _(dve):
            chain = Count(s_bias_chain)
            dve.wait_ge(s_w, W_LOADS)
            dve.tensor_scalar(bias[:, 0, :], bcol[:, 0, :], SCALE, None, ALU.mult)
            dve.tensor_scalar(bias[:, 1, :], bcol[:, 1, :], rcol[:, 0:1], None, ALU.add)
            chain.link(dve, dve.tensor_scalar(bias[:, 2, :], bcol[:, 1, :], rcol[:, 1:2], None, ALU.add))
            for v in range(2):
                for h in range(H):
                    ins = dve.tensor_tensor(vbias[:, v, h, :], vrow[:, HD * h:HD * h + HD], rrow[:, v, :], ALU.add)
            ins.then_inc(s_bias, 1)
            dve.wait_ge(s_bias, 1)
            for i in range(4):
                dve.wait_ge(s_wt, i + 1)
                dst = wt[:, i, :, :] if i < 3 else t["wot"][:, :, :]
                dve.tensor_copy(dst, ps[:, i, :].rearrange("p (k o) -> p k o", k=KE)).then_inc(s_wtc, 1)
            dve.wait_ge(s_vinit, 2)
            with dve.Fori(0, B) as b:
                for c in range(NC):
                    dve.wait_ge(s_xt, b * (2 * NC) + 2 * c + 2)
                    if c >= 2:
                        dve.wait_ge(s_v, b * (2 * NC) + 2 * (c - 1))
                    dve.tensor_copy(xt[:, c % 2, 1, :], ps[:, 1, :]).then_inc(s_xtv, 1)
                    if c >= 2:
                        dve.wait_ge(s_st[c % 2], b * (8 * STORES * NC) + 16 * STORES * (c // 2))
                    for kind in range(3):
                        dve.wait_ge(s_hi, b * (3 * NC) + 3 * c + kind + 1)
                        if c:
                            dve.wait_ge(s_lo, b * (3 * NC) + 3 * (c - 1) + kind + 1)
                        dve.tensor_tensor(rest[:, kind, :, :], full[:, c % 2, kind, :, :], parts[:, c % 2, kind, 0, :, :],
                                          ALU.subtract).then_inc(s_r1, 1)
                        dve.wait_ge(s_r1, b * (3 * NC) + 3 * c + kind + 1)
                        dve.tensor_copy(parts[:, c % 2, kind, 1, :, :], rest[:, kind, :, :]).then_inc(s_mid, 1)
                    for tt in range(TPC):
                        dve.wait_ge(s_v, b * (2 * NC) + 2 * c + tt // 2 + 1)
                        for v in range(2):
                            dve.tensor_tensor(vst[:, c % 2, tt, :, v, :, 0:HD],
                                              ps[:, 6 + tt // 2, E * (tt % 2):E * (tt % 2) + E].rearrange(
                                                  "p (g h d) -> p g h d", g=NG, h=HG),
                                              vbias[:, v, :, :].rearrange("p (g h) d -> p g h d", g=NG), ALU.add).then_inc(s_vst, 1)
                for i in range(2):
                    dve.wait_ge(s_st[i], (b + 1) * (8 * STORES * NC))


def band_pieces(kt, qc):
    out = []
    for lo, n, r0, r1 in [(P * kt - 32, 32, 0, 32), (P * kt, 32, 0, 96), (P * kt + 32, 64, 0, P),
                          (P * kt + 96, 32, 32, P), (P * kt + P, 32, 96, P)]:
        if CH * qc <= lo < CH * (qc + 1):
            out.append((lo, n, r0, r1))
    return out


def band_spans(kt, qc):
    return [(lo, m, a, e) for lo, m, r0, r1 in band_pieces(kt, qc)
            for a, e in ([(r0, r1)] if r0 != 32 else [(32, 64), (64, P)])]


MASK = {(0, 32): 0, (0, 96): 1, (32, P): 2, (96, P): 3}


def column_pieces(kt, qc):
    cut = min(max(P * kt + HALF, CH * qc), CH * (qc + 1))
    return [(a, e, kind) for a, e, kind in ((CH * qc, cut, 1), (cut, CH * (qc + 1), 0)) if e > a]


def attention(nc, t):
    with ExitStack() as ctx:
        sb = lambda n, s, d: ctx.enter_context(nc.sbuf_tensor(n, s, d))
        sem = lambda n: ctx.enter_context(nc.semaphore(n))
        qs = sb("qs", [KR + PARTS, HG, S], BF16)
        ks = sb("ks", [KR + PARTS, 2, HG, S], BF16)
        vs = sb("vs", [P, QT, 2, HG * HP], F32)
        dt = sb("dt", [P, HG, S], F32)
        pr = sb("pr", [P, 3, HG, CH], F32)
        pw = sb("pw", [P, HG, S], F32)
        osb = sb("osb", [P, S], F32)
        on = sb("on", [P, QT, HG, HD], F32)
        rcp = sb("rcp", [P, QT, HG], F32)
        mx = sb("mx", [P, HG * TPC, QC], F32)
        mneg = sb("mneg", [P, HG * TPC], F32)
        mrest = sb("mrest", [P, HG * TPC], F32)
        mparts = sb("mparts", [P, PARTS, HG * TPC], BF16)
        mt = sb("mt", [HG * TPC, PARTS, P], BF16)
        st = ctx.enter_context(nc.psum_tensor("st_ps", [P, 4, CH], F32))
        sc = ctx.enter_context(nc.psum_tensor("sc_ps", [P, 2, CH], F32))
        ops = ctx.enter_context(nc.psum_tensor("o_ps", [P, CH], F32))
        mps = ctx.enter_context(nc.psum_tensor("m_ps", [P, CH], F32))
        (s_q, s_k, s_vl, s_ones, s_d, s_dca, s_dcv, s_s, s_max, s_mc, s_mready, s_mtr, s_mcp, s_row, s_st, s_exp, s_pv,
         s_pw, s_oc, s_w2, s_w2a, s_tr, s_rcp, s_on, s_out, s_pwz, s_seen) = [sem(n) for n in (
             "q_loaded", "k_loaded", "v_loaded", "ones_ready", "corr_done", "corr_by_act", "corr_by_dve", "scores_done",
             "max_taken", "max_chain", "max_split", "max_turned", "max_copied", "max_rows", "st_done", "exp_done", "pv_done",
             "band_copied", "o_copied", "w2_done", "w2_added", "o_turned", "recip_done", "o_normed", "o_stored", "band_zero", "band_seen")]
        block = ctx.enter_context(nc.Block())

        ND = P * HG * QT // CH
        NSC = QC * HG * TPC * QC
        NST = QC * QT * 2
        NW = P * QT // CH
        RPB = CH // (HG * QT)
        BAND = [(qc, kt) for qc in range(QC) for kt in range(QT) if band_pieces(kt, qc)]
        band_before = {(qc, kt): sum(len(band_spans(x[1], x[0])) for x in BAND if x < (qc, kt))
                       for qc in range(QC) for kt in range(QT)}
        NB = sum(len(band_spans(kt, qc)) for qc, kt in BAND)
        M_STEPS = HG * TPC * QC
        NROW = 16 * PARTS * HG
        MPS = 5

        def each_group(eng):
            return eng.Fori(0, B * NG)

        @block.sync
        def _(sp):
            with each_group(sp) as g:
                sp.wait_ge(s_st, g * NST + 1)
                for r, part in enumerate(Q_PART):
                    sp.dma_start(qs[HD * r:HD * r + HD, :, :],
                                 t["qp"][bass.ds(g, 1), part, :, :].rearrange("o (h d) t -> d (o h) t", d=HD)
                                 ).then_inc(s_q, 16)
                for r, part in enumerate(K_PART):
                    for v in range(2):
                        sp.dma_start(ks[HD * r:HD * r + HD, v, :, :],
                                     t["kp"][bass.ds(g, 1), v, part, :, :].rearrange("o (h d) t -> d (o h) t", d=HD)
                                     ).then_inc(s_k, 16)
                sp.wait_ge(s_pv, g * (QC * QT) + 1)
                sp.dma_start(vs[:, :, :, :], t["vp"][bass.ds(g, 1)].rearrange("o (k p) v x -> p (o k) v x", p=P)
                             ).then_inc(s_vl, 16)
                for qc in range(QC):
                    sp.wait_ge(s_mcp, g * QC + qc + 1)
                    for part in range(PARTS):
                        for h in range(HG):
                            sp.dma_start(qs[KR + part:KR + part + 1, h, CH * qc:CH * (qc + 1)],
                                         mt[TPC * h:TPC * h + TPC, part, :]).then_inc(s_row, 16)

        @block.tensor
        def _(pe):
            ident = t["ident"]

            def scores(g, n):
                qc, r = divmod(n, M_STEPS)
                h, r = divmod(r, TPC * QC)
                qt, kc = TPC * qc + r // QC, r % QC
                if n >= 2:
                    pe.wait_ge(s_max, g * NSC + n - 1)
                bank = sc[:, n % 2, :]
                lo, hi = CH * kc, CH * (kc + 1)
                runs = []
                for a, e, kind in ((0, P * qt, 0), (P * qt + P, S, 1)):
                    a, e = max(a, lo), min(e, hi)
                    if e > a:
                        runs.append((a, e, kind, 0, P))
                if lo <= P * qt < hi:
                    runs += [(P * qt, P * qt + P, 1, 0, HALF), (P * qt, P * qt + P, 0, HALF, HALF)]
                band = []
                for j, shift in enumerate((-32, 0, 0, 32)):
                    a, e = P * qt + shift, P * qt + shift + P
                    a2, e2 = max(a, lo, 0), min(e, hi, S)
                    if e2 > a2:
                        band.append((a2, e2, P + shift + a2 - a, j))
                total, first = len(runs) + len(band), True
                for a, e, kind, q0, nq in runs:
                    mm = pe.matmul(bank[q0:q0 + nq, a - lo:e - lo], qs[0:KR, h, P * qt + q0:P * qt + q0 + nq],
                                   ks[0:KR, kind, h, a:e], start=first, stop=not band, skip_group_check=True)
                    first = False
                for a, e, i, j in band:
                    mm = pe.matmul(bank[32 * j:32 * j + 32, a - lo:e - lo], dt[:, h, P * qt + 32 * j:P * qt + 32 * j + 32],
                                   t["ident3"][:, :, :].rearrange("p j k -> p (j k)")[:, i:i + e - a],
                                   start=False, stop=True, skip_group_check=True, tile_position=(0, 32 * j))
                mm.then_inc(s_s, 1)

            def second(g, n, pair):
                qc, kt = divmod(n, QT)
                if n:
                    pe.wait_ge(s_exp, g * NST + 2 * (n - 1) + pair + 1)
                if pair == 0 and kt == 0:
                    pe.wait_ge(s_row, g * (NROW * QC) + NROW * (qc + 1))
                for h in (2 * pair, 2 * pair + 1):
                    pieces = band_pieces(kt, qc)
                    for i, (a, e, kind) in enumerate(column_pieces(kt, qc)):
                        mm = pe.matmul(st[:, h, a - CH * qc:e - CH * qc], ks[:, kind, h, P * kt:P * kt + P], qs[:, h, a:e],
                                       start=(i == 0), stop=not pieces, skip_group_check=True)
                    for lo, m, r0, r1 in pieces:
                        w = ident[:, :] if (r0, r1) == (0, P) else t["masked"][:, MASK[r0, r1], :]
                        mm = pe.matmul(st[:, h, lo - CH * qc:lo - CH * qc + m], w, dt[:, h, lo:lo + m],
                                       start=False, stop=True, skip_group_check=True)
                mm.then_inc(s_st, 1)

            def values(g, n):
                qc, kt = divmod(n, QT)
                pe.wait_ge(s_exp, g * NST + 2 * n + 2)
                if kt == 0 and qc:
                    pe.wait_ge(s_oc, g * QC + qc)
                for i, (a, e, kind) in enumerate(column_pieces(kt, qc)):
                    for h in range(HG):
                        mm = pe.matmul(ops[HP * h:HP * h + HP, a - CH * qc:e - CH * qc],
                                       vs[:, kt, kind, HP * h:HP * h + HP], pr[:, n % 3, h, a - CH * qc:e - CH * qc],
                                       start=(kt == 0 and i == 0), stop=(kt == QT - 1), skip_group_check=True,
                                       tile_position=(0, HP * h))
                mm.then_inc(s_pv, 1)

            def row_parts(g, qc):
                pe.wait_ge(s_mready, g * QC + qc + 1)
                if qc:
                    pe.wait_ge(s_mcp, g * QC + qc)
                for part in range(PARTS):
                    mm = pe.transpose(mps[0:HG * TPC, HALF * part:HALF * part + HALF].bitcast(BF16), mparts[:, part, :],
                                      t["identb"][:, :])
                mm.then_inc(s_mtr, 1)

            pe.sem_inc(s_pv, 1)
            pe.sem_inc(s_st, 1)
            with each_group(pe) as g:
                pe.wait_ge(s_q, (g + 1) * (16 * len(Q_PART)))
                for n in range(ND):
                    if n >= 2:
                        pe.wait_ge((s_dca, s_dcv)[n % 2], g * (ND // 2) + n // 2)
                    for i in range(RPB):
                        r = RPB * n + i
                        mm = pe.matmul(sc[:, n % 2, HG * QT * i:HG * QT * (i + 1)],
                                       t["line"][:, 0 if r < HALF else 1, P - 1 - r:2 * P - 1 - r],
                                       qs[0:KR, :, r:S:P], start=(i == 0), stop=True, skip_group_check=True)
                    mm.then_inc(s_d, 1)
                pe.wait_ge(s_dca, (g + 1) * (ND // 2))
                pe.wait_ge(s_dcv, (g + 1) * (ND // 2))
                pe.wait_ge(s_k, (g + 1) * (32 * len(K_PART)))
                pe.wait_ge(s_ones, 1)
                for n in range(M_STEPS):
                    scores(g, n)
                pe.wait_ge(s_vl, (g + 1) * 16)
                done = M_STEPS
                row_parts(g, 0)
                for n in range(QC * QT):
                    qc, kt = divmod(n, QT)
                    for slot in range(MPS):
                        if done < min((qc + 2) * M_STEPS, NSC):
                            scores(g, done)
                            done += 1
                        if slot in (0, 1):
                            second(g, n, slot)
                        if slot == 3 and n:
                            values(g, n - 1)
                    if kt == -(-M_STEPS // MPS) and qc < QC - 1:
                        row_parts(g, qc + 1)
                values(g, QC * QT - 1)
                pe.wait_ge(s_max, (g + 1) * NSC)
                pe.wait_ge(s_pw, (g + 1) * NB + 1)
                for n in range(NW):
                    if n >= 2:
                        pe.wait_ge(s_w2a, g * NW + n - 1)
                    for i in range(CH // QT):
                        r = CH // QT * n + i
                        place = (HALF - 1 - r) if r < HALF else (P - 1 - r)
                        for h in range(HG):
                            mm = pe.matmul(sc[HP * h:HP * h + HP, n % 2, QT * i:QT * (i + 1)],
                                           t["rvt"][:, 0 if r < HALF else 1, place, :], pw[:, h, r:S:P],
                                           start=(i == 0), stop=True, skip_group_check=True, tile_position=(0, HP * h))
                    mm.then_inc(s_w2, 1)
                pe.wait_ge(s_w2a, (g + 1) * NW)
                for n in range(QC):
                    if n >= 2:
                        pe.wait_ge(s_on, g * QC + n - 1)
                    else:
                        pe.wait_ge(s_mcp, (g + 1) * QC)
                    for i in range(TPC):
                        q = TPC * n + i
                        mm = pe.transpose((mps, ops)[n % 2][:, P * i:P * i + P], osb[:, P * q:P * q + P], ident[:, :])
                    mm.then_inc(s_tr, 1)
                pe.wait_ge(s_on, (g + 1) * QC)

        @block.scalar
        def _(act):
            with each_group(act) as g:
                for n in range(0, ND, 2):
                    act.wait_ge(s_d, g * ND + n + 1)
                    place = RPB * n
                    act.activation(dt[:, :, :].rearrange("p h (q r) -> p (h q) r", r=P)[:, :, place:place + RPB],
                                   sc[:, 0, :].rearrange("p (r x) -> p x r", r=RPB), ACT.Copy).then_inc(s_dca, 1)
                for n in range(QC * QT):
                    for pair in range(2):
                        act.wait_ge(s_st, g * NST + 2 * n + pair + 2)
                        if pair == 0 and n >= 3:
                            act.wait_ge(s_pv, g * (QC * QT) + n - 2 + 1)
                            k = band_before.get(divmod(n - 2, QT))
                            if k:
                                act.wait_ge(s_pw, g * NB + k + 1)
                        act.activation(pr[:, n % 3, 2 * pair:2 * pair + 2, :], st[:, 2 * pair:2 * pair + 2, :],
                                       ACT.Exp).then_inc(s_exp, 1)
                act.wait_ge(s_pv, (g + 1) * (QC * QT) + 1)
                act.wait_ge(s_pw, (g + 1) * NB + 1)
                act.wait_ge(s_on, (g + 1) * QC)
                act.dma_start(t["att"][bass.ds(g, 1)].rearrange("o (q p) c -> p (o q) c", p=P),
                              on[:, :, :, :].rearrange("p q h d -> p q (h d)")).then_inc(s_out, 16)
            act.wait_ge(s_out, 16 * B * NG + 16)

        @block.gpsimd
        def _(pool):
            pool.memset(pw[:, :, :], 0.0).then_inc(s_pwz, 1)
            pool.wait_ge(s_pwz, 1)
            pool.memset(ks[KR:KR + PARTS, :, :, :], 1.0).then_inc(s_ones, 1)
            pool.wait_ge(s_ones, 1)
            pool.sem_inc(s_pw, 1)
            with each_group(pool) as g:
                for qc, kt in BAND:
                    n, copied = qc * QT + kt, band_before[qc, kt]
                    pool.wait_ge(s_exp, g * NST + 2 * n + 2)
                    pool.sem_inc(s_seen, 1)
                    for i, (lo, m, a, e) in enumerate(band_spans(kt, qc)):
                        pool.wait_ge(s_pw, g * NB + copied + i + 1)
                        pool.sem_inc(s_seen, 1)
                        pool.tensor_copy(pw[a:e, :, lo:lo + m],
                                         pr[a:e, n % 3, :, lo - CH * qc:lo - CH * qc + m]).then_inc(s_pw, 1)
                pool.wait_ge(s_w2, (g + 1) * NW)

        @block.vector
        def _(dve):
            dve.sem_inc(s_out, 16)
            with each_group(dve) as g:
                for n in range(1, ND, 2):
                    dve.wait_ge(s_d, g * ND + n + 1)
                    place = RPB * n
                    dve.tensor_copy(dt[:, :, :].rearrange("p h (q r) -> p (h q) r", r=P)[:, :, place:place + RPB],
                                    sc[:, 1, :].rearrange("p (r x) -> p x r", r=RPB)).then_inc(s_dcv, 1)
                taken = 0
                links = 0

                def link(ins):
                    nonlocal links
                    ins.then_inc(s_mc, 1)
                    links += 1
                    dve.wait_ge(s_mc, g * (4 * QC) + links)

                def take(n):
                    dve.wait_ge(s_s, g * NSC + n + 1)
                    r = n % M_STEPS
                    dve.tensor_reduce(mx[:, r // QC, r % QC:r % QC + 1], sc[:, n % 2, :], AX.X, ALU.max).then_inc(s_max, 1)

                def split_rows(qc):
                    dve.wait_ge(s_max, g * NSC + M_STEPS * (qc + 1))
                    link(dve.tensor_reduce(mneg[:, :], mx[:, :, :], AX.X, ALU.max, negate=True))
                    if qc:
                        dve.wait_ge(s_mtr, g * QC + qc)
                    link(dve.tensor_copy(mparts[:, 0, :], mneg[:, :]))
                    link(dve.tensor_tensor(mrest[:, :], mneg[:, :], mparts[:, 0, :], ALU.subtract))
                    link(dve.tensor_copy(mparts[:, 1, :], mrest[:, :]))
                    dve.tensor_tensor(mparts[:, 2, :], mrest[:, :], mparts[:, 1, :], ALU.subtract).then_inc(s_mready, 1)

                def copy_rows(qc):
                    dve.wait_ge(s_mtr, g * QC + qc + 1)
                    if qc:
                        dve.wait_ge(s_row, g * (NROW * QC) + NROW * qc)
                    for part in range(PARTS):
                        ins = dve.tensor_copy(mt[:, part, :], mps[0:HG * TPC, HALF * part:HALF * part + HALF].bitcast(BF16))
                    ins.then_inc(s_mcp, 1)

                def copy_out(qc):
                    dve.wait_ge(s_pv, g * (QC * QT) + QT * (qc + 1) + 1)
                    dve.tensor_copy(osb[:, CH * qc:CH * (qc + 1)], ops[:, :]).then_inc(s_oc, 1)

                for n in range(M_STEPS):
                    take(n)
                split_rows(0)
                copy_rows(0)
                for qc in range(QC):
                    if qc + 1 < QC:
                        for n in range(M_STEPS * (qc + 1), M_STEPS * (qc + 2)):
                            take(n)
                            if n == M_STEPS * (qc + 1) + MPS - 1 and qc:
                                copy_out(qc - 1)
                        split_rows(qc + 1)
                        copy_rows(qc + 1)
                    elif qc:
                        copy_out(qc - 1)
                copy_out(QC - 1)
                for n in range(NW):
                    dve.wait_ge(s_w2, g * NW + n + 1)
                    if n == 0:
                        dve.wait_ge(s_oc, (g + 1) * QC)
                    k = CH // QT
                    view = osb[:, :].rearrange("p (q r) -> p q r", r=P)[:, :, k * n:k * n + k]
                    dve.tensor_tensor(view, sc[:, n % 2, :].rearrange("p (r q) -> p q r", q=QT), view, ALU.add
                                      ).then_inc(s_w2a, 1)
                for n in range(QC):
                    dve.wait_ge(s_tr, g * QC + n + 1)
                    bank = (mps, ops)[n % 2][:, :].rearrange("p (q h d) -> p q h d", q=TPC, h=HG)
                    dve.reciprocal(rcp[:, TPC * n:TPC * n + TPC, :], bank[:, :, :, HD]).then_inc(s_rcp, 1)
                    dve.wait_ge(s_rcp, g * QC + n + 1)
                    if n == 0:
                        dve.wait_ge(s_out, g * 16 + 16)
                    dve.tensor_tensor(on[:, TPC * n:TPC * n + TPC, :, :], bank[:, :, :, 0:HD],
                                      rcp[:, TPC * n:TPC * n + TPC, :].unsqueeze(3).to_broadcast([P, TPC, HG, HD]),
                                      ALU.mult).then_inc(s_on, 1)


def experts(nc, t, x, bo, w1, b1, w2, b2, wr, br, gamma, beta, out):
    with ExitStack() as ctx:
        sb = lambda n, s, d: ctx.enter_context(nc.sbuf_tensor(n, s, d))
        sem = lambda n: ctx.enter_context(nc.semaphore(n))
        ident = t["ident"]
        at = sb("at", [P, 2, TPC, NG, GD], F32)
        xb = sb("xb", [P, 2, TPC, E], F32)
        xo = sb("xo", [P, 2, TPC, E], F32)
        att = sb("att_t", [P, 2, KE, CH], F32)
        x1 = sb("x1", [P, QT, E], F32)
        x1t = sb("x1t", [P, KE, S], F32)
        rows = sb("rows", [P, 3, E], F32)
        wrs = sb("wrs", [P, KE, NE], F32)
        brs = sb("brs", [1, NE], F32)
        ones = sb("ones", [P, P], F32)
        epst = sb("epst", [P, 1], F32)
        stats = sb("stats", [P, TPC, 6], F32)
        mv = sb("mv", [P, TPC, 2], F32)
        sd = sb("sd", [P, TPC], F32)
        rs = sb("rs", [P, TPC], F32)
        xm = sb("xm", [P, KE], F32)
        lg = sb("lg", [1, NE], F32)
        tiny = sb("tiny_r", [1, 8], F32)
        ex = sb("ex", [1, NE], F32)
        rw = sb("rw", [1, NE], F32)
        top = sb("top", [1, 8], F32)
        idx = sb("idx", [1, 8], U32)
        tw = sb("tw", [1, TOPK], F32)
        wb = sb("wb", [P, TOPK], F32)
        w1s = sb("w1s", [P, TOPK, KE, F], F32)
        w2s = sb("w2s", [P, TOPK, KF, E], F32)
        b1s = sb("b1s", [P, TOPK, KF], F32)
        b2s = sb("b2s", [P, TOPK, E], F32)
        bsum = sb("bsum", [P, E], F32)
        hid = sb("hid", [P, 2, KF, CH], F32)
        y = sb("y", [P, 2, TPC, E], F32)
        z = sb("z", [P, 2, TPC, E], F32)
        tp = ctx.enter_context(nc.psum_tensor("tp_ps", [P, 2, CH], F32))
        hp = ctx.enter_context(nc.psum_tensor("hp_ps", [P, 2, CH], F32))
        op = ctx.enter_context(nc.psum_tensor("op_ps", [P, 2, TPC // 2, CH], F32))
        (s_c, s_at, s_ata, s_atv, s_op, s_xo, s_x1, s_ch, s_sd, s_var, s_xt, s_xta, s_xtv, s_xm, s_xmc, s_lg, s_ex,
         s_neg, s_top, s_neg2, s_ex2, s_tw, s_wb, s_wbc, s_idx, s_we, s_h, s_hid, s_o, s_y, s_z1, s_cst,
         s_bs, s_b2) = [sem(n) for n in (
             "consts", "att_turned", "att_by_act", "att_by_dve", "proj_done", "xo_ready", "x1_ready",
             "dve_chain", "sd_ready", "var_ready", "x1_turned", "x1t_by_act", "x1t_by_dve", "mean_done", "mean_copied",
             "logits_done", "exp_ready", "neg_ready", "top_ready", "neg2_ready", "exp2_ready", "tw_ready", "wb_done",
             "wb_copied", "index_ready", "expert_loaded", "hidden_done", "gelu_done", "expert_done", "y_ready",
             "z_scaled", "const_set", "bsum_ready", "b2_used")]
        s_ld = [sem(f"tile_loaded{i}") for i in range(2)]
        s_st = [sem(f"out_stored{i}") for i in range(2)]
        s_st_ready, s_pz = sem("out_ready"), sem("pool_chain")
        block = ctx.enter_context(nc.Block())
        NCONST = 5

        @block.sync
        def _(sp):
            with nc.allow_non_contiguous_dma("small tables"):
                for i, row in enumerate((bo, gamma, beta)):
                    sp.dma_start(rows[:, i, :], row.partition_broadcast(P)).then_inc(s_c, 16)
                sp.dma_start(wrs[:, :, :], wr.rearrange("(k p) e -> p k e", p=P)).then_inc(s_c, 16)
                sp.dma_start(brs[:, :], br.rearrange("(a e) -> a e", a=1)).then_inc(s_c, 16)
                for b in range(B):
                    for c in range(QC):
                        n = b * QC + c
                        if n >= 2:
                            sp.wait_ge(s_at, 2 * (n - 1))
                            sp.wait_ge(s_xo, n - 1)
                        for g in range(NG):
                            sp.dma_start(at[:, n % 2, :, g, :],
                                         t["att"][NG * b + g, CH * c:CH * (c + 1), :].rearrange(
                                             "(t p) c -> p t c", p=P)).then_inc(s_ld[n % 2], 16)
                        sp.dma_start(xb[:, n % 2, :, :], x[b, CH * c:CH * (c + 1), :].rearrange(
                            "(t p) e -> p t e", p=P)).then_inc(s_ld[n % 2], 16)
                    if b:
                        sp.wait_ge(s_o, b * QC * TOPK)
                        sp.wait_ge(s_bs, b)
                    sp.wait_ge(s_idx, b + 1)
                    for k in range(TOPK):
                        e = sp.value_load(idx[0:1, k:k + 1], min_val=0, max_val=NE - 1)
                        sp.dma_start(w1s[:, k, :, :], w1[bass.ds(e, 1)].rearrange("o (k p) f -> p (o k) f", p=P)
                                     ).then_inc(s_we, 16)
                        sp.dma_start(b1s[:, k, :], b1[bass.ds(e, 1)].rearrange("o (k p) -> p (o k)", p=P)).then_inc(s_we, 16)
                        sp.dma_start(w2s[:, k, :, :], w2[bass.ds(e, 1)].rearrange("o (k p) d -> p (o k) d", p=P)
                                     ).then_inc(s_we, 16)
                        row = b2[bass.ds(e, 1)]
                        sp.dma_start(b2s[0:1, k, :], row).then_inc(s_we, 16)
                    for c in range(QC):
                        n = b * QC + c
                        sp.wait_ge(s_st_ready, n + 1)
                        sp.dma_start(out[b, CH * c:CH * (c + 1), :].rearrange("(t p) e -> p t e", p=P), z[:, n % 2, :, :]
                                     ).then_inc(s_st[n % 2], 16)
                for i in range(2):
                    sp.wait_ge(s_st[i], 8 * B * QC)

        @block.gpsimd
        def _(pool):
            pool.memset(ones[:, :], 1.0).then_inc(s_cst, 1)
            pool.memset(epst[:, :], EPS).then_inc(s_cst, 1)
            pool.wait_ge(s_c, 16 * NCONST)
            for b in range(B):
                for c in range(QC):
                    n = b * QC + c
                    pool.wait_ge(s_ld[n % 2], 16 * (NG + 1) * (n // 2 + 1))
                    if n >= 2:
                        pool.wait_ge(s_x1, n - 1)
                    for i in range(TPC):
                        ins = pool.tensor_tensor(xo[:, n % 2, i, :], xb[:, n % 2, i, :], rows[:, 0, :], ALU.add)
                    ins.then_inc(s_xo, 1)
                for c in range(QC):
                    n = b * QC + c
                    pool.wait_ge(s_z1, n + 1)
                    for i in range(TPC):
                        pool.tensor_tensor(z[:, n % 2, i, :], z[:, n % 2, i, :], rows[:, 1, :], ALU.mult).then_inc(s_pz, 1)
                    pool.wait_ge(s_pz, TPC * (3 * n + 1))
                    for i in range(TPC):
                        pool.tensor_tensor(z[:, n % 2, i, :], z[:, n % 2, i, :], rows[:, 2, :], ALU.add).then_inc(s_pz, 1)
                    pool.wait_ge(s_pz, TPC * (3 * n + 2))
                    for i in range(TPC):
                        pool.tensor_tensor(z[:, n % 2, i, :], z[:, n % 2, i, :], x1[:, TPC * c + i, :], ALU.add).then_inc(s_pz, 1)

        @block.tensor
        def _(pe):
            pe.wait_ge(s_cst, 2)
            pe.wait_ge(s_c, 16 * NCONST)
            for b in range(B):
                for c in range(QC):
                    n = b * QC + c
                    pe.wait_ge(s_ld[n % 2], 16 * (NG + 1) * (n // 2 + 1))
                    for k in range(KE):
                        if n:
                            pe.wait_ge((s_xta, s_xtv)[k], n)
                        for i in range(TPC):
                            mm = pe.transpose(tp[:, k, P * i:P * i + P],
                                              at[:, n % 2, i, :, :].rearrange("p g c -> p (g c)")[:, P * k:P * k + P],
                                              ident[:, :])
                        mm.then_inc(s_at, 1)
                    pe.wait_ge(s_ata, n + 1)
                    pe.wait_ge(s_atv, n + 1)
                    if c:
                        pe.wait_ge(s_x1, n)
                    elif b:
                        pe.wait_ge(s_y, b * QC * TOPK)
                    for i in range(TPC):
                        for k in range(KE):
                            mm = pe.matmul(op[:, 0, i // 2, E * (i % 2):E * (i % 2) + E], att[:, n % 2, k, P * i:P * i + P],
                                           t["wot"][:, k, :], start=(k == 0), stop=(k == KE - 1))
                    mm.then_inc(s_op, 1)
                    pe.wait_ge(s_x1, n + 1)
                    for k in range(KE):
                        for i in range(TPC):
                            mm = pe.transpose(tp[:, k, P * i:P * i + P], x1[:, TPC * c + i, P * k:P * k + P], ident[:, :])
                        mm.then_inc(s_xt, 1)
                pe.wait_ge(s_xta, (b + 1) * QC)
                pe.wait_ge(s_xtv, (b + 1) * QC)
                for k in range(KE):
                    for i in range(QT):
                        mm = pe.matmul(hp[:, 0, k:k + 1], x1[:, i, P * k:P * k + P], ones[:, 0:1],
                                       start=(i == 0), stop=(i == QT - 1))
                mm.then_inc(s_xm, 1)
                pe.wait_ge(s_xmc, b + 1)
                for k in range(KE):
                    mm = pe.matmul(hp[0:1, 1, 0:NE], xm[:, k:k + 1], wrs[:, k, :], start=(k == 0), stop=(k == KE - 1))
                mm.then_inc(s_lg, 1)
                pe.wait_ge(s_tw, b + 1)
                pe.matmul(hp[:, 0, 0:TOPK], ones[0:1, :], tw[:, :], start=True, stop=True).then_inc(s_wb, 1)
                pe.wait_ge(s_wbc, b + 1)
                pe.wait_ge(s_we, 64 * TOPK * (b + 1))
                for k in range(TOPK):
                    mm = pe.matmul(hp[:, 1, E * k:E * k + E], ones[0:1, :], b2s[0:1, k, :], start=True, stop=True)
                mm.then_inc(s_b2, 1)
                pe.wait_ge(s_bs, b + 1)
                for m in range(QC * TOPK + 1):
                    n = b * QC * TOPK + m
                    if m < QC * TOPK:
                        c, k = divmod(m, TOPK)
                        for f in range(KF):
                            i = KF * n + f
                            if m or f >= 2:
                                pe.wait_ge(s_hid, i - 1)
                            for kk in range(KE):
                                mm = pe.matmul(hp[:, f % 2, :], w1s[:, k, kk, P * f:P * f + P],
                                               x1t[:, kk, CH * c:CH * (c + 1)], start=(kk == 0), stop=(kk == KE - 1))
                            mm.then_inc(s_h, 1)
                    if m:
                        c, k = divmod(m - 1, TOPK)
                        pe.wait_ge(s_hid, KF * n)
                        if m >= 3:
                            pe.wait_ge(s_y, n - 2)
                        for i in range(TPC):
                            for f in range(KF):
                                mm = pe.matmul(op[:, k, i // 2, E * (i % 2):E * (i % 2) + E],
                                               hid[:, (n - 1) % 2, f, P * i:P * i + P], w2s[:, k, f, :],
                                               start=(f == 0), stop=(f == KF - 1))
                        mm.then_inc(s_o, 1)

        @block.scalar
        def _(act):
            act.wait_ge(s_cst, 2)

            def deviations(n):
                act.wait_ge(s_var, n + 1)
                act.activation(sd[:, :], mv[:, :, 1], ACT.Sqrt, bias=epst[:, 0:1]).then_inc(s_sd, 1)

            for b in range(B):
                base = b * 3 * QC
                for c in range(QC):
                    n = b * QC + c
                    act.wait_ge(s_at, 2 * n + 1)
                    if n >= 2:
                        act.wait_ge(s_op, n - 1)
                    act.activation(att[:, n % 2, 0, :], tp[:, 0, :], ACT.Copy).then_inc(s_ata, 1)
                    deviations(base + c)
                    act.wait_ge(s_xt, 2 * n + 1)
                    if b and c == 0:
                        act.wait_ge(s_o, b * QC * TOPK)
                    act.activation(x1t[:, 0, CH * c:CH * (c + 1)], tp[:, 0, :], ACT.Copy).then_inc(s_xta, 1)
                act.wait_ge(s_neg, b + 1)
                act.activation(ex[:, :], lg[:, :], ACT.Exp, bias=tiny[0:1, 0:1]).then_inc(s_ex, 1)
                act.wait_ge(s_neg2, b + 1)
                act.activation(tiny[0:1, 4:6], top[0:1, 0:2], ACT.Exp, bias=tiny[0:1, 3:4]).then_inc(s_ex2, 1)
                for m in range(QC * TOPK):
                    n = b * QC * TOPK + m
                    c, k = divmod(m, TOPK)
                    for f in range(KF):
                        act.wait_ge(s_h, KF * n + f + 1)
                        if f == 0 and m >= 2:
                            act.wait_ge(s_o, n - 1)
                        act.activation(hid[:, n % 2, f, :], hp[:, f % 2, :], ACT.Gelu,
                                       bias=b1s[:, k, f:f + 1]).then_inc(s_hid, 1)
                    if k == 1 and c:
                        deviations(base + QC + 2 * (c - 1))
                        deviations(base + QC + 2 * (c - 1) + 1)
                deviations(base + 3 * QC - 2)
                deviations(base + 3 * QC - 1)

        @block.vector
        def _(dve):
            chain = Count(s_ch)
            norms = [0]

            def norm(src, dst):
                for i in range(TPC):
                    ins = dve.bn_stats(stats[:, i, :], src(i))
                chain.link(dve, ins)
                for i in range(TPC):
                    ins = dve.bn_aggr(mv[:, i, :], stats[:, i, :])
                ins.then_inc(s_var, 1)
                norms[0] += 1
                dve.wait_ge(s_sd, norms[0])
                chain.link(dve, dve.reciprocal(rs[:, :], sd[:, :]))
                for i in range(TPC):
                    ins = dve.tensor_scalar(dst(i), src(i), mv[:, i, 0:1], rs[:, i:i + 1], ALU.subtract, ALU.mult)
                return ins

            for b in range(B):
                for c in range(QC):
                    n = b * QC + c
                    dve.wait_ge(s_at, 2 * n + 2)
                    if n >= 2:
                        dve.wait_ge(s_op, n - 1)
                    dve.tensor_copy(att[:, n % 2, 1, :], tp[:, 1, :]).then_inc(s_atv, 1)
                    dve.wait_ge(s_op, n + 1)
                    dve.wait_ge(s_xo, n + 1)
                    for i in range(TPC):
                        ins = dve.tensor_tensor(y[:, n % 2, i, :], op[:, 0, i // 2, E * (i % 2):E * (i % 2) + E],
                                                xo[:, n % 2, i, :], ALU.add)
                    chain.link(dve, ins)
                    norm(lambda i: y[:, n % 2, i, :], lambda i: x1[:, TPC * c + i, :]).then_inc(s_x1, 1)
                    dve.wait_ge(s_xt, 2 * n + 2)
                    dve.tensor_copy(x1t[:, 1, CH * c:CH * (c + 1)], tp[:, 1, :]).then_inc(s_xtv, 1)
                dve.wait_ge(s_xm, b + 1)
                dve.tensor_scalar(xm[:, :], hp[:, 0, 0:KE], 1.0 / S, None, ALU.mult).then_inc(s_xmc, 1)
                dve.wait_ge(s_lg, b + 1)
                chain.link(dve, dve.tensor_tensor(lg[:, :], hp[0:1, 1, 0:NE], brs[:, :], ALU.add))
                dve.tensor_reduce(tiny[0:1, 0:1], lg[:, :], AX.X, ALU.max, negate=True).then_inc(s_neg, 1)
                dve.wait_ge(s_ex, b + 1)
                chain.link(dve, dve.tensor_reduce(tiny[0:1, 1:2], ex[:, :], AX.X, ALU.add))
                chain.link(dve, dve.reciprocal(tiny[0:1, 2:3], tiny[0:1, 1:2]))
                chain.link(dve, dve.tensor_scalar(rw[:, :], ex[:, :], tiny[0:1, 2:3], None, ALU.mult))
                chain.link(dve, dve.max(top[:, :], rw[:, :]))
                dve.max_index(idx[:, :], top[:, :], rw[:, :]).then_inc(s_idx, 1)
                dve.tensor_scalar(tiny[0:1, 3:4], top[0:1, 0:1], -1.0, None, ALU.mult).then_inc(s_neg2, 1)
                dve.wait_ge(s_ex2, b + 1)
                chain.link(dve, dve.tensor_reduce(tiny[0:1, 6:7], tiny[0:1, 4:6], AX.X, ALU.add))
                chain.link(dve, dve.reciprocal(tiny[0:1, 7:8], tiny[0:1, 6:7]))
                dve.tensor_scalar(tw[:, :], tiny[0:1, 4:6], tiny[0:1, 7:8], None, ALU.mult).then_inc(s_tw, 1)
                dve.wait_ge(s_wb, b + 1)
                dve.tensor_copy(wb[:, :], hp[:, 0, 0:TOPK]).then_inc(s_wbc, 1)
                dve.wait_ge(s_wbc, b + 1)
                dve.wait_ge(s_b2, b + 1)
                chain.link(dve, dve.tensor_scalar(bsum[:, :], hp[:, 1, 0:E], wb[:, 0:1], None, ALU.mult))
                dve.scalar_tensor_tensor(out=bsum[:, :], in0=hp[:, 1, E:2 * E], scalar=wb[:, 1:2], in1=bsum[:, :],
                                         op0=ALU.mult, op1=ALU.add).then_inc(s_bs, 1)
                dve.wait_ge(s_bs, b + 1)
                for c in range(QC):
                    n = b * QC + c
                    for i in range(TPC):
                        ins = dve.tensor_tensor(y[:, n % 2, i, :], x1[:, TPC * c + i, :], bsum[:, :], ALU.add)
                    chain.link(dve, ins)
                    for k in range(TOPK):
                        dve.wait_ge(s_o, TOPK * n + k + 1)
                        for i in range(TPC):
                            ins = dve.scalar_tensor_tensor(out=y[:, n % 2, i, :],
                                                           in0=op[:, k, i // 2, E * (i % 2):E * (i % 2) + E],
                                                           scalar=wb[:, k:k + 1], in1=y[:, n % 2, i, :],
                                                           op0=ALU.mult, op1=ALU.add)
                        ins.then_inc(s_y, 1)
                        dve.wait_ge(s_y, TOPK * n + k + 1)
                    if n >= 2:
                        dve.wait_ge(s_st[n % 2], 16 * (n // 2))
                    norm(lambda i: y[:, n % 2, i, :], lambda i: z[:, n % 2, i, :]).then_inc(s_z1, 1)
                    dve.wait_ge(s_pz, TPC * (3 * n + 3))
                    norm(lambda i: z[:, n % 2, i, :], lambda i: z[:, n % 2, i, :]).then_inc(s_st_ready, 1)


def program(nc, hidden, wq, bq, wk, bk, wv, bv, wo, bo, rel_k, rel_v, w1, b1, w2, b2, wr, br, gamma, beta, out):
    with ExitStack() as ctx:
        sb = lambda n, s, d: ctx.enter_context(nc.sbuf_tensor(n, s, d))
        dram = lambda n, s, d: nc.dram_tensor(n, s, d, kind="Internal").ap()
        t = {
            "ident": sb("ident", [P, P], F32),
            "identb": sb("identb", [P, P], BF16),
            "ident3": sb("ident3", [P, 3, P], F32),
            "masked": sb("masked", [P, 4, P], F32),
            "line": sb("line", [KR, 2, LINE], BF16),
            "rvt": sb("rvt", [P, 2, HALF, HP], F32),
            "wot": sb("wot", [P, KE, E], F32),
            "tiny": sb("tiny", [1, 1], F32),
            "line_v": dram("line_v", [2, LINE, HP], F32),
            "qp": dram("q_parts", [B * NG, PARTS, GD, S], BF16),
            "kp": dram("k_parts", [B * NG, 2, PARTS, GD, S], BF16),
            "vp": dram("v_padded", [B * NG, S, 2, HG * HP], F32),
            "att": dram("attended", [B * NG, S, GD], F32),
        }
        setup(nc, t, rel_k, rel_v)
        project(nc, t, hidden, wq, bq, wk, bk, wv, bv, wo, rel_k, rel_v)
        attention(nc, t)
        experts(nc, t, hidden, bo, w1, b1, w2, b2, wr, br, gamma, beta, out)


_INS = ["L0_attn_hidden_states", "L0_attn_Wq", "L0_attn_bq", "L0_attn_Wk", "L0_attn_bk", "L0_attn_Wv", "L0_attn_bv",
        "L0_attn_Wo", "L0_attn_bo", "L0_attn_rel_k", "L0_attn_rel_v", "L0_ffn_W1", "L0_ffn_b1", "L0_ffn_W2", "L0_ffn_b2",
        "L0_ffn_Wr", "L0_ffn_br", "L0_ffn_gamma", "L0_ffn_beta"]


def kernel(**inputs):
    import numpy as _np
    import concourse.bacc as _bacc
    from concourse import mybir as _mybir
    from concourse.bass_utils import run_bass_kernel_spmd as _run

    nc = _bacc.Bacc("TRN2", target_bir_lowering=False, num_devices=1)
    arrays, args = {}, []
    for name in _INS:
        a = _np.ascontiguousarray(inputs[name])
        arrays[f"in_{name}"] = a
        args.append(nc.dram_tensor(f"in_{name}", a.shape, _mybir.dt.from_np(a.dtype), kind="ExternalInput").ap())
    args.append(nc.dram_tensor("out", [B, S, E], F32, kind="ExternalOutput").ap())
    program(nc, *args)
    return _run(nc, [arrays], core_ids=[0]).results[0]["out"]
```

```python
from contextlib import ExitStack

import concourse.bass as bass
from concourse import mybir

F32 = mybir.dt.float32
BF16 = mybir.dt.bfloat16
U32 = mybir.dt.uint32
ALU = mybir.AluOpType
ACT = mybir.ActivationFunctionType
AX = mybir.AxisListType

P = 128
B, S, E = 2, 2048, 256
H, HD = 16, 16
HG = 4
NG = H // HG
GD = HG * HD
HP = 32
MR = 20
NREL = 2 * MR + 1
QT = S // P
CH = 512
QC = S // CH
TPC = CH // P
KE = E // P
PARTS = 3
Q_PART = [0, 0, 1, 1, 0, 2]
K_PART = [0, 1, 0, 1, 2, 0]
KR = HD * len(Q_PART)
SCALE = HD ** -0.5
HALF = P // 2
LINE = 2 * P
F = 1024
NE = 8
TOPK = 2
KF = F // P
EPS = 1e-5


class Count:

    def __init__(self, sem):
        self.sem, self.n = sem, 0

    def inc(self, ins, by=1):
        ins.then_inc(self.sem, by)
        self.n += by

    def link(self, eng, ins):
        self.inc(ins)
        eng.wait_ge(self.sem, self.n)


def relative_lines(eng, chain, line, rel):
    first, last = rel[:, 0:1], rel[:, NREL - 1:NREL]
    chain.link(eng, eng.memset(line[:, :, :], 0.0))
    o = P - 1
    far0 = o - MR
    eng.tensor_scalar(line[:, 0, 0:far0], line[:, 0, 0:far0], first, last, ALU.add, ALU.subtract)
    eng.tensor_scalar(line[:, 0, far0:o + MR], rel[:, 0:NREL - 1], last, None, ALU.subtract)
    eng.tensor_scalar(line[:, 0, LINE - MR:LINE], rel[:, 1:MR + 1], first, None, ALU.subtract)
    eng.tensor_scalar(line[:, 1, 0:MR - 1], rel[:, MR + 1:NREL - 1], last, None, ALU.subtract)
    eng.tensor_scalar(line[:, 1, o - MR + 1:o + MR + 1], rel[:, 1:NREL], first, None, ALU.subtract)
    chain.link(eng, eng.tensor_scalar(line[:, 1, o + MR + 1:LINE], line[:, 1, o + MR + 1:LINE],
                                      last, first, ALU.add, ALU.subtract))


def split_parts(eng, chain, parts, rest, src):
    chain.link(eng, eng.tensor_copy(parts[0], src))
    chain.link(eng, eng.tensor_tensor(rest, src, parts[0], ALU.subtract))
    chain.link(eng, eng.tensor_copy(parts[1], rest))
    chain.link(eng, eng.tensor_tensor(parts[2], rest, parts[1], ALU.subtract))


def setup(nc, t, rel_k, rel_v):
    with ExitStack() as ctx:
        sb = lambda n, s, d: ctx.enter_context(nc.sbuf_tensor(n, s, d))
        sem = lambda n: ctx.enter_context(nc.semaphore(n))
        relk = sb("relk", [HD, NREL], F32)
        relv = sb("relv", [HD, NREL], F32)
        linek = sb("linek", [HD, 2, LINE], F32)
        linev = sb("linev", [HD, 2, LINE], F32)
        restk = sb("restk", [HD, 2, LINE], F32)
        partk = sb("partk", [HD, PARTS, 2, LINE], BF16)
        turned = sb("turned", [P, 2, 2, HP], F32)
        ps = ctx.enter_context(nc.psum_tensor("setup_ps", [P, 4, HD], F32))
        s_rel, s_line, s_v = sem("s_rel"), sem("s_line"), sem("s_v")
        s_pool = sem("s_pool")
        s_id, s_idp, s_turn, s_turned, s_store = sem("s_id"), sem("s_idp"), sem("s_turn"), sem("s_turned"), sem("s_store")
        block = ctx.enter_context(nc.Block())

        @block.sync
        def _(sp):
            with nc.allow_non_contiguous_dma("small tables"):
                sp.dma_start(relk[:, :], rel_k.rearrange("r d -> d r")).then_inc(s_rel, 16)
                sp.dma_start(relv[:, :], rel_v.rearrange("r d -> d r")).then_inc(s_rel, 16)
            sp.wait_ge(s_line, 1)
            for r, part in enumerate(K_PART):
                sp.dma_start(t["line"][HD * r:HD * (r + 1), :, :], partk[:, part, :, :]).then_inc(s_store, 16)
            sp.wait_ge(s_turned, 1)
            sp.dma_start(t["line_v"].rearrange("k (h p) d -> p k h d", p=P), turned[:, :, :, :]).then_inc(s_store, 16)
            sp.wait_ge(s_store, 16 * (len(K_PART) + 1))
            for kind in range(2):
                src = t["line_v"]
                row = src[kind]
                first = HALF if kind == 0 else 0
                ap = bass.AP(row.tensor, row.offset + first * HP, [[HP, P], [1, HALF * HP]])
                sp.dma_start(t["rvt"][:, kind, :, :].rearrange("p r d -> p (r d)"), ap).then_inc(s_store, 16)
            sp.wait_ge(s_store, 16 * (len(K_PART) + 3))

        @block.gpsimd
        def _(pool):
            pool.memset(t["ident"][:, :], 0.0).then_inc(s_idp, 1)
            pool.wait_ge(s_idp, 1)
            pool.affine_select(out=t["ident"][:, :], in_=t["ident"][:, :], compare_op=ALU.not_equal, fill=1.0,
                               base=0, pattern=[[-1, P]], channel_multiplier=1).then_inc(s_id, 1)
            pool.wait_ge(s_id, 1)
            chain = Count(s_pool)
            chain.link(pool, pool.memset(t["masked"][:, :, :], 0.0))
            for k, (lo, hi) in enumerate([(0, 32), (0, 96), (32, 128), (96, 128)]):
                for q in range(lo // 32, hi // 32):
                    chain.link(pool, pool.tensor_copy(t["masked"][32 * q:32 * q + 32, k, :],
                                                      t["ident"][32 * q:32 * q + 32, :]))
            for j in range(3):
                pool.tensor_copy(t["ident3"][:, j, :], t["ident"][:, :])
            pool.tensor_copy(t["identb"][:, :], t["ident"][:, :])

        @block.vector
        def _(dve):
            chain = Count(s_v)
            chain.link(dve, dve.memset(turned[:, :, :, :], 0.0))
            dve.wait_ge(s_rel, 32)
            relative_lines(dve, chain, linek, relk)
            split_parts(dve, chain, [partk[:, i, :, :] for i in range(PARTS)], restk[:, :, :], linek[:, :, :])
            dve.memset(t["tiny"][0:1, 0:1], 0.0).then_inc(s_line, 1)
            relative_lines(dve, chain, linev, relv)
            dve.memset(t["tiny"][0:1, 0:1], 0.0).then_inc(s_line, 1)
            dve.wait_ge(s_turn, 1)
            dve.tensor_copy(turned[:, :, :, 0:HD], ps[:, :, :].rearrange("p (k h) d -> p k h d", k=2)).then_inc(s_turned, 1)

        @block.tensor
        def _(pe):
            pe.wait_ge(s_id, 1)
            pe.wait_ge(s_line, 2)
            for kind in range(2):
                for half in range(2):
                    mm = pe.transpose(ps[:, 2 * kind + half, :], linev[:, kind, P * half:P * half + P],
                                      t["ident"][0:HD, 0:HD])
            mm.then_inc(s_turn, 1)


def project(nc, t, x, wq, bq, wk, bk, wv, bv, wo, rel_k, rel_v):
    with ExitStack() as ctx:
        sb = lambda n, s, d: ctx.enter_context(nc.sbuf_tensor(n, s, d))
        sem = lambda n: ctx.enter_context(nc.semaphore(n))
        ident = t["ident"]
        wn = sb("wn", [P, 4, KE, E], F32)
        wt = sb("wt", [P, 3, KE, E], F32)
        bcol = sb("bcol", [P, 2, KE], F32)
        rcol = sb("rcol", [P, 2], F32)
        bias = sb("bias", [P, 3, KE], F32)
        vrow = sb("vrow", [P, E], F32)
        rrow = sb("rrow", [P, 2, HD], F32)
        vbias = sb("vbias", [P, 2, H, HD], F32)
        xn = sb("xn", [P, 2, TPC, E], F32)
        xt = sb("xt", [P, 2, KE, CH], F32)
        full = sb("full", [P, 2, 3, KE, CH], F32)
        rest = sb("rest", [P, 3, KE, CH], F32)
        parts = sb("parts", [P, 2, 3, PARTS, KE, CH], BF16)
        vst = sb("vst", [P, 2, TPC, NG, 2, HG, HP], F32)
        ps = ctx.enter_context(nc.psum_tensor("proj_ps", [P, 8, CH], F32))
        (s_w, s_wt, s_wtc, s_xt, s_xta, s_xtv, s_qk, s_v, s_full, s_hi, s_r1, s_mid, s_lo, s_vst, s_bias,
         s_vinit) = [sem(n) for n in (
             "w_loaded", "w_turned", "w_copied", "x_turned", "xt_by_act", "xt_by_dve", "qk_done", "v_done",
             "full_ready", "hi_ready", "rest_ready", "mid_ready", "lo_ready", "v_staged", "bias_ready", "v_init")]
        s_x = [sem(f"x_loaded{i}") for i in range(2)]
        s_st = [sem(f"stored{i}") for i in range(2)]
        s_bias_chain = sem("bias_chain")
        block = ctx.enter_context(nc.Block())
        NC = QC
        STORES = 3 * 4 + NG
        W_LOADS = 16 * (9 + 2 * P // HD)

        def store(sp, b, c):
            for kind in range(3):
                sp.wait_ge(s_lo, b * (3 * NC) + 3 * c + kind + 1)
                for m in range(KE):
                    for h in range(2):
                        src = parts[HALF * h:HALF * h + HALF, c % 2, kind, :, m, :]
                        g = b * NG + (2 * m + h)
                        if kind == 0:
                            dst = t["qp"][bass.ds(g, 1), :, c, :, :].rearrange("o a p t -> p (o a) t")
                        else:
                            dst = t["kp"][bass.ds(g, 1), kind - 1, :, :, CH * c:CH * (c + 1)].rearrange(
                                "o a p t -> p (o a) t")
                        sp.dma_start(dst, src).then_inc(s_st[c % 2], 16)
            sp.wait_ge(s_vst, b * (2 * TPC * NC) + 2 * TPC * (c + 1))
            for hg in range(NG):
                g = b * NG + hg
                dst = t["vp"][bass.ds(g, 1), CH * c:CH * (c + 1), :, :].rearrange("o (t p) v x -> p (o t) v x", p=P)
                sp.dma_start(dst, vst[:, c % 2, :, hg, :, :, :].rearrange("p t v h d -> p t v (h d)")).then_inc(s_st[c % 2], 16)

        @block.sync
        def _(sp):
            with nc.allow_non_contiguous_dma("small biases"):
                for i, w in enumerate((wq, wk, wv, wo)):
                    sp.dma_start(wn[:, i, :, :], w.rearrange("(m p) e -> p m e", p=P)).then_inc(s_w, 16)
                for i, b in enumerate((bq, bk)):
                    sp.dma_start(bcol[:, i, :], b.rearrange("(m p) -> p m", p=P)).then_inc(s_w, 16)
                for i in range(P // HD):
                    sp.dma_start(rcol[HD * i:HD * i + HD, 0:1], rel_k[0:1, :].rearrange("r d -> d r")).then_inc(s_w, 16)
                    sp.dma_start(rcol[HD * i:HD * i + HD, 1:2],
                                 rel_k[NREL - 1:NREL, :].rearrange("r d -> d r")).then_inc(s_w, 16)
                sp.dma_start(vrow[:, :], bv.partition_broadcast(P)).then_inc(s_w, 16)
                sp.dma_start(rrow[:, 0, :], rel_v[0, :].partition_broadcast(P)).then_inc(s_w, 16)
                sp.dma_start(rrow[:, 1, :], rel_v[NREL - 1, :].partition_broadcast(P)).then_inc(s_w, 16)
            with sp.Fori(0, B) as b:
                for c in range(NC):
                    if c >= 2:
                        sp.wait_ge(s_xt, b * (2 * NC) + 2 * (c - 1))
                    sp.dma_start(xn[:, c % 2, :, :],
                                 x[bass.ds(b, 1), CH * c:CH * (c + 1), :].rearrange("o (t p) e -> p (o t) e", p=P)
                                 ).then_inc(s_x[c % 2], 16)
                    if c >= 1:
                        store(sp, b, c - 1)
                store(sp, b, NC - 1)
            for i in range(2):
                sp.wait_ge(s_st[i], 8 * STORES * NC * B)

        @block.tensor
        def _(pe):
            pe.wait_ge(s_w, W_LOADS)
            for i in range(4):
                for m in range(KE):
                    for k in range(KE):
                        mm = pe.transpose(ps[:, i, CH // 2 * k + P * m:CH // 2 * k + P * m + P],
                                          wn[:, i, m, P * k:P * k + P], ident[:, :])
                mm.then_inc(s_wt, 1)
            pe.wait_ge(s_wtc, 4)
            with pe.Fori(0, B) as b:
                for c in range(NC):
                    pe.wait_ge(s_x[c % 2], b * (8 * NC) + 16 * (c // 2 + 1))
                    for k in range(KE):
                        if c:
                            pe.wait_ge((s_xta, s_xtv)[k], b * NC + c)
                        for tt in range(TPC):
                            mm = pe.transpose(ps[:, k, P * tt:P * tt + P], xn[:, c % 2, tt, P * k:P * k + P], ident[:, :])
                        mm.then_inc(s_xt, 1)
                    pe.wait_ge(s_xta, b * NC + c + 1)
                    pe.wait_ge(s_xtv, b * NC + c + 1)
                    if c:
                        pe.wait_ge(s_full, b * (6 * NC) + 6 * c)
                    for i in range(2):
                        for m in range(KE):
                            for k in range(KE):
                                mm = pe.matmul(ps[:, 2 + 2 * i + m, :], wt[:, i, k, P * m:P * m + P], xt[:, c % 2, k, :],
                                               start=(k == 0), stop=(k == KE - 1))
                            mm.then_inc(s_qk, 1)
                    if c:
                        pe.wait_ge(s_vst, b * (2 * TPC * NC) + 2 * TPC * c)
                    for tt in range(TPC):
                        for k in range(KE):
                            mm = pe.matmul(ps[:, 6 + tt // 2, E * (tt % 2):E * (tt % 2) + E],
                                           xt[:, c % 2, k, P * tt:P * tt + P], wt[:, 2, k, :],
                                           start=(k == 0), stop=(k == KE - 1))
                        if tt % 2:
                            mm.then_inc(s_v, 1)
                pe.wait_ge(s_full, (b + 1) * (6 * NC))
                pe.wait_ge(s_vst, (b + 1) * (2 * TPC * NC))

        @block.scalar
        def _(act):
            act.wait_ge(s_bias, 1)
            with act.Fori(0, B) as b:
                for c in range(NC):
                    act.wait_ge(s_xt, b * (2 * NC) + 2 * c + 1)
                    if c >= 2:
                        act.wait_ge(s_v, b * (2 * NC) + 2 * (c - 1))
                    act.activation(xt[:, c % 2, 0, :], ps[:, 0, :], ACT.Copy).then_inc(s_xta, 1)
                    if c >= 2:
                        act.wait_ge(s_lo, b * (3 * NC) + 3 * (c - 1))
                    for m in range(KE):
                        act.wait_ge(s_qk, b * (4 * NC) + 4 * c + m + 1)
                        act.activation(full[:, c % 2, 0, m, :], ps[:, 2 + m, :], ACT.Identity,
                                       bias=bias[:, 0, m:m + 1], scale=SCALE).then_inc(s_full, 1)
                    for m in range(KE):
                        act.wait_ge(s_qk, b * (4 * NC) + 4 * c + 3 + m)
                        for v in range(2):
                            act.activation(full[:, c % 2, 1 + v, m, :], ps[:, 4 + m, :], ACT.Identity,
                                           bias=bias[:, 1 + v, m:m + 1]).then_inc(s_full, 1)
                    if c >= 2:
                        act.wait_ge(s_st[c % 2], b * (8 * STORES * NC) + 16 * STORES * (c // 2))
                    for kind in range(3):
                        act.wait_ge(s_full, b * (6 * NC) + 6 * c + (2 if kind == 0 else 6))
                        act.activation(parts[:, c % 2, kind, 0, :, :], full[:, c % 2, kind, :, :], ACT.Copy).then_inc(s_hi, 1)
                act.wait_ge(s_lo, (b + 1) * (3 * NC))
                act.wait_ge(s_v, (b + 1) * (2 * NC))
                for i in range(2):
                    act.wait_ge(s_st[i], (b + 1) * (8 * STORES * NC))

        @block.gpsimd
        def _(pool):
            pool.memset(vst[:, :, :, :, :, :, :], 0.0).then_inc(s_vinit, 1)
            pool.wait_ge(s_vinit, 1)
            pool.memset(vst[:, :, :, :, :, :, HD:HD + 1].rearrange("p a t g v h o -> p (a t g v h) o"), 1.0).then_inc(s_vinit, 1)
            with pool.Fori(0, B) as b:
                for c in range(NC):
                    for kind in range(3):
                        pool.wait_ge(s_mid, b * (3 * NC) + 3 * c + kind + 1)
                        pool.tensor_tensor(parts[:, c % 2, kind, 2, :, :], rest[:, kind, :, :],
                                           parts[:, c % 2, kind, 1, :, :], ALU.subtract).then_inc(s_lo, 1)

        @block.vector
        def _(dve):
            chain = Count(s_bias_chain)
            dve.wait_ge(s_w, W_LOADS)
            dve.tensor_scalar(bias[:, 0, :], bcol[:, 0, :], SCALE, None, ALU.mult)
            dve.tensor_scalar(bias[:, 1, :], bcol[:, 1, :], rcol[:, 0:1], None, ALU.add)
            chain.link(dve, dve.tensor_scalar(bias[:, 2, :], bcol[:, 1, :], rcol[:, 1:2], None, ALU.add))
            for v in range(2):
                for h in range(H):
                    ins = dve.tensor_tensor(vbias[:, v, h, :], vrow[:, HD * h:HD * h + HD], rrow[:, v, :], ALU.add)
            ins.then_inc(s_bias, 1)
            dve.wait_ge(s_bias, 1)
            for i in range(4):
                dve.wait_ge(s_wt, i + 1)
                dst = wt[:, i, :, :] if i < 3 else t["wot"][:, :, :]
                dve.tensor_copy(dst, ps[:, i, :].rearrange("p (k o) -> p k o", k=KE)).then_inc(s_wtc, 1)
            dve.wait_ge(s_vinit, 2)
            with dve.Fori(0, B) as b:
                for c in range(NC):
                    dve.wait_ge(s_xt, b * (2 * NC) + 2 * c + 2)
                    if c >= 2:
                        dve.wait_ge(s_v, b * (2 * NC) + 2 * (c - 1))
                    dve.tensor_copy(xt[:, c % 2, 1, :], ps[:, 1, :]).then_inc(s_xtv, 1)
                    if c >= 2:
                        dve.wait_ge(s_st[c % 2], b * (8 * STORES * NC) + 16 * STORES * (c // 2))
                    for kind in range(3):
                        dve.wait_ge(s_hi, b * (3 * NC) + 3 * c + kind + 1)
                        if c:
                            dve.wait_ge(s_lo, b * (3 * NC) + 3 * (c - 1) + kind + 1)
                        dve.tensor_tensor(rest[:, kind, :, :], full[:, c % 2, kind, :, :], parts[:, c % 2, kind, 0, :, :],
                                          ALU.subtract).then_inc(s_r1, 1)
                        dve.wait_ge(s_r1, b * (3 * NC) + 3 * c + kind + 1)
                        dve.tensor_copy(parts[:, c % 2, kind, 1, :, :], rest[:, kind, :, :]).then_inc(s_mid, 1)
                    for tt in range(TPC):
                        dve.wait_ge(s_v, b * (2 * NC) + 2 * c + tt // 2 + 1)
                        for v in range(2):
                            dve.tensor_tensor(vst[:, c % 2, tt, :, v, :, 0:HD],
                                              ps[:, 6 + tt // 2, E * (tt % 2):E * (tt % 2) + E].rearrange(
                                                  "p (g h d) -> p g h d", g=NG, h=HG),
                                              vbias[:, v, :, :].rearrange("p (g h) d -> p g h d", g=NG), ALU.add).then_inc(s_vst, 1)
                for i in range(2):
                    dve.wait_ge(s_st[i], (b + 1) * (8 * STORES * NC))


def band_pieces(kt, qc):
    out = []
    for lo, n, r0, r1 in [(P * kt - 32, 32, 0, 32), (P * kt, 32, 0, 96), (P * kt + 32, 64, 0, P),
                          (P * kt + 96, 32, 32, P), (P * kt + P, 32, 96, P)]:
        if CH * qc <= lo < CH * (qc + 1):
            out.append((lo, n, r0, r1))
    return out


def band_spans(kt, qc):
    return [(lo, m, a, e) for lo, m, r0, r1 in band_pieces(kt, qc)
            for a, e in ([(r0, r1)] if r0 != 32 else [(32, 64), (64, P)])]


MASK = {(0, 32): 0, (0, 96): 1, (32, P): 2, (96, P): 3}


def column_pieces(kt, qc):
    cut = min(max(P * kt + HALF, CH * qc), CH * (qc + 1))
    return [(a, e, kind) for a, e, kind in ((CH * qc, cut, 1), (cut, CH * (qc + 1), 0)) if e > a]


PRB = 4
RING = 3
PER = 6
START = 1


def attention(nc, t):
    with ExitStack() as ctx:
        sb = lambda n, s, d: ctx.enter_context(nc.sbuf_tensor(n, s, d))
        sem = lambda n: ctx.enter_context(nc.semaphore(n))
        qs = sb("qs", [KR + PARTS, QC, HG, CH], BF16)
        ks = sb("ks", [KR + PARTS, 2, HG, S], BF16)
        vs = sb("vs", [P, QT, 2, HG * HP], F32)
        dt = sb("dt", [P, QC, HG, CH], F32)
        pr = sb("pr", [P, PRB, HG, CH], F32)
        pw = sb("pw", [P, HG, S], F32)
        osb = sb("osb", [P, S], F32)
        on = sb("on", [P, QT, HG, HD], F32)
        rcp = sb("rcp", [P, QT, HG], F32)
        mx = sb("mx", [P, HG * TPC, QC], F32)
        mneg = sb("mneg", [P, HG * TPC], F32)
        mrest = sb("mrest", [P, HG * TPC], F32)
        mparts = sb("mparts", [P, PARTS, HG * TPC], BF16)
        mt = sb("mt", [HG * TPC, PARTS, P], BF16)
        st = ctx.enter_context(nc.psum_tensor("st_ps", [P, 4, CH], F32))
        sc = ctx.enter_context(nc.psum_tensor("sc_ps", [P, RING, CH], F32))
        ops = ctx.enter_context(nc.psum_tensor("o_ps", [P, CH], F32))
        (s_q, s_k, s_v, s_qlast, s_kend, s_knear, s_krest, s_vnear, s_vrest, s_ones, s_job, s_taken, s_mc, s_mready,
         s_row, s_st, s_exp, s_pv, s_pw, s_oc, s_rcp, s_out, s_pwz, s_seen) = [sem(n) for n in (
             "q_loaded", "k_loaded", "v_loaded", "q_last_loaded", "k_end_loaded", "k_near_loaded", "k_rest_loaded",
             "v_near_loaded", "v_rest_loaded", "ones_ready", "job_done", "job_taken", "max_chain", "max_split",
             "max_rows", "st_done", "exp_done", "pv_done", "band_copied", "o_copied", "recip_done",
             "o_stored", "band_zero", "band_seen")]
        block = ctx.enter_context(nc.Block())

        STEPS = QC * QT
        NST = STEPS * 2
        ORDER = [[5, 6, 7, 0, 8, 1, 9, 2, 10, 3, 11, 4, 12, 13, 14, 15],
                 [0, 3, 1, 4, 2, 5, 9, 6, 10, 7, 11, 8, 12, 13, 14, 15],
                 [0, 7, 1, 8, 2, 9, 3, 10, 4, 11, 5, 12, 6, 13, 14, 15],
                 [12, 0, 13, 1, 14, 2, 15, 3, 11, 4, 5, 6, 7, 8, 9, 10]]
        NEAR = QT // 2
        step = lambda n: (n // QT, ORDER[n // QT][n % QT])
        BAND = [n for n in range(STEPS) if band_pieces(step(n)[1], step(n)[0])]
        band_before = [sum(len(band_spans(step(m)[1], step(m)[0])) for m in BAND if m < n) for n in range(STEPS + 1)]
        NB = band_before[STEPS]
        NROW = 16 * PARTS
        LQ = QC - 1
        NT, LT = TPC * LQ, QT - TPC * LQ

        def corrections(first, tiles):
            k = CH // (HG * tiles)
            return [("d", r, min(k, P - r), first, tiles) for r in range(0, P, k)]

        def first_pass(qc, order):
            return [("m", qc, kc, h, TPC * qc + i) for kc in order for h in range(HG) for i in range(TPC)]

        NW = P * QT // CH
        m1, m2, m3 = (first_pass(qc, range(QC)) for qc in (1, 2, 3))
        LAG = 3
        JA = corrections(0, NT) + first_pass(0, [*range(1, QC), 0]) + [("r", 0)]
        JWT = [("w", i) for i in range(NW)] + [("t", i) for i in range(QC)]
        JB = JWT + corrections(NT, LT) + m1
        JC = m2[:LAG] + [("r", 1)] + m2[LAG:] + m3[:LAG] + [("r", 2)] + m3[LAG:] + [("r", 3)]
        NJ = len(JA) + len(JB) + len(JC)
        AT_A, AT_B, AT_C = -len(JWT), len(JA) - len(JWT), len(JA) + len(JB) - len(JWT)
        AT_R = [AT_A + len(JA) - 1] + [AT_C + JC.index(("r", qc)) for qc in range(1, QC)]
        CLOSING = (JA[-2], m1[-1], m2[-1], m3[-1])
        EARLY = 10

        def val(go, per, n):
            return go[0] * per + (go[1] * per + n)

        def wait(eng, s, v):
            if not isinstance(v, int) or v > 0:
                eng.wait_ge(s, v)

        PV0 = PRB

        @block.sync
        def _(sp):
            def load_q(go, a, e, s):
                for r, part in enumerate(Q_PART):
                    src = (t["qp"][go[1], part] if isinstance(go[0], int) else
                           t["qp"][bass.ds(go[0] + go[1], 1), part].rearrange("o c r t -> (o c) r t"))
                    sp.dma_start(qs[HD * r:HD * r + HD, a:e, :, :].rearrange("d c h t -> d (c h) t"),
                                 src[a:e].rearrange("c (h d) t -> d (c h) t", d=HD)
                                 ).then_inc(s, 16)

            def load_k(go, kind, a, e, s):
                for r, part in enumerate(K_PART):
                    src = (t["kp"][go[1], kind, part] if isinstance(go[0], int) else
                           t["kp"][bass.ds(go[0] + go[1], 1), kind, part].rearrange("o c t -> (o c) t"))
                    sp.dma_start(ks[HD * r:HD * r + HD, kind, :, a:e], src[:, a:e].rearrange("(h d) t -> d h t", d=HD)
                                 ).then_inc(s, 16)

            def load_v(go, kind, a, e, s):
                src = (t["vp"][go[1]] if isinstance(go[0], int) else
                       t["vp"][bass.ds(go[0] + go[1], 1)].rearrange("o s v x -> (o s) v x"))
                sp.dma_start(vs[:, a // P:e // P, kind, :], src[a:e, kind, :].rearrange("(k p) x -> p k x", p=P)
                             ).then_inc(s, 16)

            def rows(go, qc):
                sp.wait_ge(s_taken, val(go, NJ, AT_R[qc] + 1))
                send_rows(qc)

            def send_rows(qc):
                for part in range(PARTS):
                    sp.dma_start(qs[KR + part:KR + part + 1, qc, :, :].rearrange("o h t -> o (h t)"), mt[:, part, :]).then_inc(s_row, 16)

            def load_first(go, last):
                if last:
                    sp.wait_ge(s_st, val(last, NST, 2 * QT * LQ))
                    sp.wait_ge(s_job, val(last, NJ, AT_C + len(JC)))
                load_q(go, 0, LQ, s_q)
                load_k(go, 1, 0, P * NT, s_k)
                if last:
                    sp.wait_ge(s_pv, val(last, STEPS, QT * LQ + PV0))
                load_v(go, 1, 0, P * NT, s_v)
                if last:
                    sp.wait_ge(s_st, val(last, NST, 2 * (QT * LQ + NEAR)))
                load_k(go, 1, P * NT, S, s_kend)
                load_k(go, 0, 0, CH, s_knear)
                if last:
                    sp.wait_ge(s_pv, val(last, STEPS, QT * LQ + NEAR + PV0))
                load_v(go, 1, P * NT, S, s_vnear)
                load_v(go, 0, 0, CH, s_vnear)

            def load_rest(go, last):
                if last:
                    sp.wait_ge(s_st, val(last, NST, NST))
                load_q(go, LQ, QC, s_qlast)
                load_k(go, 0, CH, S, s_krest)
                if last:
                    sp.wait_ge(s_pv, val(last, STEPS, STEPS + PV0))
                load_v(go, 0, CH, S, s_vrest)

            def store(go):
                sp.wait_ge(s_taken, val(go, NJ, NJ + (AT_B if go[1] == 0 else AT_A) + len(JWT)))
                dst = (t["att"][go[1]] if isinstance(go[0], int) else
                       t["att"][bass.ds(go[0] + go[1], 1)].rearrange("o s c -> (o s) c"))
                sp.dma_start(dst.rearrange("(q p) c -> p q c", p=P),
                             on[:, :, :, :].rearrange("p q h d -> p q (h d)")).then_inc(s_out, 16)

            load_first((0, 0), None)
            load_rest((0, 0), None)
            sp.wait_ge(s_taken, len(JA))
            send_rows(0)
            with sp.Fori(0, B * NG - 1) as g:
                for qc in range(1, QC):
                    rows((g, 0), qc)
                load_first((g, 1), (g, 0))
                rows((g, 1), 0)
                load_rest((g, 1), (g, 0))
                store((g, 0))
            for qc in range(1, QC):
                rows((0, B * NG - 1), qc)
            store((0, B * NG - 1))
            sp.wait_ge(s_out, 16 * B * NG + 16)

        @block.tensor
        def _(pe):
            ident = t["ident"]

            def run_job(go, job, at):
                kind = job[0]
                wait(pe, s_taken, val(go, NJ, at - RING + 1))
                bank = sc[:, at % RING, :]
                if kind == "d":
                    _, r0, places, first, tiles = job
                    if r0 == 0:
                        pe.wait_ge(s_qlast if first else s_q, val(go, 16 * len(Q_PART), 16 * len(Q_PART)))
                    w = HG * tiles
                    for i in range(places):
                        r = r0 + i
                        mm = pe.matmul(bank[:, w * i:w * (i + 1)],
                                       t["line"][:, 0 if r < HALF else 1, P - 1 - r:2 * P - 1 - r],
                                       qs[:, :, :, :].rearrange("d c h (q r) -> d (c h q) r", r=P)[
                                           0:KR, HG * first:HG * (first + tiles), r],
                                       start=(i == 0), stop=True, skip_group_check=True)
                elif kind == "m":
                    mm = scores(go, job, at, bank)
                elif kind == "r":
                    pe.wait_ge(s_mready, val(go, QC, job[1] + 1))
                    for part in range(PARTS):
                        mm = pe.transpose(bank[0:HG * TPC, HALF * part:HALF * part + HALF].bitcast(BF16),
                                          mparts[:, part, :], t["identb"][:, :])
                elif kind == "w":
                    if job[1] == 0:
                        pe.wait_ge(s_pw, val(go, NB, 1))
                    for i in range(CH // QT):
                        r = CH // QT * job[1] + i
                        place = (HALF - 1 - r) if r < HALF else (P - 1 - r)
                        for h in range(HG):
                            mm = pe.matmul(bank[HP * h:HP * h + HP, QT * i:QT * (i + 1)],
                                           t["rvt"][:, 0 if r < HALF else 1, place, :], pw[:, h, r:S:P],
                                           start=(i == 0), stop=True, skip_group_check=True, tile_position=(0, HP * h))
                else:
                    if job[1] == 0:
                        pe.wait_ge(s_taken, val(go, NJ, at))
                    for i in range(TPC):
                        q = TPC * job[1] + i
                        mm = pe.transpose(bank[:, P * i:P * i + P], osb[:, P * q:P * q + P], ident[:, :])
                mm.then_inc(s_job, 1)

            def scores(go, job, at, bank):
                _, qc, kc, h, qt = job
                if h == 0 and qt == TPC * qc:
                    if qc == 0 and kc == 1:
                        pe.wait_ge(s_taken, val(go, NJ, at))
                        pe.wait_ge(s_k, val(go, 16 * len(K_PART), 16 * len(K_PART)))
                    if qc == 0 and kc == QC - 1:
                        pe.wait_ge(s_kend, val(go, 16 * len(K_PART), 16 * len(K_PART)))
                    if qc == 0 and kc == 0:
                        pe.wait_ge(s_knear, val(go, 16 * len(K_PART), 16 * len(K_PART)))
                    if qc == 1 and kc == 0:
                        pe.wait_ge(s_krest, val(go, 16 * len(K_PART), 16 * len(K_PART)))
                lo, hi = CH * kc, CH * (kc + 1)
                runs = []
                for a, e, kind in ((0, P * qt, 0), (P * qt + P, S, 1)):
                    a, e = max(a, lo), min(e, hi)
                    if e > a:
                        runs.append((a, e, kind, 0, P))
                if lo <= P * qt < hi:
                    runs += [(P * qt, P * qt + P, 1, 0, HALF), (P * qt, P * qt + P, 0, HALF, HALF)]
                band = []
                for j, shift in enumerate((-32, 0, 0, 32)):
                    a, e = P * qt + shift, P * qt + shift + P
                    a2, e2 = max(a, lo, 0), min(e, hi, S)
                    if e2 > a2:
                        band.append((a2, e2, P + shift + a2 - a, j))
                first = True
                for a, e, kind, q0, nq in runs:
                    mm = pe.matmul(bank[q0:q0 + nq, a - lo:e - lo], qs[0:KR, qc, h, q0 + P * (qt - TPC * qc):q0 + nq + P * (qt - TPC * qc)],
                                   ks[0:KR, kind, h, a:e], start=first, stop=not band, skip_group_check=True)
                    first = False
                for a, e, i, j in band:
                    mm = pe.matmul(bank[32 * j:32 * j + 32, a - lo:e - lo], dt[:, qc, h, P * (qt - TPC * qc) + 32 * j:P * (qt - TPC * qc) + 32 * j + 32],
                                   t["ident3"][:, :, :].rearrange("p j k -> p (j k)")[:, i:i + e - a],
                                   start=False, stop=True, skip_group_check=True, tile_position=(0, 32 * j))
                return mm

            def second(go, n, pair):
                qc, kt = step(n)
                wait(pe, s_exp, val(go, NST, 2 * (n - 1) + pair + 1))
                if pair == 0 and n % QT == 0:
                    pe.wait_ge(s_row, val(go, NROW * QC, NROW * (qc + 1)))
                for h in (2 * pair, 2 * pair + 1):
                    pieces = band_pieces(kt, qc)
                    for i, (a, e, kind) in enumerate(column_pieces(kt, qc)):
                        mm = pe.matmul(st[:, h, a - CH * qc:e - CH * qc], ks[:, kind, h, P * kt:P * kt + P],
                                       qs[:, qc, h, a - CH * qc:e - CH * qc],
                                       start=(i == 0), stop=not pieces, skip_group_check=True)
                    for lo, m, r0, r1 in pieces:
                        w = ident[:, :] if (r0, r1) == (0, P) else t["masked"][:, MASK[r0, r1], :]
                        mm = pe.matmul(st[:, h, lo - CH * qc:lo - CH * qc + m], w, dt[:, qc, h, lo - CH * qc:lo - CH * qc + m],
                                       start=False, stop=True, skip_group_check=True)
                mm.then_inc(s_st, 1)

            def values(go, n):
                qc, kt = step(n)
                pe.wait_ge(s_exp, val(go, NST, 2 * n + 2))
                if n % QT == 0:
                    wait(pe, s_oc, val(go, QC, qc))
                if n == 0:
                    pe.wait_ge(s_v, val(go, 16, 16))
                if n == ORDER[0].index(0):
                    pe.wait_ge(s_vnear, val(go, 32, 32))
                if n == QT:
                    pe.wait_ge(s_vrest, val(go, 16, 16))
                for i, (a, e, kind) in enumerate(column_pieces(kt, qc)):
                    for h in range(HG):
                        mm = pe.matmul(ops[HP * h:HP * h + HP, a - CH * qc:e - CH * qc],
                                       vs[:, kt, kind, HP * h:HP * h + HP], pr[:, n % PRB, h, a - CH * qc:e - CH * qc],
                                       start=(n % QT == 0 and i == 0), stop=(n % QT == QT - 1), skip_group_check=True,
                                       tile_position=(0, HP * h))
                mm.then_inc(s_pv, 1)

            def chunk(go, qc, jobs, at, per, start=0):
                jobs, late = (jobs[:-1], jobs[-1:]) if jobs and jobs[-1][0] == "r" else (jobs, [])
                jgo, jobs = (go if qc < LQ else (go[0], go[1] + 1)), list(jobs)
                for i in range(QT):
                    n = QT * qc + i
                    mine = [jobs.pop(0) for _ in range(min(per, len(jobs)))] if i >= start else []
                    if late and not mine and not jobs and i > start:
                        mine, late = late, []
                    prev = (lambda: values(go, n - 1)) if n else (lambda: values((go[0], go[1] - 1), STEPS - 1))
                    if n == 0 and isinstance(go[0], int) and go[1] == 0:
                        prev = lambda: None
                    acts = [lambda: second(go, n, 0), lambda: second(go, n, 1), prev]
                    places = (0, 0, 0) if i == 0 else (1, 2, 4)
                    done = 0
                    for act, k in zip(acts, places):
                        while done < min(k, len(mine)):
                            run_job(jgo, mine[done], at)
                            at, done = at + 1, done + 1
                        act()
                    for job in mine[done:]:
                        run_job(jgo, job, at)
                        at += 1
                assert not jobs and not late, (qc, jobs, late)

            pe.sem_inc(s_pv, PV0)
            pe.wait_ge(s_ones, 1)
            for i, job in enumerate(JA):
                run_job((0, 0), job, i)
            chunk((0, 0), 0, JB[len(JWT):] + JC[:EARLY], AT_B + len(JWT), PER)
            with pe.Fori(0, B * NG - 1) as g:
                chunk((g, 0), 1, JC[EARLY:EARLY + QT * 4], AT_C + EARLY, 4)
                chunk((g, 0), 2, JC[EARLY + QT * 4:], AT_C + EARLY + QT * 4, 5)
                chunk((g, 0), 3, JA, AT_A, PER, START)
                chunk((g, 1), 0, JB + JC[:EARLY], AT_B, PER)
            last = (0, B * NG - 1)
            chunk(last, 1, JC[EARLY:EARLY + QT * 4], AT_C + EARLY, 4)
            chunk(last, 2, JC[EARLY + QT * 4:], AT_C + EARLY + QT * 4, 5)
            chunk(last, 3, [], 0, 0)
            values(last, STEPS - 1)
            for i, job in enumerate(JWT):
                run_job((0, B * NG), job, AT_A + i)

        @block.scalar
        def _(act):
            with act.Fori(0, B * NG) as g:
                for n in range(STEPS):
                    for pair in range(2):
                        act.wait_ge(s_st, g * NST + 2 * n + pair + 1)
                        if pair == 0:
                            act.wait_ge(s_pv, g * STEPS + n - PRB + 1 + PV0)
                            k = band_before[max(n - PRB + 1, 0)]
                            if n == 0 or k:
                                act.wait_ge(s_pw, g * NB + k + 1)
                        act.activation(pr[:, n % PRB, 2 * pair:2 * pair + 2, :], st[:, 2 * pair:2 * pair + 2, :],
                                       ACT.Exp).then_inc(s_exp, 1)

        @block.gpsimd
        def _(pool):
            pool.memset(ks[KR:KR + PARTS, :, :, :], 1.0).then_inc(s_ones, 1)
            pool.wait_ge(s_ones, 1)
            pool.memset(pw[:, :, :], 0.0).then_inc(s_pwz, 1)
            pool.wait_ge(s_pwz, 1)
            pool.sem_inc(s_pw, 1)
            with pool.Fori(0, B * NG) as g:
                pool.wait_ge(s_job, g * NJ + (AT_B + NW))
                pool.sem_inc(s_seen, 1)
                for n in BAND:
                    qc, kt = step(n)
                    pool.wait_ge(s_exp, g * NST + 2 * n + 2)
                    pool.sem_inc(s_seen, 1)
                    for i, (lo, m, a, e) in enumerate(band_spans(kt, qc)):
                        pool.wait_ge(s_pw, g * NB + band_before[n] + i + 1)
                        pool.sem_inc(s_seen, 1)
                        pool.tensor_copy(pw[a:e, :, lo:lo + m],
                                         pr[a:e, n % PRB, :, lo - CH * qc:lo - CH * qc + m]).then_inc(s_pw, 1)

        @block.vector
        def _(dve):
            def link(ins, go, number):
                ins.then_inc(s_mc, 1)
                dve.wait_ge(s_mc, val(go, 4 * QC, number))

            def take(go, job, at):
                kind = job[0]
                dve.wait_ge(s_job, val(go, NJ, at + 1))
                bank = sc[:, at % RING, :]
                if kind == "d":
                    _, r, places, first, tiles = job
                    if r == 0:
                        wait(dve, s_st, val(go, NST, 0 if first else 2 * QT * LQ - NST))
                    ins = dve.tensor_copy(
                        dt[:, :, :, :].rearrange("p c h (q r) -> p (c h q) r", r=P)[
                            :, HG * first:HG * (first + tiles), r:r + places],
                        bank[:, 0:HG * tiles * places].rearrange("p (r x) -> p x r", r=places))
                elif kind == "m":
                    _, qc, kc, h, qt = job
                    row = TPC * h + qt - TPC * qc
                    ins = dve.tensor_reduce(mx[:, row, kc:kc + 1], bank, AX.X, ALU.max)
                elif kind == "r":
                    wait(dve, s_row, val(go, NROW * QC, NROW * job[1]))
                    ins = dve.tensor_copy(mt[:, :, :], bank[0:HG * TPC, 0:HALF * PARTS].bitcast(BF16)
                                    .rearrange("p (a x) -> p a x", a=PARTS))
                elif kind == "w":
                    k = CH // QT
                    if job[1] == 0:
                        dve.wait_ge(s_oc, val(go, QC, 0))
                    view = osb[:, :].rearrange("p (q r) -> p q r", r=P)[:, :, k * job[1]:k * job[1] + k]
                    ins = dve.tensor_tensor(view, bank.rearrange("p (r q) -> p q r", q=QT), view, ALU.add)
                else:
                    n = job[1]
                    rows = bank.rearrange("p (q h d) -> p q h d", q=TPC, h=HG)
                    dve.reciprocal(rcp[:, TPC * n:TPC * n + TPC, :], rows[:, :, :, HD]).then_inc(s_rcp, 1)
                    dve.wait_ge(s_rcp, val(go, QC, n + 1 - QC))
                    if n == 0:
                        dve.wait_ge(s_out, val(go, 16, 0))
                    ins = dve.tensor_tensor(on[:, TPC * n:TPC * n + TPC, :, :], rows[:, :, :, 0:HD],
                                            rcp[:, TPC * n:TPC * n + TPC, :].unsqueeze(3).to_broadcast([P, TPC, HG, HD]),
                                            ALU.mult)
                ins.then_inc(s_taken, 1)

            def split_rows(go, qc, at):
                dve.wait_ge(s_taken, val(go, NJ, at))
                link(dve.tensor_reduce(mneg[:, :], mx[:, :, :], AX.X, ALU.max, negate=True), go, 4 * qc + 1)
                link(dve.tensor_copy(mparts[:, 0, :], mneg[:, :]), go, 4 * qc + 2)
                link(dve.tensor_tensor(mrest[:, :], mneg[:, :], mparts[:, 0, :], ALU.subtract), go, 4 * qc + 3)
                link(dve.tensor_copy(mparts[:, 1, :], mrest[:, :]), go, 4 * qc + 4)
                dve.tensor_tensor(mparts[:, 2, :], mrest[:, :], mparts[:, 1, :], ALU.subtract).then_inc(s_mready, 1)

            def copy_out(go, qc):
                dve.wait_ge(s_pv, val(go, STEPS, QT * (qc + 1) + PV0))
                dve.tensor_copy(osb[:, CH * qc:CH * (qc + 1)], ops[:, :]).then_inc(s_oc, 1)

            def stream(go, jobs, at, outs=()):
                outs = list(outs)
                for i, job in enumerate(jobs):
                    if outs and outs[0][0] == i:
                        copy_out(*outs.pop(0)[1:])
                    take(go, job, at + i)
                    if job in CLOSING:
                        split_rows(go, job[1], at + i + 1)
                for o in outs:
                    copy_out(*o[1:])

            dve.sem_inc(s_out, 16)
            stream((0, 0), JA, 0)
            stream((0, 0), JB[len(JWT):] + JC[:EARLY], AT_B + len(JWT))
            rest = [(3, 0), (QT * 4 + 4, 1)]
            with dve.Fori(0, B * NG - 1) as g:
                stream((g, 0), JC[EARLY:], AT_C + EARLY, [(k, (g, 0), qc) for k, qc in rest])
                stream((g, 1), JA, AT_A, [(0 if START else PER - 1, (g, 0), 2)])
                stream((g, 1), JB + JC[:EARLY], AT_B, [(0, (g, 0), 3)])
            last = (0, B * NG - 1)
            stream(last, JC[EARLY:], AT_C + EARLY, [(k, last, qc) for k, qc in rest])
            copy_out(last, 2)
            copy_out(last, 3)
            for i, job in enumerate(JWT):
                take((0, B * NG), job, AT_A + i)


def experts(nc, t, x, bo, w1, b1, w2, b2, wr, br, gamma, beta, out):
    with ExitStack() as ctx:
        sb = lambda n, s, d: ctx.enter_context(nc.sbuf_tensor(n, s, d))
        sem = lambda n: ctx.enter_context(nc.semaphore(n))
        ident = t["ident"]
        at = sb("at", [P, 2, TPC, NG, GD], F32)
        xb = sb("xb", [P, 2, TPC, E], F32)
        xo = sb("xo", [P, 2, TPC, E], F32)
        att = sb("att_t", [P, 2, KE, CH], F32)
        x1 = sb("x1", [P, QT, E], F32)
        x1t = sb("x1t", [P, KE, S], F32)
        rows = sb("rows", [P, 3, E], F32)
        wrs = sb("wrs", [P, KE, NE], F32)
        brs = sb("brs", [1, NE], F32)
        ones = sb("ones", [P, P], F32)
        epst = sb("epst", [P, 1], F32)
        stats = sb("stats", [P, TPC, 6], F32)
        mv = sb("mv", [P, TPC, 2], F32)
        sd = sb("sd", [P, TPC], F32)
        rs = sb("rs", [P, TPC], F32)
        xm = sb("xm", [P, KE], F32)
        lg = sb("lg", [1, NE], F32)
        tiny = sb("tiny_r", [1, 8], F32)
        ex = sb("ex", [1, NE], F32)
        rw = sb("rw", [1, NE], F32)
        top = sb("top", [1, 8], F32)
        idx = sb("idx", [1, 8], U32)
        tw = sb("tw", [1, TOPK], F32)
        wb = sb("wb", [P, TOPK], F32)
        w1s = sb("w1s", [P, TOPK, KE, F], F32)
        w2s = sb("w2s", [P, TOPK, KF, E], F32)
        b1s = sb("b1s", [P, TOPK, KF], F32)
        b2s = sb("b2s", [P, TOPK, E], F32)
        bsum = sb("bsum", [P, E], F32)
        hid = sb("hid", [P, 2, KF, CH], F32)
        y = sb("y", [P, 2, TPC, E], F32)
        z = sb("z", [P, 2, TPC, E], F32)
        tp = ctx.enter_context(nc.psum_tensor("tp_ps", [P, 2, CH], F32))
        hp = ctx.enter_context(nc.psum_tensor("hp_ps", [P, 2, CH], F32))
        op = ctx.enter_context(nc.psum_tensor("op_ps", [P, 2, TPC // 2, CH], F32))
        (s_c, s_at, s_ata, s_atv, s_op, s_xo, s_x1, s_ch, s_sd, s_var, s_xt, s_xta, s_xtv, s_xm, s_xmc, s_lg, s_ex,
         s_neg, s_top, s_neg2, s_ex2, s_tw, s_wb, s_wbc, s_idx, s_we, s_h, s_hid, s_o, s_y, s_z1, s_cst,
         s_bs, s_b2) = [sem(n) for n in (
             "consts", "att_turned", "att_by_act", "att_by_dve", "proj_done", "xo_ready", "x1_ready",
             "dve_chain", "sd_ready", "var_ready", "x1_turned", "x1t_by_act", "x1t_by_dve", "mean_done", "mean_copied",
             "logits_done", "exp_ready", "neg_ready", "top_ready", "neg2_ready", "exp2_ready", "tw_ready", "wb_done",
             "wb_copied", "index_ready", "expert_loaded", "hidden_done", "gelu_done", "expert_done", "y_ready",
             "z_scaled", "const_set", "bsum_ready", "b2_used")]
        s_ld = [sem(f"tile_loaded{i}") for i in range(2)]
        s_st = [sem(f"out_stored{i}") for i in range(2)]
        s_st_ready, s_pz = sem("out_ready"), sem("pool_chain")
        block = ctx.enter_context(nc.Block())
        NCONST = 5

        @block.sync
        def _(sp):
            with nc.allow_non_contiguous_dma("small tables"):
                for i, row in enumerate((bo, gamma, beta)):
                    sp.dma_start(rows[:, i, :], row.partition_broadcast(P)).then_inc(s_c, 16)
                sp.dma_start(wrs[:, :, :], wr.rearrange("(k p) e -> p k e", p=P)).then_inc(s_c, 16)
                sp.dma_start(brs[:, :], br.rearrange("(a e) -> a e", a=1)).then_inc(s_c, 16)
                for b in range(B):
                    for c in range(QC):
                        n = b * QC + c
                        if n >= 2:
                            sp.wait_ge(s_at, 2 * (n - 1))
                            sp.wait_ge(s_xo, n - 1)
                        for g in range(NG):
                            sp.dma_start(at[:, n % 2, :, g, :],
                                         t["att"][NG * b + g, CH * c:CH * (c + 1), :].rearrange(
                                             "(t p) c -> p t c", p=P)).then_inc(s_ld[n % 2], 16)
                        sp.dma_start(xb[:, n % 2, :, :], x[b, CH * c:CH * (c + 1), :].rearrange(
                            "(t p) e -> p t e", p=P)).then_inc(s_ld[n % 2], 16)
                    if b:
                        sp.wait_ge(s_o, b * QC * TOPK)
                        sp.wait_ge(s_bs, b)
                    sp.wait_ge(s_idx, b + 1)
                    for k in range(TOPK):
                        e = sp.value_load(idx[0:1, k:k + 1], min_val=0, max_val=NE - 1)
                        sp.dma_start(w1s[:, k, :, :], w1[bass.ds(e, 1)].rearrange("o (k p) f -> p (o k) f", p=P)
                                     ).then_inc(s_we, 16)
                        sp.dma_start(b1s[:, k, :], b1[bass.ds(e, 1)].rearrange("o (k p) -> p (o k)", p=P)).then_inc(s_we, 16)
                        sp.dma_start(w2s[:, k, :, :], w2[bass.ds(e, 1)].rearrange("o (k p) d -> p (o k) d", p=P)
                                     ).then_inc(s_we, 16)
                        row = b2[bass.ds(e, 1)]
                        sp.dma_start(b2s[0:1, k, :], row).then_inc(s_we, 16)
                    for c in range(QC):
                        n = b * QC + c
                        sp.wait_ge(s_st_ready, n + 1)
                        sp.dma_start(out[b, CH * c:CH * (c + 1), :].rearrange("(t p) e -> p t e", p=P), z[:, n % 2, :, :]
                                     ).then_inc(s_st[n % 2], 16)
                for i in range(2):
                    sp.wait_ge(s_st[i], 8 * B * QC)

        @block.gpsimd
        def _(pool):
            pool.memset(ones[:, :], 1.0).then_inc(s_cst, 1)
            pool.memset(epst[:, :], EPS).then_inc(s_cst, 1)
            pool.wait_ge(s_c, 16 * NCONST)
            for b in range(B):
                for c in range(QC):
                    n = b * QC + c
                    pool.wait_ge(s_ld[n % 2], 16 * (NG + 1) * (n // 2 + 1))
                    if n >= 2:
                        pool.wait_ge(s_x1, n - 1)
                    for i in range(TPC):
                        ins = pool.tensor_tensor(xo[:, n % 2, i, :], xb[:, n % 2, i, :], rows[:, 0, :], ALU.add)
                    ins.then_inc(s_xo, 1)
                for c in range(QC):
                    n = b * QC + c
                    pool.wait_ge(s_z1, n + 1)
                    for i in range(TPC):
                        pool.tensor_tensor(z[:, n % 2, i, :], z[:, n % 2, i, :], rows[:, 1, :], ALU.mult).then_inc(s_pz, 1)
                    pool.wait_ge(s_pz, TPC * (3 * n + 1))
                    for i in range(TPC):
                        pool.tensor_tensor(z[:, n % 2, i, :], z[:, n % 2, i, :], rows[:, 2, :], ALU.add).then_inc(s_pz, 1)
                    pool.wait_ge(s_pz, TPC * (3 * n + 2))
                    for i in range(TPC):
                        pool.tensor_tensor(z[:, n % 2, i, :], z[:, n % 2, i, :], x1[:, TPC * c + i, :], ALU.add).then_inc(s_pz, 1)

        @block.tensor
        def _(pe):
            pe.wait_ge(s_cst, 2)
            pe.wait_ge(s_c, 16 * NCONST)
            for b in range(B):
                for c in range(QC):
                    n = b * QC + c
                    pe.wait_ge(s_ld[n % 2], 16 * (NG + 1) * (n // 2 + 1))
                    for k in range(KE):
                        if n:
                            pe.wait_ge((s_xta, s_xtv)[k], n)
                        for i in range(TPC):
                            mm = pe.transpose(tp[:, k, P * i:P * i + P],
                                              at[:, n % 2, i, :, :].rearrange("p g c -> p (g c)")[:, P * k:P * k + P],
                                              ident[:, :])
                        mm.then_inc(s_at, 1)
                    pe.wait_ge(s_ata, n + 1)
                    pe.wait_ge(s_atv, n + 1)
                    if c:
                        pe.wait_ge(s_x1, n)
                    elif b:
                        pe.wait_ge(s_y, b * QC * TOPK)
                    for i in range(TPC):
                        for k in range(KE):
                            mm = pe.matmul(op[:, 0, i // 2, E * (i % 2):E * (i % 2) + E], att[:, n % 2, k, P * i:P * i + P],
                                           t["wot"][:, k, :], start=(k == 0), stop=(k == KE - 1))
                    mm.then_inc(s_op, 1)
                    pe.wait_ge(s_x1, n + 1)
                    for k in range(KE):
                        for i in range(TPC):
                            mm = pe.transpose(tp[:, k, P * i:P * i + P], x1[:, TPC * c + i, P * k:P * k + P], ident[:, :])
                        mm.then_inc(s_xt, 1)
                pe.wait_ge(s_xta, (b + 1) * QC)
                pe.wait_ge(s_xtv, (b + 1) * QC)
                for k in range(KE):
                    for i in range(QT):
                        mm = pe.matmul(hp[:, 0, k:k + 1], x1[:, i, P * k:P * k + P], ones[:, 0:1],
                                       start=(i == 0), stop=(i == QT - 1))
                mm.then_inc(s_xm, 1)
                pe.wait_ge(s_xmc, b + 1)
                for k in range(KE):
                    mm = pe.matmul(hp[0:1, 1, 0:NE], xm[:, k:k + 1], wrs[:, k, :], start=(k == 0), stop=(k == KE - 1))
                mm.then_inc(s_lg, 1)
                pe.wait_ge(s_tw, b + 1)
                pe.matmul(hp[:, 0, 0:TOPK], ones[0:1, :], tw[:, :], start=True, stop=True).then_inc(s_wb, 1)
                pe.wait_ge(s_wbc, b + 1)
                pe.wait_ge(s_we, 64 * TOPK * (b + 1))
                for k in range(TOPK):
                    mm = pe.matmul(hp[:, 1, E * k:E * k + E], ones[0:1, :], b2s[0:1, k, :], start=True, stop=True)
                mm.then_inc(s_b2, 1)
                pe.wait_ge(s_bs, b + 1)
                for m in range(QC * TOPK + 1):
                    n = b * QC * TOPK + m
                    if m < QC * TOPK:
                        c, k = divmod(m, TOPK)
                        for f in range(KF):
                            i = KF * n + f
                            if m or f >= 2:
                                pe.wait_ge(s_hid, i - 1)
                            for kk in range(KE):
                                mm = pe.matmul(hp[:, f % 2, :], w1s[:, k, kk, P * f:P * f + P],
                                               x1t[:, kk, CH * c:CH * (c + 1)], start=(kk == 0), stop=(kk == KE - 1))
                            mm.then_inc(s_h, 1)
                    if m:
                        c, k = divmod(m - 1, TOPK)
                        pe.wait_ge(s_hid, KF * n)
                        if m >= 3:
                            pe.wait_ge(s_y, n - 2)
                        for i in range(TPC):
                            for f in range(KF):
                                mm = pe.matmul(op[:, k, i // 2, E * (i % 2):E * (i % 2) + E],
                                               hid[:, (n - 1) % 2, f, P * i:P * i + P], w2s[:, k, f, :],
                                               start=(f == 0), stop=(f == KF - 1))
                        mm.then_inc(s_o, 1)

        @block.scalar
        def _(act):
            act.wait_ge(s_cst, 2)

            def deviations(n):
                act.wait_ge(s_var, n + 1)
                act.activation(sd[:, :], mv[:, :, 1], ACT.Sqrt, bias=epst[:, 0:1]).then_inc(s_sd, 1)

            for b in range(B):
                base = b * 3 * QC
                for c in range(QC):
                    n = b * QC + c
                    act.wait_ge(s_at, 2 * n + 1)
                    if n >= 2:
                        act.wait_ge(s_op, n - 1)
                    act.activation(att[:, n % 2, 0, :], tp[:, 0, :], ACT.Copy).then_inc(s_ata, 1)
                    deviations(base + c)
                    act.wait_ge(s_xt, 2 * n + 1)
                    if b and c == 0:
                        act.wait_ge(s_o, b * QC * TOPK)
                    act.activation(x1t[:, 0, CH * c:CH * (c + 1)], tp[:, 0, :], ACT.Copy).then_inc(s_xta, 1)
                act.wait_ge(s_neg, b + 1)
                act.activation(ex[:, :], lg[:, :], ACT.Exp, bias=tiny[0:1, 0:1]).then_inc(s_ex, 1)
                act.wait_ge(s_neg2, b + 1)
                act.activation(tiny[0:1, 4:6], top[0:1, 0:2], ACT.Exp, bias=tiny[0:1, 3:4]).then_inc(s_ex2, 1)
                for m in range(QC * TOPK):
                    n = b * QC * TOPK + m
                    c, k = divmod(m, TOPK)
                    for f in range(KF):
                        act.wait_ge(s_h, KF * n + f + 1)
                        if f == 0 and m >= 2:
                            act.wait_ge(s_o, n - 1)
                        act.activation(hid[:, n % 2, f, :], hp[:, f % 2, :], ACT.Gelu,
                                       bias=b1s[:, k, f:f + 1]).then_inc(s_hid, 1)
                    if k == 1 and c:
                        deviations(base + QC + 2 * (c - 1))
                        deviations(base + QC + 2 * (c - 1) + 1)
                deviations(base + 3 * QC - 2)
                deviations(base + 3 * QC - 1)

        @block.vector
        def _(dve):
            chain = Count(s_ch)
            norms = [0]

            def norm(src, dst):
                for i in range(TPC):
                    ins = dve.bn_stats(stats[:, i, :], src(i))
                chain.link(dve, ins)
                for i in range(TPC):
                    ins = dve.bn_aggr(mv[:, i, :], stats[:, i, :])
                ins.then_inc(s_var, 1)
                norms[0] += 1
                dve.wait_ge(s_sd, norms[0])
                chain.link(dve, dve.reciprocal(rs[:, :], sd[:, :]))
                for i in range(TPC):
                    ins = dve.tensor_scalar(dst(i), src(i), mv[:, i, 0:1], rs[:, i:i + 1], ALU.subtract, ALU.mult)
                return ins

            for b in range(B):
                for c in range(QC):
                    n = b * QC + c
                    dve.wait_ge(s_at, 2 * n + 2)
                    if n >= 2:
                        dve.wait_ge(s_op, n - 1)
                    dve.tensor_copy(att[:, n % 2, 1, :], tp[:, 1, :]).then_inc(s_atv, 1)
                    dve.wait_ge(s_op, n + 1)
                    dve.wait_ge(s_xo, n + 1)
                    for i in range(TPC):
                        ins = dve.tensor_tensor(y[:, n % 2, i, :], op[:, 0, i // 2, E * (i % 2):E * (i % 2) + E],
                                                xo[:, n % 2, i, :], ALU.add)
                    chain.link(dve, ins)
                    norm(lambda i: y[:, n % 2, i, :], lambda i: x1[:, TPC * c + i, :]).then_inc(s_x1, 1)
                    dve.wait_ge(s_xt, 2 * n + 2)
                    dve.tensor_copy(x1t[:, 1, CH * c:CH * (c + 1)], tp[:, 1, :]).then_inc(s_xtv, 1)
                dve.wait_ge(s_xm, b + 1)
                dve.tensor_scalar(xm[:, :], hp[:, 0, 0:KE], 1.0 / S, None, ALU.mult).then_inc(s_xmc, 1)
                dve.wait_ge(s_lg, b + 1)
                chain.link(dve, dve.tensor_tensor(lg[:, :], hp[0:1, 1, 0:NE], brs[:, :], ALU.add))
                dve.tensor_reduce(tiny[0:1, 0:1], lg[:, :], AX.X, ALU.max, negate=True).then_inc(s_neg, 1)
                dve.wait_ge(s_ex, b + 1)
                chain.link(dve, dve.tensor_reduce(tiny[0:1, 1:2], ex[:, :], AX.X, ALU.add))
                chain.link(dve, dve.reciprocal(tiny[0:1, 2:3], tiny[0:1, 1:2]))
                chain.link(dve, dve.tensor_scalar(rw[:, :], ex[:, :], tiny[0:1, 2:3], None, ALU.mult))
                chain.link(dve, dve.max(top[:, :], rw[:, :]))
                dve.max_index(idx[:, :], top[:, :], rw[:, :]).then_inc(s_idx, 1)
                dve.tensor_scalar(tiny[0:1, 3:4], top[0:1, 0:1], -1.0, None, ALU.mult).then_inc(s_neg2, 1)
                dve.wait_ge(s_ex2, b + 1)
                chain.link(dve, dve.tensor_reduce(tiny[0:1, 6:7], tiny[0:1, 4:6], AX.X, ALU.add))
                chain.link(dve, dve.reciprocal(tiny[0:1, 7:8], tiny[0:1, 6:7]))
                dve.tensor_scalar(tw[:, :], tiny[0:1, 4:6], tiny[0:1, 7:8], None, ALU.mult).then_inc(s_tw, 1)
                dve.wait_ge(s_wb, b + 1)
                dve.tensor_copy(wb[:, :], hp[:, 0, 0:TOPK]).then_inc(s_wbc, 1)
                dve.wait_ge(s_wbc, b + 1)
                dve.wait_ge(s_b2, b + 1)
                chain.link(dve, dve.tensor_scalar(bsum[:, :], hp[:, 1, 0:E], wb[:, 0:1], None, ALU.mult))
                dve.scalar_tensor_tensor(out=bsum[:, :], in0=hp[:, 1, E:2 * E], scalar=wb[:, 1:2], in1=bsum[:, :],
                                         op0=ALU.mult, op1=ALU.add).then_inc(s_bs, 1)
                dve.wait_ge(s_bs, b + 1)
                for c in range(QC):
                    n = b * QC + c
                    for i in range(TPC):
                        ins = dve.tensor_tensor(y[:, n % 2, i, :], x1[:, TPC * c + i, :], bsum[:, :], ALU.add)
                    chain.link(dve, ins)
                    for k in range(TOPK):
                        dve.wait_ge(s_o, TOPK * n + k + 1)
                        for i in range(TPC):
                            ins = dve.scalar_tensor_tensor(out=y[:, n % 2, i, :],
                                                           in0=op[:, k, i // 2, E * (i % 2):E * (i % 2) + E],
                                                           scalar=wb[:, k:k + 1], in1=y[:, n % 2, i, :],
                                                           op0=ALU.mult, op1=ALU.add)
                        ins.then_inc(s_y, 1)
                        dve.wait_ge(s_y, TOPK * n + k + 1)
                    if n >= 2:
                        dve.wait_ge(s_st[n % 2], 16 * (n // 2))
                    norm(lambda i: y[:, n % 2, i, :], lambda i: z[:, n % 2, i, :]).then_inc(s_z1, 1)
                    dve.wait_ge(s_pz, TPC * (3 * n + 3))
                    norm(lambda i: z[:, n % 2, i, :], lambda i: z[:, n % 2, i, :]).then_inc(s_st_ready, 1)


def program(nc, hidden, wq, bq, wk, bk, wv, bv, wo, bo, rel_k, rel_v, w1, b1, w2, b2, wr, br, gamma, beta, out):
    with ExitStack() as ctx:
        sb = lambda n, s, d: ctx.enter_context(nc.sbuf_tensor(n, s, d))
        dram = lambda n, s, d: nc.dram_tensor(n, s, d, kind="Internal").ap()
        t = {
            "ident": sb("ident", [P, P], F32),
            "identb": sb("identb", [P, P], BF16),
            "ident3": sb("ident3", [P, 3, P], F32),
            "masked": sb("masked", [P, 4, P], F32),
            "line": sb("line", [KR, 2, LINE], BF16),
            "rvt": sb("rvt", [P, 2, HALF, HP], F32),
            "wot": sb("wot", [P, KE, E], F32),
            "tiny": sb("tiny", [1, 1], F32),
            "line_v": dram("line_v", [2, LINE, HP], F32),
            "qp": dram("q_parts", [B * NG, PARTS, QC, GD, CH], BF16),
            "kp": dram("k_parts", [B * NG, 2, PARTS, GD, S], BF16),
            "vp": dram("v_padded", [B * NG, S, 2, HG * HP], F32),
            "att": dram("attended", [B * NG, S, GD], F32),
        }
        setup(nc, t, rel_k, rel_v)
        project(nc, t, hidden, wq, bq, wk, bk, wv, bv, wo, rel_k, rel_v)
        attention(nc, t)
        experts(nc, t, hidden, bo, w1, b1, w2, b2, wr, br, gamma, beta, out)


_INS = ["L0_attn_hidden_states", "L0_attn_Wq", "L0_attn_bq", "L0_attn_Wk", "L0_attn_bk", "L0_attn_Wv", "L0_attn_bv",
        "L0_attn_Wo", "L0_attn_bo", "L0_attn_rel_k", "L0_attn_rel_v", "L0_ffn_W1", "L0_ffn_b1", "L0_ffn_W2", "L0_ffn_b2",
        "L0_ffn_Wr", "L0_ffn_br", "L0_ffn_gamma", "L0_ffn_beta"]


def kernel(**inputs):
    import numpy as _np
    import concourse.bacc as _bacc
    from concourse import mybir as _mybir
    from concourse.bass_utils import run_bass_kernel_spmd as _run

    nc = _bacc.Bacc("TRN2", target_bir_lowering=False, num_devices=1)
    arrays, args = {}, []
    for name in _INS:
        a = _np.ascontiguousarray(inputs[name])
        arrays[f"in_{name}"] = a
        args.append(nc.dram_tensor(f"in_{name}", a.shape, _mybir.dt.from_np(a.dtype), kind="ExternalInput").ap())
    args.append(nc.dram_tensor("out", [B, S, E], F32, kind="ExternalOutput").ap())
    program(nc, *args)
    return _run(nc, [arrays], core_ids=[0]).results[0]["out"]
```

```python
from contextlib import ExitStack

import concourse.bass as bass
from concourse import mybir

F32 = mybir.dt.float32
BF16 = mybir.dt.bfloat16
U32 = mybir.dt.uint32
ALU = mybir.AluOpType
ACT = mybir.ActivationFunctionType
AX = mybir.AxisListType

P = 128
B, S, E = 2, 2048, 256
H, HD = 16, 16
HG = 4
NG = H // HG
GD = HG * HD
HP = 32
MR = 20
NREL = 2 * MR + 1
QT = S // P
CH = 512
QC = S // CH
TPC = CH // P
KE = E // P
PARTS = 3
Q_PART = [0, 0, 1, 1, 0, 2]
K_PART = [0, 1, 0, 1, 2, 0]
KR = HD * len(Q_PART)
SCALE = HD ** -0.5
HALF = P // 2
LINE = 2 * P
F = 1024
NE = 8
TOPK = 2
KF = F // P
EPS = 1e-5


class Count:

    def __init__(self, sem):
        self.sem, self.n = sem, 0

    def inc(self, ins, by=1):
        ins.then_inc(self.sem, by)
        self.n += by

    def link(self, eng, ins):
        self.inc(ins)
        eng.wait_ge(self.sem, self.n)


def relative_lines(eng, chain, line, rel):
    first, last = rel[:, 0:1], rel[:, NREL - 1:NREL]
    chain.link(eng, eng.memset(line[:, :, :], 0.0))
    o = P - 1
    far0 = o - MR
    eng.tensor_scalar(line[:, 0, 0:far0], line[:, 0, 0:far0], first, last, ALU.add, ALU.subtract)
    eng.tensor_scalar(line[:, 0, far0:o + MR], rel[:, 0:NREL - 1], last, None, ALU.subtract)
    eng.tensor_scalar(line[:, 0, LINE - MR:LINE], rel[:, 1:MR + 1], first, None, ALU.subtract)
    eng.tensor_scalar(line[:, 1, 0:MR - 1], rel[:, MR + 1:NREL - 1], last, None, ALU.subtract)
    eng.tensor_scalar(line[:, 1, o - MR + 1:o + MR + 1], rel[:, 1:NREL], first, None, ALU.subtract)
    chain.link(eng, eng.tensor_scalar(line[:, 1, o + MR + 1:LINE], line[:, 1, o + MR + 1:LINE],
                                      last, first, ALU.add, ALU.subtract))


def split_parts(eng, chain, parts, rest, src):
    chain.link(eng, eng.tensor_copy(parts[0], src))
    chain.link(eng, eng.tensor_tensor(rest, src, parts[0], ALU.subtract))
    chain.link(eng, eng.tensor_copy(parts[1], rest))
    chain.link(eng, eng.tensor_tensor(parts[2], rest, parts[1], ALU.subtract))


def setup(nc, t, rel_k, rel_v):
    with ExitStack() as ctx:
        sb = lambda n, s, d: ctx.enter_context(nc.sbuf_tensor(n, s, d))
        sem = lambda n: ctx.enter_context(nc.semaphore(n))
        relk = sb("relk", [HD, NREL], F32)
        relv = sb("relv", [HD, NREL], F32)
        linek = sb("linek", [HD, 2, LINE], F32)
        linev = sb("linev", [HD, 2, LINE], F32)
        restk = sb("restk", [HD, 2, LINE], F32)
        partk = sb("partk", [HD, PARTS, 2, LINE], BF16)
        turned = sb("turned", [P, 2, 2, HD], F32)
        ps = ctx.enter_context(nc.psum_tensor("setup_ps", [P, 4, HD], F32))
        s_rel, s_line, s_v = sem("s_rel"), sem("s_line"), sem("s_v")
        s_pool = sem("s_pool")
        s_id, s_idp, s_turn, s_turned, s_store = sem("s_id"), sem("s_idp"), sem("s_turn"), sem("s_turned"), sem("s_store")
        block = ctx.enter_context(nc.Block())

        @block.sync
        def _(sp):
            with nc.allow_non_contiguous_dma("small tables"):
                sp.dma_start(relk[:, :], rel_k.rearrange("r d -> d r")).then_inc(s_rel, 16)
                sp.dma_start(relv[:, :], rel_v.rearrange("r d -> d r")).then_inc(s_rel, 16)
            sp.wait_ge(s_line, 1)
            for r, part in enumerate(K_PART):
                sp.dma_start(t["line"][HD * r:HD * (r + 1), :, :], partk[:, part, :, :]).then_inc(s_store, 16)
            sp.wait_ge(s_turned, 1)
            sp.dma_start(t["line_v"].rearrange("k (h p) d -> p k h d", p=P), turned[:, :, :, :]).then_inc(s_store, 16)
            sp.wait_ge(s_store, 16 * (len(K_PART) + 1))
            for kind in range(2):
                src = t["line_v"]
                row = src[kind]
                first = HALF if kind == 0 else 0
                ap = bass.AP(row.tensor, row.offset + first * HD, [[HD, P], [1, HALF * HD]])
                sp.dma_start(t["rvt"][:, kind, :, :].rearrange("p r d -> p (r d)"), ap).then_inc(s_store, 16)
            sp.wait_ge(s_store, 16 * (len(K_PART) + 3))

        @block.gpsimd
        def _(pool):
            pool.memset(t["ident"][:, :], 0.0).then_inc(s_idp, 1)
            pool.wait_ge(s_idp, 1)
            pool.affine_select(out=t["ident"][:, :], in_=t["ident"][:, :], compare_op=ALU.not_equal, fill=1.0,
                               base=0, pattern=[[-1, P]], channel_multiplier=1).then_inc(s_id, 1)
            pool.wait_ge(s_id, 1)
            chain = Count(s_pool)
            chain.link(pool, pool.memset(t["masked"][:, :, :], 0.0))
            for k, (lo, hi) in enumerate([(0, 32), (0, 96), (32, 128), (96, 128)]):
                for q in range(lo // 32, hi // 32):
                    chain.link(pool, pool.tensor_copy(t["masked"][32 * q:32 * q + 32, k, :],
                                                      t["ident"][32 * q:32 * q + 32, :]))
            for j in range(3):
                pool.tensor_copy(t["ident3"][:, j, :], t["ident"][:, :])
            pool.tensor_copy(t["identb"][:, :], t["ident"][:, :])

        @block.vector
        def _(dve):
            chain = Count(s_v)
            dve.wait_ge(s_rel, 32)
            relative_lines(dve, chain, linek, relk)
            split_parts(dve, chain, [partk[:, i, :, :] for i in range(PARTS)], restk[:, :, :], linek[:, :, :])
            dve.memset(t["tiny"][0:1, 0:1], 0.0).then_inc(s_line, 1)
            relative_lines(dve, chain, linev, relv)
            dve.memset(t["tiny"][0:1, 0:1], 0.0).then_inc(s_line, 1)
            dve.wait_ge(s_turn, 1)
            dve.tensor_copy(turned[:, :, :, :], ps[:, :, :].rearrange("p (k h) d -> p k h d", k=2)).then_inc(s_turned, 1)

        @block.tensor
        def _(pe):
            pe.wait_ge(s_id, 1)
            pe.wait_ge(s_line, 2)
            for kind in range(2):
                for half in range(2):
                    mm = pe.transpose(ps[:, 2 * kind + half, :], linev[:, kind, P * half:P * half + P],
                                      t["ident"][0:HD, 0:HD])
            mm.then_inc(s_turn, 1)


def project(nc, t, x, wq, bq, wk, bk, wv, bv, wo, rel_k, rel_v):
    with ExitStack() as ctx:
        sb = lambda n, s, d: ctx.enter_context(nc.sbuf_tensor(n, s, d))
        sem = lambda n: ctx.enter_context(nc.semaphore(n))
        ident = t["ident"]
        wn = sb("wn", [P, 4, KE, E], F32)
        wt = sb("wt", [P, 3, KE, E], F32)
        bcol = sb("bcol", [P, 2, KE], F32)
        rcol = sb("rcol", [P, 2], F32)
        bias = sb("bias", [P, 3, KE], F32)
        vrow = sb("vrow", [P, E], F32)
        rrow = sb("rrow", [P, 2, HD], F32)
        vbias = sb("vbias", [P, 2, H, HD], F32)
        xn = sb("xn", [P, 2, TPC, E], F32)
        xt = sb("xt", [P, 2, KE, CH], F32)
        full = sb("full", [P, 2, 3, KE, CH], F32)
        rest = sb("rest", [P, 3, KE, CH], F32)
        parts = sb("parts", [P, 2, 3, PARTS, KE, CH], BF16)
        vst = sb("vst", [P, 2, TPC, NG, 2, HG, HP], F32)
        ps = ctx.enter_context(nc.psum_tensor("proj_ps", [P, 8, CH], F32))
        (s_w, s_wt, s_wtc, s_xt, s_xta, s_xtv, s_qk, s_v, s_full, s_hi, s_r1, s_mid, s_lo, s_vst, s_bias,
         s_vinit) = [sem(n) for n in (
             "w_loaded", "w_turned", "w_copied", "x_turned", "xt_by_act", "xt_by_dve", "qk_done", "v_done",
             "full_ready", "hi_ready", "rest_ready", "mid_ready", "lo_ready", "v_staged", "bias_ready", "v_init")]
        s_x = [sem(f"x_loaded{i}") for i in range(2)]
        s_st = [sem(f"stored{i}") for i in range(2)]
        s_bias_chain = sem("bias_chain")
        block = ctx.enter_context(nc.Block())
        s_b = sem("biases_loaded")
        NC = QC
        CHUNKS = [(b * NC + c, b, c) for b in range(B) for c in range(NC)]
        STORES = 3 * 4 + NG
        B_LOADS = 16 * (5 + 2 * P // HD)

        def stored(n):
            return 16 * STORES * (n // 2 + 1)

        @block.sync
        def _(sp):
            def load(n):
                b, c = divmod(n, NC)
                if n >= 2:
                    sp.wait_ge(s_xt, 2 * (n - 1))
                sp.dma_start(xn[:, n % 2, :, :], x[b, CH * c:CH * (c + 1), :].rearrange("(t p) e -> p t e", p=P)
                             ).then_inc(s_x[n % 2], 16)

            def store(n):
                b, c = divmod(n, NC)
                for kind in range(3):
                    sp.wait_ge(s_lo, 3 * n + kind + 1)
                    for m in range(KE):
                        for h in range(2):
                            src = parts[HALF * h:HALF * h + HALF, n % 2, kind, :, m, :]
                            g = b * NG + (2 * m + h)
                            dst = (t["qp"][g, :, c, :, :] if kind == 0 else
                                   t["kp"][g, kind - 1, :, :, CH * c:CH * (c + 1)])
                            sp.dma_start(dst.rearrange("a p t -> p a t"), src).then_inc(s_st[n % 2], 16)
                sp.wait_ge(s_vst, 2 * TPC * (n + 1))
                for hg in range(NG):
                    dst = t["vp"][b * NG + hg, CH * c:CH * (c + 1), :, :].rearrange("(t p) v x -> p t v x", p=P)
                    sp.dma_start(dst, vst[:, n % 2, :, hg, :, :, :].rearrange("p t v h d -> p t v (h d)")
                                 ).then_inc(s_st[n % 2], 16)

            for i, w in enumerate((wq, wk, wv, wo)):
                sp.dma_start(wn[:, i, :, :], w.rearrange("(m p) e -> p m e", p=P)).then_inc(s_w, 16)
            load(0)
            load(1)
            with nc.allow_non_contiguous_dma("small biases"):
                for i, b in enumerate((bq, bk)):
                    sp.dma_start(bcol[:, i, :], b.rearrange("(m p) -> p m", p=P)).then_inc(s_b, 16)
                for i in range(P // HD):
                    sp.dma_start(rcol[HD * i:HD * i + HD, 0:1], rel_k[0:1, :].rearrange("r d -> d r")).then_inc(s_b, 16)
                    sp.dma_start(rcol[HD * i:HD * i + HD, 1:2],
                                 rel_k[NREL - 1:NREL, :].rearrange("r d -> d r")).then_inc(s_b, 16)
                sp.dma_start(vrow[:, :], bv.partition_broadcast(P)).then_inc(s_b, 16)
                sp.dma_start(rrow[:, 0, :], rel_v[0, :].partition_broadcast(P)).then_inc(s_b, 16)
                sp.dma_start(rrow[:, 1, :], rel_v[NREL - 1, :].partition_broadcast(P)).then_inc(s_b, 16)
            for n in range(1, B * NC):
                if n + 1 < B * NC:
                    load(n + 1)
                store(n - 1)
            store(B * NC - 1)
            for i in range(2):
                sp.wait_ge(s_st[i], stored(B * NC - 2 + i))

        @block.tensor
        def _(pe):
            pe.wait_ge(s_w, 16 * 4)
            for i in range(4):
                for m in range(KE):
                    for k in range(KE):
                        mm = pe.transpose(ps[:, i, CH // 2 * k + P * m:CH // 2 * k + P * m + P],
                                          wn[:, i, m, P * k:P * k + P], ident[:, :])
                mm.then_inc(s_wt, 1)
            pe.wait_ge(s_wtc, 4)
            for n, b, c in CHUNKS:
                pe.wait_ge(s_x[n % 2], 16 * (n // 2 + 1))
                for k in range(KE):
                    if n:
                        pe.wait_ge((s_xta, s_xtv)[k], n)
                    for tt in range(TPC):
                        mm = pe.transpose(ps[:, k, P * tt:P * tt + P], xn[:, n % 2, tt, P * k:P * k + P], ident[:, :])
                    mm.then_inc(s_xt, 1)
                pe.wait_ge(s_xta, n + 1)
                pe.wait_ge(s_xtv, n + 1)
                if n:
                    pe.wait_ge(s_full, 6 * n)
                for i in range(2):
                    for m in range(KE):
                        for k in range(KE):
                            mm = pe.matmul(ps[:, 2 + 2 * i + m, :], wt[:, i, k, P * m:P * m + P], xt[:, n % 2, k, :],
                                           start=(k == 0), stop=(k == KE - 1))
                        mm.then_inc(s_qk, 1)
                if n:
                    pe.wait_ge(s_vst, 2 * TPC * n)
                for tt in range(TPC):
                    for k in range(KE):
                        mm = pe.matmul(ps[:, 6 + tt // 2, E * (tt % 2):E * (tt % 2) + E],
                                       xt[:, n % 2, k, P * tt:P * tt + P], wt[:, 2, k, :],
                                       start=(k == 0), stop=(k == KE - 1))
                    if tt % 2:
                        mm.then_inc(s_v, 1)

        @block.scalar
        def _(act):
            act.wait_ge(s_bias, 1)
            for n, b, c in CHUNKS:
                act.wait_ge(s_xt, 2 * n + 1)
                if n >= 2:
                    act.wait_ge(s_v, 2 * (n - 1))
                act.activation(xt[:, n % 2, 0, :], ps[:, 0, :], ACT.Copy).then_inc(s_xta, 1)
                if n >= 2:
                    act.wait_ge(s_lo, 3 * (n - 1))
                for m in range(KE):
                    act.wait_ge(s_qk, 4 * n + m + 1)
                    act.activation(full[:, n % 2, 0, m, :], ps[:, 2 + m, :], ACT.Identity,
                                   bias=bias[:, 0, m:m + 1], scale=SCALE).then_inc(s_full, 1)
                for m in range(KE):
                    act.wait_ge(s_qk, 4 * n + 3 + m)
                    for v in range(2):
                        act.activation(full[:, n % 2, 1 + v, m, :], ps[:, 4 + m, :], ACT.Identity,
                                       bias=bias[:, 1 + v, m:m + 1]).then_inc(s_full, 1)
                if n >= 2:
                    act.wait_ge(s_st[n % 2], stored(n - 2))
                for kind in range(3):
                    act.wait_ge(s_full, 6 * n + (2 if kind == 0 else 6))
                    act.activation(parts[:, n % 2, kind, 0, :, :], full[:, n % 2, kind, :, :], ACT.Copy).then_inc(s_hi, 1)

        @block.gpsimd
        def _(pool):
            pool.memset(vst[:, :, :, :, :, :, :], 0.0).then_inc(s_vinit, 1)
            pool.wait_ge(s_vinit, 1)
            pool.memset(vst[:, :, :, :, :, :, HD:HD + 1].rearrange("p a t g v h o -> p (a t g v h) o"), 1.0).then_inc(s_vinit, 1)
            for n, b, c in CHUNKS:
                for kind in range(3):
                    pool.wait_ge(s_mid, 3 * n + kind + 1)
                    pool.tensor_tensor(parts[:, n % 2, kind, 2, :, :], rest[:, kind, :, :],
                                       parts[:, n % 2, kind, 1, :, :], ALU.subtract).then_inc(s_lo, 1)

        @block.vector
        def _(dve):
            chain = Count(s_bias_chain)
            dve.wait_ge(s_b, B_LOADS)
            dve.tensor_scalar(bias[:, 0, :], bcol[:, 0, :], SCALE, None, ALU.mult)
            dve.tensor_scalar(bias[:, 1, :], bcol[:, 1, :], rcol[:, 0:1], None, ALU.add)
            chain.link(dve, dve.tensor_scalar(bias[:, 2, :], bcol[:, 1, :], rcol[:, 1:2], None, ALU.add))
            for v in range(2):
                for h in range(H):
                    ins = dve.tensor_tensor(vbias[:, v, h, :], vrow[:, HD * h:HD * h + HD], rrow[:, v, :], ALU.add)
            ins.then_inc(s_bias, 1)
            dve.wait_ge(s_bias, 1)
            for i in range(4):
                dve.wait_ge(s_wt, i + 1)
                dst = wt[:, i, :, :] if i < 3 else t["wot"][:, :, :]
                dve.tensor_copy(dst, ps[:, i, :].rearrange("p (k o) -> p k o", k=KE)).then_inc(s_wtc, 1)

            def split(n):
                for kind in range(3):
                    dve.wait_ge(s_hi, 3 * n + kind + 1)
                    if n:
                        dve.wait_ge(s_lo, 3 * (n - 1) + kind + 1)
                    dve.tensor_tensor(rest[:, kind, :, :], full[:, n % 2, kind, :, :], parts[:, n % 2, kind, 0, :, :],
                                      ALU.subtract).then_inc(s_r1, 1)
                    dve.wait_ge(s_r1, 3 * n + kind + 1)
                    dve.tensor_copy(parts[:, n % 2, kind, 1, :, :], rest[:, kind, :, :]).then_inc(s_mid, 1)

            for n, b, c in CHUNKS:
                dve.wait_ge(s_xt, 2 * n + 2)
                if n >= 2:
                    dve.wait_ge(s_v, 2 * (n - 1))
                dve.tensor_copy(xt[:, n % 2, 1, :], ps[:, 1, :]).then_inc(s_xtv, 1)
                if n:
                    split(n - 1)
                else:
                    dve.wait_ge(s_vinit, 2)
                if n >= 2:
                    dve.wait_ge(s_st[n % 2], stored(n - 2))
                for tt in range(TPC):
                    dve.wait_ge(s_v, 2 * n + tt // 2 + 1)
                    for v in range(2):
                        dve.tensor_tensor(vst[:, n % 2, tt, :, v, :, 0:HD],
                                          ps[:, 6 + tt // 2, E * (tt % 2):E * (tt % 2) + E].rearrange(
                                              "p (g h d) -> p g h d", g=NG, h=HG),
                                          vbias[:, v, :, :].rearrange("p (g h) d -> p g h d", g=NG), ALU.add).then_inc(s_vst, 1)
            split(B * NC - 1)




def band_pieces(kt, qc):
    out = []
    for lo, n, r0, r1 in [(P * kt - 32, 32, 0, 32), (P * kt, 32, 0, 96), (P * kt + 32, 64, 0, P),
                          (P * kt + 96, 32, 32, P), (P * kt + P, 32, 96, P)]:
        if CH * qc <= lo < CH * (qc + 1):
            out.append((lo, n, r0, r1))
    return out


def band_spans(kt, qc):
    return [(lo, m, a, e) for lo, m, r0, r1 in band_pieces(kt, qc)
            for a, e in ([(r0, r1)] if r0 != 32 else [(32, 64), (64, P)])]


MASK = {(0, 32): 0, (0, 96): 1, (32, P): 2, (96, P): 3}


def column_pieces(kt, qc):
    cut = min(max(P * kt + HALF, CH * qc), CH * (qc + 1))
    return [(a, e, kind) for a, e, kind in ((CH * qc, cut, 1), (cut, CH * (qc + 1), 0)) if e > a]


PRB = 4
RING = 3
LEAD = 4
PER = 6


def attention(nc, t):
    with ExitStack() as ctx:
        sb = lambda n, s, d: ctx.enter_context(nc.sbuf_tensor(n, s, d))
        sem = lambda n: ctx.enter_context(nc.semaphore(n))
        qs = sb("qs", [KR + PARTS, QC, HG, CH], BF16)
        ks = sb("ks", [KR + PARTS, 2, HG, S], BF16)
        vs = sb("vs", [P, QT, 2, HG * HP], F32)
        dt = sb("dt", [P, PARTS, QC, HG, CH], BF16)
        rest = sb("corr_less", [P, 2, CH], F32)
        pr = sb("pr", [P, PRB, HG, CH], F32)
        pw = sb("pw", [P, HG, S], F32)
        zeros = sb("zeros", [P, P], BF16)
        osb = sb("osb", [P, S], F32)
        on = sb("on", [P, QT, HG, HD], F32)
        rcp = sb("rcp", [P, QT, HG], F32)
        mx = sb("mx", [P, HG * TPC, QC], F32)
        mneg = sb("mneg", [P, HG * TPC], F32)
        mrest = sb("mrest", [P, HG * TPC], F32)
        mparts = sb("mparts", [P, PARTS, HG * TPC], BF16)
        mt = sb("mt", [HG * TPC, PARTS, P], BF16)
        st = ctx.enter_context(nc.psum_tensor("st_ps", [P, 4, CH], F32))
        sc = ctx.enter_context(nc.psum_tensor("sc_ps", [P, RING, CH], F32))
        ops = ctx.enter_context(nc.psum_tensor("o_ps", [P, CH], F32))
        (s_q, s_k, s_v, s_qmid, s_kmid, s_qlast, s_kend, s_knear, s_krest, s_vnear, s_vrest, s_ones, s_job, s_taken, s_mc, s_mready,
         s_row, s_st, s_exp, s_pv, s_pw, s_oc, s_rcp, s_out, s_pwz, s_seen, s_d0, s_rest, s_split, s_d1, s_held, s_split_odd) = [sem(n) for n in (
             "q_loaded", "k_loaded", "v_loaded", "q_mid_loaded", "k_mid_loaded", "q_last_loaded", "k_end_loaded", "k_near_loaded", "k_rest_loaded",
             "v_near_loaded", "v_rest_loaded", "ones_ready", "job_done", "job_taken", "max_chain", "max_split",
             "max_rows", "st_done", "exp_done", "pv_done", "band_copied", "o_copied", "recip_done",
             "o_stored", "band_zero", "band_seen",
             "corr_first", "corr_rest", "corr_split", "corr_second", "load_held", "corr_split_odd")]
        block = ctx.enter_context(nc.Block())

        STEPS = QC * QT
        NST = STEPS * 2
        ORDER = [[5, 6, 7, 0, 8, 1, 9, 2, 10, 3, 11, 4, 12, 13, 14, 15],
                 [0, 3, 1, 4, 2, 5, 9, 6, 10, 7, 11, 8, 12, 13, 14, 15],
                 [0, 7, 1, 8, 2, 9, 3, 10, 4, 11, 5, 12, 6, 13, 14, 15],
                 [12, 0, 13, 14, 1, 15, 2, 3, 4, 11, 5, 6, 7, 8, 9, 10]]
        NEAR = ORDER[QC - 1].index(TPC - 1) + 1
        END = ORDER[QC - 1].index(QT - 1) + 1
        step = lambda n: (n // QT, ORDER[n // QT][n % QT])
        BAND = [n for n in range(STEPS) if band_pieces(step(n)[1], step(n)[0])]
        band_before = [sum(len(band_spans(step(m)[1], step(m)[0])) for m in BAND if m < n) for n in range(STEPS + 1)]
        NB = band_before[STEPS]
        NROW = 16 * PARTS
        LQ = QC - 1
        NT, LT = TPC * LQ, QT - TPC * LQ

        def corrections(first, tiles):
            k = CH // (HG * tiles)
            return [("d", r, min(k, P - r), first, tiles) for r in range(0, P, k)]

        def first_pass(qc, order):
            return [("m", qc, kc, h, TPC * qc + i) for kc in order for h in range(HG) for i in range(TPC)]

        NW = P * QT // CH
        m1, m2, m3 = (first_pass(qc, range(QC)) for qc in (1, 2, 3))
        LAG = 2
        d0, d1 = corrections(0, NT), corrections(NT, LT)
        m0 = [j for j in first_pass(0, [1]) if j[4] < TPC - 1]
        AHEAD = 8
        mid = first_pass(0, [2])
        apart = (m0[AHEAD:] + mid + first_pass(0, [3]))
        lead, apart = apart[:LEAD], apart[LEAD:]
        k = 2 * len(d0)
        JA = m0[:AHEAD] + lead + [j for three in zip(d0, apart[0:k:2], apart[1:k:2]) for j in three] + apart[k:] + [
            j for j in first_pass(0, [1, 0]) if j not in m0] + [("r", 0)]
        JWT = [("w", i) for i in range(NW)] + [("t", i) for i in range(QC)]
        k = 10
        JB = JWT + [j for i, d in enumerate(d1) for j in m1[k * i:k * i + k] + [d]] + m1[k * len(d1):]
        JC = m2[:LAG] + [("r", 1)] + m2[LAG:] + m3[:LAG] + [("r", 2)] + m3[LAG:] + [("r", 3)]
        NJ = len(JA) + len(JB) + len(JC)
        AT_A, AT_B, AT_C = -len(JWT), len(JA) - len(JWT), len(JA) + len(JB) - len(JWT)
        AT_R = [AT_A + len(JA) - 1] + [AT_C + JC.index(("r", qc)) for qc in range(1, QC)]
        CORR = corrections(0, NT) + corrections(NT, LT)
        NDA, ND = len(corrections(0, NT)), len(CORR)
        EVEN = lambda n: (n + 1) // 2
        correction_number = CORR.index

        def corrected(part, job):
            _, r, places, first, tiles = job
            return dt[:, part, :, :, :].rearrange("p c h (q r) -> p (c h q) r", r=P)[
                :, HG * first:HG * (first + tiles), r:r + places]

        def rest_of(job):
            _, r, places, first, tiles = job
            return rest[:, correction_number(job) % 2, 0:HG * tiles * places].rearrange("p (r x) -> p x r", r=places)

        CLOSING = (JA[-2], m1[-1], m2[-1], m3[-1])
        EARLY = 10
        LATE = EARLY + 75

        def plan(counts, *runs):
            jobs = [(o, at + i, job) for o, at, js in runs for i, job in enumerate(js)]
            steps = []
            for i in range(QT):
                k = counts[min(i, len(counts) - 1)]
                if 1 < len(jobs) <= k and jobs[-1][2][0] == "r":
                    k = len(jobs) - 1
                steps.append([jobs.pop(0) for _ in range(min(k, len(jobs)))])
            assert not jobs, jobs
            return steps

        PLAN_B = plan([2, 3, 5, 6], (0, AT_B, JB), (0, AT_C, JC[:EARLY]))
        PLAN_B0 = plan([6], (0, AT_B + len(JWT), JB[len(JWT):]), (0, AT_C, JC[:EARLY]))
        PLAN_C1 = plan([4] + [5] * 11 + [4], (0, AT_C + EARLY, JC[EARLY:LATE]))
        PLAN_C2 = plan([4], (0, AT_C + LATE, JC[LATE:]), (1, AT_A, JA[:AHEAD]))
        PLAN_C2_END = plan([4], (0, AT_C + LATE, JC[LATE:]))
        PLAN_A = plan([4, 4, 4, 4, 5, 5, 6], (1, AT_A + AHEAD, JA[AHEAD:]))
        NONE = [[] for _ in range(QT)]

        def val(go, per, n):
            return go[0] * per + (go[1] * per + n)

        def wait(eng, s, v):
            if not isinstance(v, int) or v > 0:
                eng.wait_ge(s, v)

        PV0 = PRB

        @block.sync
        def _(sp):
            def load_q(go, a, e, s):
                for r, part in enumerate(Q_PART):
                    src = (t["qp"][go[1], part] if isinstance(go[0], int) else
                           t["qp"][bass.ds(go[0] + go[1], 1), part].rearrange("o c r t -> (o c) r t"))
                    sp.dma_start(qs[HD * r:HD * r + HD, a:e, :, :].rearrange("d c h t -> d (c h) t"),
                                 src[a:e].rearrange("c (h d) t -> d (c h) t", d=HD)
                                 ).then_inc(s, 16)

            def load_k(go, kind, a, e, s):
                for r, part in enumerate(K_PART):
                    src = (t["kp"][go[1], kind, part] if isinstance(go[0], int) else
                           t["kp"][bass.ds(go[0] + go[1], 1), kind, part].rearrange("o c t -> (o c) t"))
                    sp.dma_start(ks[HD * r:HD * r + HD, kind, :, a:e], src[:, a:e].rearrange("(h d) t -> d h t", d=HD)
                                 ).then_inc(s, 16)

            def load_v(go, kind, a, e, s):
                src = (t["vp"][go[1]] if isinstance(go[0], int) else
                       t["vp"][bass.ds(go[0] + go[1], 1)].rearrange("o s v x -> (o s) v x"))
                sp.dma_start(vs[:, a // P:e // P, kind, :], src[a:e, kind, :].rearrange("(k p) x -> p k x", p=P)
                             ).then_inc(s, 16)

            def rows(go, qc):
                sp.wait_ge(s_taken, val(go, NJ, AT_R[qc] + 1))
                send_rows(qc)

            def send_rows(qc):
                for part in range(PARTS):
                    sp.dma_start(qs[KR + part:KR + part + 1, qc, :, :].rearrange("o h t -> o (h t)"), mt[:, part, :]).then_inc(s_row, 16)

            def hold(s, v):
                sp.wait_ge(s, v)
                sp.sem_inc(s_held, 1)

            def load_ahead(go, last):
                if last:
                    hold(s_st, val(last, NST, 2 * QT * 2))
                load_q(go, 0, 2, s_q)
                load_k(go, 1, 0, 2 * CH, s_k)

            def load_first(go, last):
                if last:
                    hold(s_st, val(last, NST, 2 * (QT * 2 + ORDER[2].index(TPC * LQ - 1) + 1)))
                load_k(go, 1, 2 * CH, P * NT, s_kmid)
                if last:
                    hold(s_st, val(last, NST, 2 * QT * LQ))
                load_q(go, 2, LQ, s_qmid)
                if last:
                    hold(s_pv, val(last, STEPS, QT * LQ + PV0))
                load_v(go, 1, 0, P * NT, s_v)
                if last:
                    hold(s_st, val(last, NST, 2 * (QT * LQ + END)))
                load_k(go, 1, P * NT, S, s_kend)
                if last:
                    hold(s_st, val(last, NST, 2 * (QT * LQ + NEAR)))
                load_k(go, 0, 0, CH, s_knear)
                if last:
                    hold(s_pv, val(last, STEPS, QT * LQ + max(END, NEAR) + PV0))
                load_v(go, 1, P * NT, S, s_vnear)
                load_v(go, 0, 0, CH, s_vnear)

            def load_rest(go, last):
                if last:
                    hold(s_st, val(last, NST, NST))
                load_q(go, LQ, QC, s_qlast)
                load_k(go, 0, CH, S, s_krest)
                if last:
                    hold(s_pv, val(last, STEPS, STEPS + PV0))
                load_v(go, 0, CH, S, s_vrest)

            def store(go):
                sp.wait_ge(s_taken, val(go, NJ, NJ + (AT_B if go[1] == 0 else AT_A) + len(JWT)))
                dst = (t["att"][go[1]] if isinstance(go[0], int) else
                       t["att"][bass.ds(go[0] + go[1], 1)].rearrange("o s c -> (o s) c"))
                sp.dma_start(dst.rearrange("(q p) c -> p q c", p=P),
                             on[:, :, :, :].rearrange("p q h d -> p q (h d)")).then_inc(s_out, 16)

            load_ahead((0, 0), None)
            load_first((0, 0), None)
            load_rest((0, 0), None)
            sp.wait_ge(s_taken, len(JA))
            send_rows(0)
            with sp.Fori(0, B * NG - 1) as g:
                rows((g, 0), 1)
                rows((g, 0), 2)
                load_ahead((g, 1), (g, 0))
                rows((g, 0), 3)
                load_first((g, 1), (g, 0))
                rows((g, 1), 0)
                load_rest((g, 1), (g, 0))
                store((g, 0))
            for qc in range(1, QC):
                rows((0, B * NG - 1), qc)
            store((0, B * NG - 1))
            sp.wait_ge(s_out, 16 * B * NG + 16)

        @block.tensor
        def _(pe):
            ident = t["ident"]

            def run_job(go, job, at):
                kind = job[0]
                wait(pe, s_taken, val(go, NJ, at - RING + 1))
                bank = sc[:, at % RING, :]
                if kind == "d":
                    _, r0, places, first, tiles = job
                    if r0 == 0:
                        pe.wait_ge(s_qlast if first else s_qmid, val(go, 16 * len(Q_PART), 16 * len(Q_PART)))
                    w = HG * tiles
                    for i in range(places):
                        r = r0 + i
                        mm = pe.matmul(bank[:, w * i:w * (i + 1)],
                                       t["line"][:, 0 if r < HALF else 1, P - 1 - r:2 * P - 1 - r],
                                       qs[:, :, :, :].rearrange("d c h (q r) -> d (c h q) r", r=P)[
                                           0:KR, HG * first:HG * (first + tiles), r],
                                       start=(i == 0), stop=True, skip_group_check=True)
                elif kind == "m":
                    mm = scores(go, job, at, bank)
                elif kind == "r":
                    pe.wait_ge(s_mready, val(go, QC, job[1] + 1))
                    for part in range(PARTS):
                        mm = pe.transpose(bank[0:HG * TPC, HALF * part:HALF * part + HALF].bitcast(BF16),
                                          mparts[:, part, :], t["identb"][:, :])
                elif kind == "w":
                    if job[1] == 0:
                        pe.wait_ge(s_pw, val(go, NB, 1))
                    pe.matmul(bank, zeros[:, :], t["masked"][:, :, :].rearrange("p k x -> p (k x)"), start=True, stop=False, skip_group_check=True)
                    for i in range(CH // QT):
                        r = CH // QT * job[1] + i
                        place = (HALF - 1 - r) if r < HALF else (P - 1 - r)
                        for h in range(HG):
                            mm = pe.matmul(bank[HP * h:HP * h + HD, QT * i:QT * (i + 1)],
                                           t["rvt"][:, 0 if r < HALF else 1, place, :], pw[:, h, r:S:P],
                                           start=False, stop=True, skip_group_check=True, tile_position=(0, HP * h))
                else:
                    if job[1] == 0:
                        pe.wait_ge(s_taken, val(go, NJ, at))
                    for i in range(TPC):
                        q = TPC * job[1] + i
                        mm = pe.transpose(bank[:, P * i:P * i + P], osb[:, P * q:P * q + P], ident[:, :])
                mm.then_inc(s_job, 1)

            def scores(go, job, at, bank):
                _, qc, kc, h, qt = job
                all_parts = val(go, 16 * len(K_PART), 16 * len(K_PART))
                if job == m0[0]:
                    pe.wait_ge(s_q, all_parts)
                    pe.wait_ge(s_k, all_parts)
                if job == mid[0]:
                    pe.wait_ge(s_kmid, all_parts)
                if job == ("m", 0, 1, 0, TPC - 1):
                    pe.wait_ge(s_split, val(go, EVEN(ND), EVEN(NDA)))
                    pe.wait_ge(s_split_odd, val(go, ND // 2, NDA // 2))
                if h == 0 and qt == TPC * qc:
                    if (qc, kc) == (0, 0):
                        pe.wait_ge(s_knear, all_parts)
                    if (qc, kc) == (0, QC - 1):
                        pe.wait_ge(s_kend, all_parts)
                    if (qc, kc) == (1, 0):
                        pe.wait_ge(s_krest, all_parts)
                    if (qc, kc) == (LQ, 0):
                        pe.wait_ge(s_split, val(go, EVEN(ND), EVEN(ND)))
                        pe.wait_ge(s_split_odd, val(go, ND // 2, ND // 2))
                lo, hi = CH * kc, CH * (kc + 1)
                runs = []
                for a, e, kind in ((0, P * qt, 0), (P * qt + P, S, 1)):
                    a, e = max(a, lo), min(e, hi)
                    if e > a:
                        runs.append((a, e, kind, 0, P))
                if lo <= P * qt < hi:
                    runs += [(P * qt, P * qt + P, 1, 0, HALF), (P * qt, P * qt + P, 0, HALF, HALF)]
                band = []
                for j, shift in enumerate((-32, 0, 0, 32)):
                    a, e = P * qt + shift, P * qt + shift + P
                    a2, e2 = max(a, lo, 0), min(e, hi, S)
                    if e2 > a2:
                        band.append((a2, e2, P + shift + a2 - a, j))
                first = True
                for a, e, kind, q0, nq in runs:
                    mm = pe.matmul(bank[q0:q0 + nq, a - lo:e - lo], qs[0:KR, qc, h, q0 + P * (qt - TPC * qc):q0 + nq + P * (qt - TPC * qc)],
                                   ks[0:KR, kind, h, a:e], start=first, stop=not band, skip_group_check=True)
                    first = False
                for part in range(PARTS):
                    for a, e, i, j in band:
                        q0 = P * (qt - TPC * qc) + 32 * j
                        mm = pe.matmul(bank[32 * j:32 * j + 32, a - lo:e - lo], dt[:, part, qc, h, q0:q0 + 32],
                                       t["ident3"][:, :, :].rearrange("p j k -> p (j k)")[:, i:i + e - a],
                                       start=False, stop=True, skip_group_check=True, tile_position=(0, 32 * j))
                return mm

            def second(go, n, pair):
                qc, kt = step(n)
                wait(pe, s_exp, val(go, NST, 2 * (n - 1) + pair + 1))
                if pair == 0 and n % QT == 0:
                    pe.wait_ge(s_row, val(go, NROW * QC, NROW * (qc + 1)))
                pieces = band_pieces(kt, qc)
                for h in (2 * pair, 2 * pair + 1):
                    for i, (a, e, kind) in enumerate(column_pieces(kt, qc)):
                        mm = pe.matmul(st[:, h, a - CH * qc:e - CH * qc], ks[:, kind, h, P * kt:P * kt + P],
                                       qs[:, qc, h, a - CH * qc:e - CH * qc],
                                       start=(i == 0), stop=not pieces, skip_group_check=True)
                for lo, m, r0, r1 in pieces:
                    w = t["identb"][:, :] if (r0, r1) == (0, P) else t["masked"][:, MASK[r0, r1], :]
                    for h in (2 * pair, 2 * pair + 1):
                        for part in range(PARTS):
                            mm = pe.matmul(st[:, h, lo - CH * qc:lo - CH * qc + m], w,
                                           dt[:, part, qc, h, lo - CH * qc:lo - CH * qc + m],
                                           start=False, stop=True, skip_group_check=True)
                mm.then_inc(s_st, 1)

            def values(go, n):
                qc, kt = step(n)
                pe.wait_ge(s_exp, val(go, NST, 2 * n + 2))
                if n % QT == 0:
                    wait(pe, s_oc, val(go, QC, qc))
                if n == 0:
                    pe.wait_ge(s_v, val(go, 16, 16))
                if n == ORDER[0].index(0):
                    pe.wait_ge(s_vnear, val(go, 32, 32))
                if n == QT:
                    pe.wait_ge(s_vrest, val(go, 16, 16))
                for i, (a, e, kind) in enumerate(column_pieces(kt, qc)):
                    for h in range(HG):
                        mm = pe.matmul(ops[HP * h:HP * h + HP, a - CH * qc:e - CH * qc],
                                       vs[:, kt, kind, HP * h:HP * h + HP], pr[:, n % PRB, h, a - CH * qc:e - CH * qc],
                                       start=(n % QT == 0 and i == 0), stop=(n % QT == QT - 1), skip_group_check=True,
                                       tile_position=(0, HP * h))
                mm.then_inc(s_pv, 1)

            def chunk(go, qc, steps):
                for i, mine in enumerate(steps):
                    n = QT * qc + i
                    prev = lambda: values(*((go, n - 1) if n else ((go[0], go[1] - 1), STEPS - 1)))
                    if n == 0 and isinstance(go[0], int):
                        prev = lambda: None
                    done = 0
                    places = (0, 0, 0) if i == 0 else (1, 2, 4)
                    for act, k in zip((lambda: second(go, n, 0), lambda: second(go, n, 1), prev), places):
                        for o, at, job in mine[done:k]:
                            run_job((go[0], go[1] + o), job, at)
                        done = max(done, k)
                        act()
                    for o, at, job in mine[done:]:
                        run_job((go[0], go[1] + o), job, at)

            pe.sem_inc(s_pv, PV0)
            for i, job in enumerate(JA):
                run_job((0, 0), job, i)
            pe.wait_ge(s_ones, 2)
            chunk((0, 0), 0, PLAN_B0)
            with pe.Fori(0, B * NG - 1) as g:
                chunk((g, 0), 1, PLAN_C1)
                chunk((g, 0), 2, PLAN_C2)
                chunk((g, 0), 3, PLAN_A)
                chunk((g, 1), 0, PLAN_B)
            last = (0, B * NG - 1)
            for qc, steps in ((1, PLAN_C1), (2, PLAN_C2_END), (3, NONE)):
                chunk(last, qc, steps)
            values(last, STEPS - 1)
            for i, job in enumerate(JWT):
                run_job((0, B * NG), job, AT_A + i)

        @block.scalar
        def _(act):
            def split(go, jobs):
                for o, _, job in jobs:
                    if job[0] == "d":
                        number = correction_number(job)
                        act.wait_ge(s_rest, val((go[0], go[1] + o), ND, number + 1))
                        act.activation(corrected(1, job), rest_of(job), ACT.Copy).then_inc(s_d1, 1)

            def chunk(go, qc, steps):
                for i, jobs in enumerate(steps):
                    n = QT * qc + i
                    for pair in range(2):
                        act.wait_ge(s_st, val(go, NST, 2 * n + pair + 1))
                        if pair == 0:
                            act.wait_ge(s_pv, val(go, STEPS, max(n - PRB + 1, 0 if STEPS % PRB else -PRB) + PV0))
                            k = band_before[max(n - PRB + 1, 0)]
                            if n == 0 or k:
                                act.wait_ge(s_pw, val(go, NB, k + 1))
                        act.activation(pr[:, n % PRB, 2 * pair:2 * pair + 2, :], st[:, 2 * pair:2 * pair + 2, :],
                                       ACT.Exp).then_inc(s_exp, 1)
                    split(go, jobs)

            split((0, 0), [(0, 0, job) for job in JA])
            chunk((0, 0), 0, PLAN_B0)
            with act.Fori(0, B * NG - 1) as g:
                chunk((g, 0), 1, PLAN_C1)
                chunk((g, 0), 2, PLAN_C2)
                chunk((g, 0), 3, PLAN_A)
                chunk((g, 1), 0, PLAN_B)
            for qc, steps in ((1, PLAN_C1), (2, PLAN_C2_END), (3, NONE)):
                chunk((0, B * NG - 1), qc, steps)

        @block.gpsimd
        def _(pool):
            pool.memset(ks[KR:KR + PARTS, :, :, :], 1.0).then_inc(s_ones, 1)
            pool.wait_ge(s_ones, 1)
            pool.memset(zeros[:, :], 0.0).then_inc(s_ones, 1)
            pool.sem_inc(s_pw, 1)

            def split(go, jobs):
                for o, _, job in jobs:
                    if job[0] != "d" or correction_number(job) % 2:
                        continue
                    number, owner = correction_number(job), (go[0], go[1] + o)
                    pool.wait_ge(s_d1, val(owner, ND, number + 1))
                    pool.sem_inc(s_seen, 1)
                    pool.tensor_tensor(corrected(2, job), rest_of(job), corrected(1, job), ALU.subtract).then_inc(s_split, 1)
                    pool.wait_ge(s_split, val(owner, EVEN(ND), EVEN(number + 1)))
                    pool.sem_inc(s_seen, 1)

            def band(go, n):
                qc, kt = step(n)
                pool.wait_ge(s_exp, val(go, NST, 2 * n + 2))
                pool.sem_inc(s_seen, 1)
                for i, (lo, m, a, e) in enumerate(band_spans(kt, qc)):
                    pool.tensor_copy(pw[a:e, :, lo:lo + m],
                                     pr[a:e, n % PRB, :, lo - CH * qc:lo - CH * qc + m]).then_inc(s_pw, 1)
                    pool.wait_ge(s_pw, val(go, NB, band_before[n] + i + 2))
                    pool.sem_inc(s_seen, 1)

            def chunk(go, qc, steps):
                for i, jobs in enumerate(steps):
                    if QT * qc + i in BAND:
                        band(go, QT * qc + i)
                    split(go, jobs)

            split((0, 0), [(0, 0, job) for job in JA])
            pool.memset(pw[:, :, :], 0.0).then_inc(s_pwz, 1)
            pool.wait_ge(s_pwz, 1)
            chunk((0, 0), 0, PLAN_B0)
            with pool.Fori(0, B * NG - 1) as g:
                chunk((g, 0), 1, PLAN_C1)
                chunk((g, 0), 2, PLAN_C2)
                chunk((g, 0), 3, PLAN_A)
                pool.wait_ge(s_job, val((g, 1), NJ, AT_B + NW))
                pool.sem_inc(s_seen, 1)
                chunk((g, 1), 0, PLAN_B)
            for qc, steps in ((1, PLAN_C1), (2, PLAN_C2_END), (3, NONE)):
                chunk((0, B * NG - 1), qc, steps)

        @block.vector
        def _(dve):
            def link(ins, go, number):
                ins.then_inc(s_mc, 1)
                dve.wait_ge(s_mc, val(go, 4 * QC, number))

            def take(go, job, at):
                kind = job[0]
                dve.wait_ge(s_job, val(go, NJ, at + 1))
                bank = sc[:, at % RING, :]
                if kind == "d":
                    _, r, places, first, tiles = job
                    number, w = correction_number(job), HG * tiles * places
                    if r == 0:
                        wait(dve, s_st, val(go, NST, 0 if first else 2 * QT * LQ - NST))
                    first_part = corrected(0, job)
                    src = bank[:, 0:w].rearrange("p (r x) -> p x r", r=places)
                    dve.tensor_copy(first_part, src).then_inc(s_d0, 1)
                    dve.wait_ge(s_d0, val(go, ND, number + 1))
                    if number % 2 == 0:
                        wait(dve, s_split, val(go, EVEN(ND), EVEN(number - 1)))
                    dve.tensor_tensor(rest_of(job), src, first_part,
                                      ALU.subtract).then_inc(s_rest, 1)
                    dve.wait_ge(s_rest, val(go, ND, number + 1))
                    dve.sem_inc(s_taken, 1)
                    if number % 2 == 0 and number:
                        job = CORR[number - 1]
                        dve.wait_ge(s_d1, val(go, ND, number))
                        dve.tensor_tensor(corrected(2, job), rest_of(job), corrected(1, job), ALU.subtract
                                          ).then_inc(s_split_odd, 1)
                    return
                elif kind == "m":
                    _, qc, kc, h, qt = job
                    row = TPC * h + qt - TPC * qc
                    ins = dve.tensor_reduce(mx[:, row, kc:kc + 1], bank, AX.X, ALU.max)
                elif kind == "r":
                    wait(dve, s_row, val(go, NROW * QC, NROW * job[1]))
                    ins = dve.tensor_copy(mt[:, :, :], bank[0:HG * TPC, 0:HALF * PARTS].bitcast(BF16)
                                    .rearrange("p (a x) -> p a x", a=PARTS))
                elif kind == "w":
                    k = CH // QT
                    if job[1] == 0:
                        dve.wait_ge(s_oc, val(go, QC, 0))
                    view = osb[:, :].rearrange("p (q r) -> p q r", r=P)[:, :, k * job[1]:k * job[1] + k]
                    ins = dve.tensor_tensor(view, bank.rearrange("p (r q) -> p q r", q=QT), view, ALU.add)
                else:
                    n = job[1]
                    rows = bank.rearrange("p (q h d) -> p q h d", q=TPC, h=HG)
                    dve.reciprocal(rcp[:, TPC * n:TPC * n + TPC, :], rows[:, :, :, HD]).then_inc(s_rcp, 1)
                    dve.wait_ge(s_rcp, val(go, QC, n + 1 - QC))
                    if n == 0:
                        dve.wait_ge(s_out, val(go, 16, 0))
                    ins = dve.tensor_tensor(on[:, TPC * n:TPC * n + TPC, :, :], rows[:, :, :, 0:HD],
                                            rcp[:, TPC * n:TPC * n + TPC, :].unsqueeze(3).to_broadcast([P, TPC, HG, HD]),
                                            ALU.mult)
                ins.then_inc(s_taken, 1)

            def split_rows(go, qc, at):
                dve.wait_ge(s_taken, val(go, NJ, at))
                link(dve.tensor_reduce(mneg[:, :], mx[:, :, :], AX.X, ALU.max, negate=True), go, 4 * qc + 1)
                link(dve.tensor_copy(mparts[:, 0, :], mneg[:, :]), go, 4 * qc + 2)
                link(dve.tensor_tensor(mrest[:, :], mneg[:, :], mparts[:, 0, :], ALU.subtract), go, 4 * qc + 3)
                link(dve.tensor_copy(mparts[:, 1, :], mrest[:, :]), go, 4 * qc + 4)
                dve.tensor_tensor(mparts[:, 2, :], mrest[:, :], mparts[:, 1, :], ALU.subtract).then_inc(s_mready, 1)

            def copy_out(go, qc):
                dve.wait_ge(s_pv, val(go, STEPS, QT * (qc + 1) + PV0))
                dve.tensor_copy(osb[:, CH * qc:CH * (qc + 1)], ops[:, :]).then_inc(s_oc, 1)

            def stream(go, jobs, at, outs=()):
                outs = list(outs)
                for i, job in enumerate(jobs):
                    if outs and outs[0][0] == i:
                        copy_out(*outs.pop(0)[1:])
                    take(go, job, at + i)
                    if job in CLOSING:
                        split_rows(go, job[1], at + i + 1)
                for o in outs:
                    copy_out(*o[1:])

            dve.sem_inc(s_out, 16)
            stream((0, 0), JA, 0)
            stream((0, 0), JB[len(JWT):] + JC[:EARLY], AT_B + len(JWT))
            outs_at = [(3, 0), (LATE - EARLY + 3, 1)]
            with dve.Fori(0, B * NG - 1) as g:
                stream((g, 0), JC[EARLY:], AT_C + EARLY, [(k, (g, 0), qc) for k, qc in outs_at])
                stream((g, 1), JA, AT_A, [(AHEAD + 3, (g, 0), 2)])
                stream((g, 1), JB + JC[:EARLY], AT_B, [(0, (g, 0), 3)])
            last = (0, B * NG - 1)
            stream(last, JC[EARLY:], AT_C + EARLY, [(k, last, qc) for k, qc in outs_at])
            copy_out(last, 2)
            copy_out(last, 3)
            for i, job in enumerate(JWT):
                take((0, B * NG), job, AT_A + i)


def experts(nc, t, x, bo, w1, b1, w2, b2, wr, br, gamma, beta, out):
    with ExitStack() as ctx:
        sb = lambda n, s, d: ctx.enter_context(nc.sbuf_tensor(n, s, d))
        sem = lambda n: ctx.enter_context(nc.semaphore(n))
        ident = t["ident"]
        at = sb("at", [P, 2, TPC, NG, GD], F32)
        xb = sb("xb", [P, 2, TPC, E], F32)
        xo = sb("xo", [P, 2, TPC, E], F32)
        att = sb("att_t", [P, 2, KE, CH], F32)
        x1 = sb("x1", [P, B, QT, E], F32)
        x1t = sb("x1t", [P, B, KE, S], F32)
        rows = sb("rows", [P, 3, E], F32)
        wrs = sb("wrs", [P, KE, NE], F32)
        brs = sb("brs", [1, NE], F32)
        ones = sb("ones", [P, P], F32)
        epst = sb("epst", [P, 1], F32)
        stats = sb("stats", [P, TPC, 6], F32)
        mv = sb("mv", [P, TPC, 2], F32)
        sd = sb("sd", [P, TPC], F32)
        rs = sb("rs", [P, TPC], F32)
        xm = sb("xm", [P, KE], F32)
        lg = sb("lg", [1, NE], F32)
        tiny = sb("tiny_r", [1, 8], F32)
        ex = sb("ex", [1, NE], F32)
        rw = sb("rw", [1, NE], F32)
        top = sb("top", [1, 8], F32)
        idx = sb("idx", [1, 8], U32)
        tw = sb("tw", [1, TOPK], F32)
        wb = sb("wb", [P, B, TOPK], F32)
        w1s = sb("w1s", [P, TOPK, KE, F], F32)
        w2s = sb("w2s", [P, TOPK, KF, E], F32)
        b1s = sb("b1s", [P, TOPK, KF], F32)
        b2s = sb("b2s", [P, TOPK, E], F32)
        bsum = sb("bsum", [P, B, E], F32)
        hid = sb("hid", [P, 2, KF, CH], F32)
        y = sb("y", [P, 2, TPC, E], F32)
        z = sb("z", [P, 2, TPC, E], F32)
        tp = ctx.enter_context(nc.psum_tensor("tp_ps", [P, 2, CH], F32))
        hp = ctx.enter_context(nc.psum_tensor("hp_ps", [P, 2, CH], F32))
        op = ctx.enter_context(nc.psum_tensor("op_ps", [P, 2, TPC // 2, CH], F32))
        (s_c, s_at, s_ata, s_atv, s_op, s_xo, s_x1, s_ch, s_sd, s_var, s_xt, s_xta, s_xtv, s_xm, s_xmc, s_lg, s_ex,
         s_neg, s_top, s_neg2, s_ex2, s_tw, s_wb, s_wbc, s_idx, s_b2l, s_h, s_hid, s_o, s_y, s_z1, s_cst,
         s_bs, s_b2) = [sem(n) for n in (
             "consts", "att_turned", "att_by_act", "att_by_dve", "proj_done", "xo_ready", "x1_ready",
             "dve_chain", "sd_ready", "var_ready", "x1_turned", "x1t_by_act", "x1t_by_dve", "mean_done", "mean_copied",
             "logits_done", "exp_ready", "neg_ready", "top_ready", "neg2_ready", "exp2_ready", "tw_ready", "wb_done",
             "wb_copied", "index_ready", "b2_loaded", "hidden_done", "gelu_done", "expert_done", "y_ready",
             "z_scaled", "const_set", "bsum_ready", "b2_used")]
        s_ld = [sem(f"tile_loaded{i}") for i in range(2)]
        s_st = [sem(f"out_stored{i}") for i in range(2)]
        s_we = [sem(f"expert_loaded{k}") for k in range(TOPK)]
        s_st_ready, s_pz = sem("out_ready"), sem("pool_chain")
        block = ctx.enter_context(nc.Block())
        NCONST = 5
        STAGES = QC * TOPK

        order, owed = [], []

        def owe(kind, arg, after):
            owed.append([after, (kind, arg)])

        def pay(all_of_it=False):
            while owed and (all_of_it or owed[0][0] <= 0):
                order.append(owed.pop(0)[1])

        def front(n):
            return [("turn", n), ("project", n), ("back", n)]

        def put(step):
            order.append(step)
            if step[0] in ("project", "norm1", "norm2"):
                owe("dev", 0, 2)
            if step[0] == "logits":
                owe("ex", step[1], 2)
                owe("ex2", step[1], 4)

        for c in range(QC):
            for one in front(c):
                put(one)
                pay(True)
        for kind in ("mean", "logits", "weigh", "bias"):
            put((kind, 0))
            pay(True)
        for b in range(B):
            between = {}
            if b + 1 < B:
                steps = [one for c in range(QC) for one in front((b + 1) * QC + c)]
                between = dict(enumerate(steps + [("mean", b + 1), ("logits", b + 1)]))
                between[2 * STAGES - 1], between[2 * STAGES] = ("weigh", b + 1), ("bias", b + 1)
            for m in range(STAGES + 1):
                if m == STAGES:
                    pay(True)
                for half in range(2):
                    for f in range(KF // 2 * half, KF // 2 * (half + 1)):
                        if m < STAGES:
                            order.append(("hidden", (b * STAGES + m, f)))
                            for o in owed:
                                o[0] -= 1
                            pay()
                    if half and m:
                        order.append(("expert", b * STAGES + m - 1))
                    if 2 * m + half in between:
                        put(between[2 * m + half])
                if m >= 2 and m % 2 == 0:
                    put(("norm1", b * QC + (m - 2) // 2))
                if m >= 3 and m % 2:
                    put(("norm2", b * QC + (m - 3) // 2))
                if m == 0 and b:
                    put(("norm2", b * QC - 1))
        pay(True)
        put(("norm2", B * QC - 1))
        pay(True)

        @block.sync
        def _(sp):
            def load(n):
                b, c = divmod(n, QC)
                if n >= 2:
                    sp.wait_ge(s_at, 2 * (n - 1))
                    sp.wait_ge(s_xo, n - 1)
                for g in range(NG):
                    sp.dma_start(at[:, n % 2, :, g, :],
                                 t["att"][NG * b + g, CH * c:CH * (c + 1), :].rearrange(
                                     "(t p) c -> p t c", p=P)).then_inc(s_ld[n % 2], 16)
                sp.dma_start(xb[:, n % 2, :, :], x[b, CH * c:CH * (c + 1), :].rearrange(
                    "(t p) e -> p t e", p=P)).then_inc(s_ld[n % 2], 16)

            def load_experts(b):
                sp.wait_ge(s_idx, b + 1)
                if b:
                    sp.wait_ge(s_b2, b)
                es = [sp.value_load(idx[0:1, k:k + 1], min_val=0, max_val=NE - 1) for k in range(TOPK)]
                for k, e in enumerate(es):
                    sp.dma_start(b2s[0:1, k, :], b2[bass.ds(e, 1)]).then_inc(s_b2l, 16)
                for k, e in enumerate(es):
                    if b:
                        sp.wait_ge(s_o, b * STAGES - TOPK + k + 1)
                    sp.dma_start(w1s[:, k, :, :], w1[bass.ds(e, 1)].rearrange("o (k p) f -> p (o k) f", p=P)
                                 ).then_inc(s_we[k], 16)
                    sp.dma_start(b1s[:, k, :], b1[bass.ds(e, 1)].rearrange("o (k p) -> p (o k)", p=P)
                                 ).then_inc(s_we[k], 16)
                    sp.dma_start(w2s[:, k, :, :], w2[bass.ds(e, 1)].rearrange("o (k p) d -> p (o k) d", p=P)
                                 ).then_inc(s_we[k], 16)

            def store(n):
                b, c = divmod(n, QC)
                sp.wait_ge(s_st_ready, n + 1)
                sp.dma_start(out[b, CH * c:CH * (c + 1), :].rearrange("(t p) e -> p t e", p=P), z[:, n % 2, :, :]
                             ).then_inc(s_st[n % 2], 16)

            with nc.allow_non_contiguous_dma("small tables"):
                for i, row in enumerate((bo, gamma, beta)):
                    sp.dma_start(rows[:, i, :], row.partition_broadcast(P)).then_inc(s_c, 16)
                sp.dma_start(wrs[:, :, :], wr.rearrange("(k p) e -> p k e", p=P)).then_inc(s_c, 16)
                sp.dma_start(brs[:, :], br.rearrange("(a e) -> a e", a=1)).then_inc(s_c, 16)
                for n in range(QC):
                    load(n)
                load_experts(0)
                for b in range(1, B):
                    for c in range(QC):
                        load(b * QC + c)
                    store((b - 1) * QC)
                    store((b - 1) * QC + 1)
                    load_experts(b)
                    store((b - 1) * QC + 2)
                    store((b - 1) * QC + 3)
                for c in range(QC):
                    store((B - 1) * QC + c)
                for i in range(2):
                    sp.wait_ge(s_st[i], 8 * B * QC)

        @block.gpsimd
        def _(pool):
            def residual(n):
                pool.wait_ge(s_ld[n % 2], 16 * (NG + 1) * (n // 2 + 1))
                if n >= 2:
                    pool.wait_ge(s_x1, n - 1)
                for i in range(TPC):
                    ins = pool.tensor_tensor(xo[:, n % 2, i, :], xb[:, n % 2, i, :], rows[:, 0, :], ALU.add)
                ins.then_inc(s_xo, 1)

            def affine(n):
                b, c = divmod(n, QC)
                pool.wait_ge(s_z1, n + 1)
                for i in range(TPC):
                    pool.tensor_tensor(z[:, n % 2, i, :], z[:, n % 2, i, :], rows[:, 1, :], ALU.mult).then_inc(s_pz, 1)
                pool.wait_ge(s_pz, TPC * (3 * n + 1))
                for i in range(TPC):
                    pool.tensor_tensor(z[:, n % 2, i, :], z[:, n % 2, i, :], rows[:, 2, :], ALU.add).then_inc(s_pz, 1)
                pool.wait_ge(s_pz, TPC * (3 * n + 2))
                for i in range(TPC):
                    pool.tensor_tensor(z[:, n % 2, i, :], z[:, n % 2, i, :], x1[:, b, TPC * c + i, :], ALU.add
                                       ).then_inc(s_pz, 1)

            pool.memset(ones[:, :], 1.0).then_inc(s_cst, 1)
            pool.memset(epst[:, :], EPS).then_inc(s_cst, 1)
            pool.wait_ge(s_c, 16 * NCONST)
            for n in range(QC):
                residual(n)
            for b in range(B):
                if b + 1 < B:
                    for c in range(QC):
                        residual((b + 1) * QC + c)
                for c in range(QC):
                    affine(b * QC + c)

        @block.tensor
        def _(pe):
            def turn(n):
                b, c = divmod(n, QC)
                pe.wait_ge(s_ld[n % 2], 16 * (NG + 1) * (n // 2 + 1))
                if b and c == 0:
                    pe.wait_ge(s_bs, b)
                for k in range(KE):
                    if n:
                        pe.wait_ge((s_xta, s_xtv)[k], n)
                    for i in range(TPC):
                        mm = pe.transpose(tp[:, k, P * i:P * i + P],
                                          at[:, n % 2, i, :, :].rearrange("p g c -> p (g c)")[:, P * k:P * k + P],
                                          ident[:, :])
                    mm.then_inc(s_at, 1)

            def project_out(n):
                pe.wait_ge(s_ata, n + 1)
                pe.wait_ge(s_atv, n + 1)
                for i in range(TPC):
                    for k in range(KE):
                        mm = pe.matmul(tp[:, i // 2, E * (i % 2):E * (i % 2) + E], att[:, n % 2, k, P * i:P * i + P],
                                       t["wot"][:, k, :], start=(k == 0), stop=(k == KE - 1))
                mm.then_inc(s_op, 1)

            def back(n):
                b, c = divmod(n, QC)
                pe.wait_ge(s_x1, n + 1)
                for k in range(KE):
                    for i in range(TPC):
                        mm = pe.transpose(tp[:, k, P * i:P * i + P], x1[:, b, TPC * c + i, P * k:P * k + P], ident[:, :])
                    mm.then_inc(s_xt, 1)

            def mean(b):
                pe.wait_ge(s_xta, (b + 1) * QC)
                pe.wait_ge(s_xtv, (b + 1) * QC)
                for k in range(KE):
                    for i in range(QT):
                        mm = pe.matmul(tp[:, 0, k:k + 1], x1[:, b, i, P * k:P * k + P], ones[:, 0:1],
                                       start=(i == 0), stop=(i == QT - 1))
                mm.then_inc(s_xm, 1)

            def logits(b):
                pe.wait_ge(s_xmc, b + 1)
                for k in range(KE):
                    mm = pe.matmul(tp[0:1, 1, 0:NE], xm[:, k:k + 1], wrs[:, k, :], start=(k == 0), stop=(k == KE - 1))
                mm.then_inc(s_lg, 1)

            def weigh(b):
                pe.wait_ge(s_tw, b + 1)
                pe.matmul(tp[:, 0, 0:TOPK], ones[0:1, :], tw[:, :], start=True, stop=True).then_inc(s_wb, 1)

            def bias(b):
                pe.wait_ge(s_wbc, b + 1)
                pe.wait_ge(s_b2l, 16 * TOPK * (b + 1))
                for k in range(TOPK):
                    mm = pe.matmul(tp[:, 1, E * k:E * k + E], ones[0:1, :], b2s[0:1, k, :], start=True, stop=True)
                mm.then_inc(s_b2, 1)

            def hidden(arg):
                m, f = arg
                b, (c, k) = m // STAGES, divmod(m % STAGES, TOPK)
                i = KF * m + f
                if c == 0 and f == 0:
                    pe.wait_ge(s_we[k], 48 * (b + 1))
                if i >= 2:
                    pe.wait_ge(s_hid, i - 1)
                for kk in range(KE):
                    mm = pe.matmul(hp[:, f % 2, :], w1s[:, k, kk, P * f:P * f + P],
                                   x1t[:, b, kk, CH * c:CH * (c + 1)], start=(kk == 0), stop=(kk == KE - 1))
                mm.then_inc(s_h, 1)

            def expert(m):
                k = m % TOPK
                pe.wait_ge(s_hid, KF * (m + 1))
                if m >= 2:
                    pe.wait_ge(s_y, m - 1)
                for i in range(TPC):
                    for f in range(KF):
                        mm = pe.matmul(op[:, k, i // 2, E * (i % 2):E * (i % 2) + E],
                                       hid[:, m % 2, f, P * i:P * i + P], w2s[:, k, f, :],
                                       start=(f == 0), stop=(f == KF - 1))
                mm.then_inc(s_o, 1)

            pe.wait_ge(s_cst, 2)
            pe.wait_ge(s_c, 16 * NCONST)
            steps = {"turn": turn, "project": project_out, "back": back, "mean": mean, "logits": logits,
                     "weigh": weigh, "bias": bias, "hidden": hidden, "expert": expert}
            for kind, arg in order:
                if kind in steps:
                    steps[kind](arg)

        @block.scalar
        def _(act):
            devs = 0

            def turn(n):
                act.wait_ge(s_at, 2 * n + 1)
                if n >= 2:
                    act.wait_ge(s_op, n - 1)
                act.activation(att[:, n % 2, 0, :], tp[:, 0, :], ACT.Copy).then_inc(s_ata, 1)

            def back(n):
                b, c = divmod(n, QC)
                act.wait_ge(s_xt, 2 * n + 1)
                act.activation(x1t[:, b, 0, CH * c:CH * (c + 1)], tp[:, 0, :], ACT.Copy).then_inc(s_xta, 1)

            def dev(_):
                nonlocal devs
                devs += 1
                act.wait_ge(s_var, devs)
                act.activation(sd[:, :], mv[:, :, 1], ACT.Sqrt, bias=epst[:, 0:1]).then_inc(s_sd, 1)

            def ex_all(b):
                act.wait_ge(s_neg, b + 1)
                act.activation(ex[:, :], lg[:, :], ACT.Exp, bias=tiny[0:1, 0:1]).then_inc(s_ex, 1)

            def ex_top(b):
                act.wait_ge(s_neg2, b + 1)
                act.activation(tiny[0:1, 4:6], top[0:1, 0:2], ACT.Exp, bias=tiny[0:1, 3:4]).then_inc(s_ex2, 1)

            def hidden(arg):
                m, f = arg
                k = m % TOPK
                act.wait_ge(s_h, KF * m + f + 1)
                if f == 0 and m >= 2:
                    act.wait_ge(s_o, m - 1)
                act.activation(hid[:, m % 2, f, :], hp[:, f % 2, :], ACT.Gelu, bias=b1s[:, k, f:f + 1]).then_inc(s_hid, 1)

            act.wait_ge(s_cst, 2)
            steps = {"turn": turn, "back": back, "dev": dev, "ex": ex_all, "ex2": ex_top, "hidden": hidden}
            for kind, arg in order:
                if kind in steps:
                    steps[kind](arg)

        @block.vector
        def _(dve):
            chain = Count(s_ch)
            norms = [0]

            def norm(src, dst):
                for i in range(TPC):
                    ins = dve.bn_stats(stats[:, i, :], src(i))
                chain.link(dve, ins)
                for i in range(TPC):
                    ins = dve.bn_aggr(mv[:, i, :], stats[:, i, :])
                ins.then_inc(s_var, 1)
                norms[0] += 1
                dve.wait_ge(s_sd, norms[0])
                chain.link(dve, dve.reciprocal(rs[:, :], sd[:, :]))
                for i in range(TPC):
                    ins = dve.tensor_scalar(dst(i), src(i), mv[:, i, 0:1], rs[:, i:i + 1], ALU.subtract, ALU.mult)
                return ins

            def turn(n):
                dve.wait_ge(s_at, 2 * n + 2)
                if n >= 2:
                    dve.wait_ge(s_op, n - 1)
                dve.tensor_copy(att[:, n % 2, 1, :], tp[:, 1, :]).then_inc(s_atv, 1)

            def project_out(n):
                b, c = divmod(n, QC)
                dve.wait_ge(s_op, n + 1)
                dve.wait_ge(s_xo, n + 1)
                for i in range(TPC):
                    ins = dve.tensor_tensor(xo[:, n % 2, i, :], tp[:, i // 2, E * (i % 2):E * (i % 2) + E],
                                            xo[:, n % 2, i, :], ALU.add)
                chain.link(dve, ins)
                norm(lambda i: xo[:, n % 2, i, :], lambda i: x1[:, b, TPC * c + i, :]).then_inc(s_x1, 1)

            def back(n):
                b, c = divmod(n, QC)
                dve.wait_ge(s_xt, 2 * n + 2)
                dve.tensor_copy(x1t[:, b, 1, CH * c:CH * (c + 1)], tp[:, 1, :]).then_inc(s_xtv, 1)

            def mean(b):
                dve.wait_ge(s_xm, b + 1)
                dve.tensor_scalar(xm[:, :], tp[:, 0, 0:KE], 1.0 / S, None, ALU.mult).then_inc(s_xmc, 1)

            def logits(b):
                dve.wait_ge(s_lg, b + 1)
                chain.link(dve, dve.tensor_tensor(lg[:, :], tp[0:1, 1, 0:NE], brs[:, :], ALU.add))
                dve.tensor_reduce(tiny[0:1, 0:1], lg[:, :], AX.X, ALU.max, negate=True).then_inc(s_neg, 1)
                dve.wait_ge(s_ex, b + 1)
                chain.link(dve, dve.tensor_reduce(tiny[0:1, 1:2], ex[:, :], AX.X, ALU.add))
                chain.link(dve, dve.reciprocal(tiny[0:1, 2:3], tiny[0:1, 1:2]))
                chain.link(dve, dve.tensor_scalar(rw[:, :], ex[:, :], tiny[0:1, 2:3], None, ALU.mult))
                chain.link(dve, dve.max(top[:, :], rw[:, :]))
                dve.max_index(idx[:, :], top[:, :], rw[:, :]).then_inc(s_idx, 1)
                dve.tensor_scalar(tiny[0:1, 3:4], top[0:1, 0:1], -1.0, None, ALU.mult).then_inc(s_neg2, 1)
                dve.wait_ge(s_ex2, b + 1)
                chain.link(dve, dve.tensor_reduce(tiny[0:1, 6:7], tiny[0:1, 4:6], AX.X, ALU.add))
                chain.link(dve, dve.reciprocal(tiny[0:1, 7:8], tiny[0:1, 6:7]))
                dve.tensor_scalar(tw[:, :], tiny[0:1, 4:6], tiny[0:1, 7:8], None, ALU.mult).then_inc(s_tw, 1)

            def weigh(b):
                dve.wait_ge(s_wb, b + 1)
                dve.tensor_copy(wb[:, b, :], tp[:, 0, 0:TOPK]).then_inc(s_wbc, 1)
                dve.wait_ge(s_wbc, b + 1)

            def bias(b):
                dve.wait_ge(s_b2, b + 1)
                chain.link(dve, dve.tensor_scalar(bsum[:, b, :], tp[:, 1, 0:E], wb[:, b, 0:1], None, ALU.mult))
                dve.scalar_tensor_tensor(out=bsum[:, b, :], in0=tp[:, 1, E:2 * E], scalar=wb[:, b, 1:2],
                                         in1=bsum[:, b, :], op0=ALU.mult, op1=ALU.add).then_inc(s_bs, 1)
                dve.wait_ge(s_bs, b + 1)

            def expert(m):
                n, k = divmod(m, TOPK)
                b, c = divmod(n, QC)
                if k == 0:
                    for i in range(TPC):
                        ins = dve.tensor_tensor(y[:, n % 2, i, :], x1[:, b, TPC * c + i, :], bsum[:, b, :], ALU.add)
                    chain.link(dve, ins)
                dve.wait_ge(s_o, m + 1)
                for i in range(TPC):
                    ins = dve.scalar_tensor_tensor(out=y[:, n % 2, i, :],
                                                   in0=op[:, k, i // 2, E * (i % 2):E * (i % 2) + E],
                                                   scalar=wb[:, b, k:k + 1], in1=y[:, n % 2, i, :],
                                                   op0=ALU.mult, op1=ALU.add)
                ins.then_inc(s_y, 1)
                dve.wait_ge(s_y, m + 1)

            def norm1(n):
                if n >= 2:
                    dve.wait_ge(s_st[n % 2], 16 * (n // 2))
                norm(lambda i: y[:, n % 2, i, :], lambda i: z[:, n % 2, i, :]).then_inc(s_z1, 1)

            def norm2(n):
                dve.wait_ge(s_pz, TPC * (3 * n + 3))
                norm(lambda i: z[:, n % 2, i, :], lambda i: z[:, n % 2, i, :]).then_inc(s_st_ready, 1)

            steps = {"turn": turn, "project": project_out, "back": back, "mean": mean, "logits": logits,
                     "weigh": weigh, "bias": bias, "expert": expert, "norm1": norm1, "norm2": norm2}
            for kind, arg in order:
                if kind in steps:
                    steps[kind](arg)


def program(nc, hidden, wq, bq, wk, bk, wv, bv, wo, bo, rel_k, rel_v, w1, b1, w2, b2, wr, br, gamma, beta, out):
    with ExitStack() as ctx:
        sb = lambda n, s, d: ctx.enter_context(nc.sbuf_tensor(n, s, d))
        dram = lambda n, s, d: nc.dram_tensor(n, s, d, kind="Internal").ap()
        t = {
            "ident": sb("ident", [P, P], F32),
            "identb": sb("identb", [P, P], BF16),
            "ident3": sb("ident3", [P, 3, P], BF16),
            "masked": sb("masked", [P, 4, P], BF16),
            "line": sb("line", [KR, 2, LINE], BF16),
            "rvt": sb("rvt", [P, 2, HALF, HD], F32),
            "wot": sb("wot", [P, KE, E], F32),
            "tiny": sb("tiny", [1, 1], F32),
            "line_v": dram("line_v", [2, LINE, HD], F32),
            "qp": dram("q_parts", [B * NG, PARTS, QC, GD, CH], BF16),
            "kp": dram("k_parts", [B * NG, 2, PARTS, GD, S], BF16),
            "vp": dram("v_padded", [B * NG, S, 2, HG * HP], F32),
            "att": dram("attended", [B * NG, S, GD], F32),
        }
        setup(nc, t, rel_k, rel_v)
        project(nc, t, hidden, wq, bq, wk, bk, wv, bv, wo, rel_k, rel_v)
        attention(nc, t)
        experts(nc, t, hidden, bo, w1, b1, w2, b2, wr, br, gamma, beta, out)


_INS = ["L0_attn_hidden_states", "L0_attn_Wq", "L0_attn_bq", "L0_attn_Wk", "L0_attn_bk", "L0_attn_Wv", "L0_attn_bv",
        "L0_attn_Wo", "L0_attn_bo", "L0_attn_rel_k", "L0_attn_rel_v", "L0_ffn_W1", "L0_ffn_b1", "L0_ffn_W2", "L0_ffn_b2",
        "L0_ffn_Wr", "L0_ffn_br", "L0_ffn_gamma", "L0_ffn_beta"]


def kernel(**inputs):
    import numpy as _np
    import concourse.bacc as _bacc
    from concourse import mybir as _mybir
    from concourse.bass_utils import run_bass_kernel_spmd as _run

    nc = _bacc.Bacc("TRN2", target_bir_lowering=False, num_devices=1)
    arrays, args = {}, []
    for name in _INS:
        a = _np.ascontiguousarray(inputs[name])
        arrays[f"in_{name}"] = a
        args.append(nc.dram_tensor(f"in_{name}", a.shape, _mybir.dt.from_np(a.dtype), kind="ExternalInput").ap())
    args.append(nc.dram_tensor("out", [B, S, E], F32, kind="ExternalOutput").ap())
    program(nc, *args)
    return _run(nc, [arrays], core_ids=[0]).results[0]["out"]
```
